# Optimizing a Trainium2 kernel written in Bass

```python
import numpy as np
import jax
import jax.numpy as jnp

def _softmax(x, axis=-1):
    return jax.nn.softmax(x, axis=axis)

def _gelu(x):
    return jax.nn.gelu(x, approximate=True)

def _silu(x):
    return jax.nn.silu(x)

def _sigmoid(x):
    return jax.nn.sigmoid(x)

def _layernorm(x, axis=-1, eps=1e-05):
    m = jnp.mean(x, axis=axis, keepdims=True)
    v = jnp.var(x, axis=axis, keepdims=True)
    return (x - m) / jnp.sqrt(v + eps)

def _scatter_add(tgt, idx, src, axis=0):
    return tgt.at[idx].add(src)

def _segment_sum(src, seg, n):
    return jax.ops.segment_sum(src, seg, n)
kernel_name = 'mk_xattn_seq_d4_seqx_r4_c29718'

def setup_inputs(seed: int=0):
    np.random.seed(seed)
    _w = jnp.asarray

    def _rec_inputs():
        import jax
        import jax.numpy as jnp
        _rk = jax.random.key(seed)
        x = -0.0002928 + 1 * jax.random.normal(jax.random.fold_in(_rk, 1), (8, 112, 512), jnp.float32)
        _lenS = 112 - jax.random.randint(jax.random.fold_in(_rk, 7), (8,), 0, max(1, 112 // 4) + 1, jnp.int32)
        _lenS2 = 375 - jax.random.randint(jax.random.fold_in(_rk, 8), (8,), 0, max(1, 375 // 4) + 1, jnp.int32)
        _ctx_2048P = jax.random.normal(jax.random.fold_in(_rk, 11), (8, 16, 512), jnp.float32)
        _ctx_2048c = jax.random.dirichlet(jax.random.fold_in(_rk, 511), 0.3 * jnp.ones((16,), jnp.float32), (8, 375))
        _ctx_2048t = jnp.einsum('bsk,bkd->bsd', _ctx_2048c, _ctx_2048P)
        _ctx_2048t = _ctx_2048t * jax.lax.rsqrt(jnp.mean(jnp.square(_ctx_2048t)) + 1e-12) * 0.953939
        ctx_2048 = 0.000189249 + 0.0999589 * (_ctx_2048t + 0.3 * jax.random.normal(jax.random.fold_in(_rk, 611), (8, 375, 512), jnp.float32))
        _validS = jnp.arange(112)[None, :] < _lenS[:, None]
        _validS2 = jnp.arange(375)[None, :] < _lenS2[:, None]
        _causal = jnp.tril(jnp.ones((112, 112), dtype=bool))
        mask_BxS2_ik0 = jnp.where(jnp.broadcast_to(_validS2[:, :], (8, 375)), 0, 1).astype(jnp.int32)
        return (x, ctx_2048, mask_BxS2_ik0)
    x, ctx_2048, mask_BxS2_ik0 = _rec_inputs()

    def _L0_xattn_setup():
        import jax, jax.numpy as jnp
        import numpy as np
        B, L, E, H = (4, 128, 512, 32)
        S = E // H
        EXTRA_MAA, EXTRA_DECAY = (32, 64)
        EPS = 1e-05

        def _ln(x, w, b):
            m = jnp.mean(x, axis=-1, keepdims=True)
            v = jnp.mean((x - m) ** 2, axis=-1, keepdims=True)
            return (x - m) * jax.lax.rsqrt(v + EPS) * w + b

        def _token_shift(xn, prev_row):
            first = (prev_row - xn[:, 0])[:, None]
            rest = xn[:, :-1] - xn[:, 1:]
            return jnp.concatenate([first, rest], axis=1)
        key = jax.random.key(seed)
        ks = jax.random.split(key, 24)
        rn = lambda k, shp, s=1.0: jax.random.normal(k, shp, dtype=jnp.float32) * s
        return dict(x=rn(ks[0], (B, L, E)), state=rn(ks[1], (B, 2 + S, E), 0.1), ln1_w=jnp.ones((E,), jnp.float32), ln1_b=jnp.zeros((E,), jnp.float32), ln2_w=jnp.ones((E,), jnp.float32), ln2_b=jnp.zeros((E,), jnp.float32), maa_x=rn(ks[2], (E,), 0.02), maa_w1=rn(ks[3], (E, 5 * EXTRA_MAA), 0.02), maa_w2=rn(ks[4], (5, EXTRA_MAA, E), 0.02), maa_stack=rn(ks[5], (5, E), 0.02), time_decay=rn(ks[6], (E,), 0.5), decay_w1=rn(ks[7], (E, EXTRA_DECAY), 0.02), decay_w2=rn(ks[8], (EXTRA_DECAY, E), 0.02), faaaa=rn(ks[9], (H, S), 0.1), Wr=rn(ks[10], (E, E), 0.02), Wk=rn(ks[11], (E, E), 0.02), Wv=rn(ks[12], (E, E), 0.02), Wg=rn(ks[13], (E, E), 0.02), Wo=rn(ks[14], (E, E), 0.02), gn_w=jnp.ones((E,), jnp.float32), gn_b=jnp.zeros((E,), jnp.float32), ffn_maa_k=rn(ks[15], (E,), 0.02), ffn_maa_r=rn(ks[16], (E,), 0.02), ffn_Wk=rn(ks[17], (E, E), 0.02), ffn_Wr=rn(ks[18], (E, E), 0.02), ffn_Wv=rn(ks[19], (E, E), 0.02), i=0)
    _L0_xattn_all = _L0_xattn_setup()
    _L0_xattn_in = {k: v for k, v in _L0_xattn_all.items() if k in ('ln1_w', 'ln1_b', 'ln2_w', 'ln2_b', 'maa_x', 'maa_w1', 'maa_w2', 'maa_stack', 'time_decay', 'decay_w1', 'decay_w2', 'faaaa', 'Wr', 'Wk', 'Wv', 'Wg', 'Wo', 'gn_w', 'gn_b', 'ffn_maa_k', 'ffn_maa_r', 'ffn_Wk', 'ffn_Wr', 'ffn_Wv')}
    del _L0_xattn_all

    def _L1_xattn_setup():
        import jax, jax.numpy as jnp
        import numpy as np
        B, Q, S1, S2 = (4, 64, 512, 512)
        D, H, K, F = (512, 16, 128, 2048)
        LN_EPS = 1e-05

        def _layer_norm(x, scale, offset):
            mu = jnp.mean(x, axis=-1, keepdims=True)
            var = jnp.var(x, axis=-1, keepdims=True)
            return (x - mu) * jax.lax.rsqrt(var + LN_EPS) * scale + offset

        def _cross_attention(q_in, kv_in, wq, bq, wk, bk, wv, bv, wo, bo, bias_k, bias_v):
            b, q_len, _ = q_in.shape
            t = kv_in.shape[1]
            qh = (q_in @ wq + bq).reshape(b, q_len, H, K)
            kh = (kv_in @ wk + bk).reshape(b, t, H, K)
            vh = (kv_in @ wv + bv).reshape(b, t, H, K)
            kh = jnp.concatenate([kh, jnp.broadcast_to(bias_k, (b, 1, H, K))], axis=1)
            vh = jnp.concatenate([vh, jnp.broadcast_to(bias_v, (b, 1, H, K))], axis=1)
            scale = jnp.sqrt(jnp.asarray(K, q_in.dtype))
            logits = jnp.einsum('bqhk,bthk->bhqt', qh, kh) / scale
            weights = jax.nn.softmax(logits, axis=-1)
            ctx = jnp.einsum('bhqt,bthk->bqhk', weights, vh).reshape(b, q_len, H * K)
            return ctx @ wo + bo

        def _forward(x, xf_1, xf_2, ln1_scale, ln1_offset, wq1, bq1, wk1, bk1, wv1, bv1, wo1, bo1, bias_k1, bias_v1, ln2_scale, ln2_offset, wq2, bq2, wk2, bk2, wv2, bv2, wo2, bo2, bias_k2, bias_v2, ln_mlp_scale, ln_mlp_offset, w_fc1, b_fc1, w_fc2, b_fc2):
            res = x
            h = _layer_norm(x, ln1_scale, ln1_offset)
            x = res + _cross_attention(h, xf_1, wq1, bq1, wk1, bk1, wv1, bv1, wo1, bo1, bias_k1, bias_v1)
            res = x
            h = _layer_norm(x, ln2_scale, ln2_offset)
            x = res + _cross_attention(h, xf_2, wq2, bq2, wk2, bk2, wv2, bv2, wo2, bo2, bias_k2, bias_v2)
            h = _layer_norm(x, ln_mlp_scale, ln_mlp_offset)
            h = jax.nn.gelu(h @ w_fc1 + b_fc1, approximate=False) @ w_fc2 + b_fc2
            return x + h
        key = jax.random.key(seed)
        ks = iter(jax.random.split(key, 64))

        def rn(shape, s=0.02):
            return jax.random.normal(next(ks), shape, jnp.float32) * s
        inp = {'x': rn((B, Q, D), 1.0), 'xf_1': rn((B, S1, D), 1.0), 'xf_2': rn((B, S2, D), 1.0)}
        for i in (1, 2):
            inp[f'ln{i}_scale'] = jnp.ones((D,), jnp.float32)
            inp[f'ln{i}_offset'] = jnp.zeros((D,), jnp.float32)
            inp[f'wq{i}'] = rn((D, H * K))
            inp[f'bq{i}'] = jnp.zeros((H * K,), jnp.float32)
            inp[f'wk{i}'] = rn((D, H * K))
            inp[f'bk{i}'] = jnp.zeros((H * K,), jnp.float32)
            inp[f'wv{i}'] = rn((D, H * K))
            inp[f'bv{i}'] = jnp.zeros((H * K,), jnp.float32)
            inp[f'wo{i}'] = rn((H * K, D))
            inp[f'bo{i}'] = jnp.zeros((D,), jnp.float32)
            inp[f'bias_k{i}'] = rn((1, 1, H, K))
            inp[f'bias_v{i}'] = rn((1, 1, H, K))
        inp['ln_mlp_scale'] = jnp.ones((D,), jnp.float32)
        inp['ln_mlp_offset'] = jnp.zeros((D,), jnp.float32)
        inp['w_fc1'] = rn((D, F))
        inp['b_fc1'] = jnp.zeros((F,), jnp.float32)
        inp['w_fc2'] = rn((F, D))
        inp['b_fc2'] = jnp.zeros((D,), jnp.float32)
        return inp
    _L1_xattn_all = _L1_xattn_setup()
    _L1_xattn_in = {k: v for k, v in _L1_xattn_all.items() if k in ('ln1_scale', 'ln1_offset', 'wq1', 'bq1', 'wk1', 'bk1', 'wv1', 'bv1', 'wo1', 'bo1', 'bias_k1', 'bias_v1', 'ln2_scale', 'ln2_offset', 'wq2', 'bq2', 'wk2', 'bk2', 'wv2', 'bv2', 'wo2', 'bo2', 'bias_k2', 'bias_v2', 'ln_mlp_scale', 'ln_mlp_offset', 'w_fc1', 'b_fc1', 'w_fc2', 'b_fc2')}
    del _L1_xattn_all

    def _L2_xattn_setup():
        import jax, jax.numpy as jnp
        import numpy as np
        B, P, K, H, NH = (4, 512, 64, 512, 16)
        DH = H // NH
        EPS = 1e-06

        def rmsnorm(x, w):
            var = jnp.mean(jnp.square(x), axis=-1, keepdims=True)
            return x * jax.lax.rsqrt(var + EPS) * w
        key = jax.random.key(seed)
        ks = jax.random.split(key, 12)
        s = 0.02
        return {'x': jax.random.normal(ks[0], (B, P, H), jnp.float32), 'latents': jax.random.normal(ks[1], (B, K, H), jnp.float32), 'attention_mask': jax.random.randint(ks[2], (B, P), 0, 2, jnp.int32), 'q_w': s * jax.random.normal(ks[3], (H, H), jnp.float32), 'q_b': jnp.zeros((H,), jnp.float32), 'kv_w': s * jax.random.normal(ks[4], (H, 2 * H), jnp.float32), 'kv_b': jnp.zeros((2 * H,), jnp.float32), 'out_w': s * jax.random.normal(ks[5], (H, H), jnp.float32), 'out_b': jnp.zeros((H,), jnp.float32), 'postnorm_w': jnp.ones((H,), jnp.float32), 'mlp_w1': s * jax.random.normal(ks[6], (H, 4 * H), jnp.float32), 'mlp_b1': jnp.zeros((4 * H,), jnp.float32), 'mlp_w2': s * jax.random.normal(ks[7], (4 * H, H), jnp.float32), 'mlp_b2': jnp.zeros((H,), jnp.float32)}
    _L2_xattn_all = _L2_xattn_setup()
    _L2_xattn_in = {k: v for k, v in _L2_xattn_all.items() if k in ('q_w', 'q_b', 'kv_w', 'kv_b', 'out_w', 'out_b', 'postnorm_w', 'mlp_w1', 'mlp_b1', 'mlp_w2', 'mlp_b2')}
    del _L2_xattn_all

    def _L3_xattn_setup():
        import jax, jax.numpy as jnp
        import numpy as np
        H = 512
        B, L, S = (4, 1024, 10)
        key = jax.random.key(seed)
        k1, k2, k3, k4, k5, k6 = jax.random.split(key, 6)
        scale = 1.0 / np.sqrt(H)
        return {'h_english': jax.random.normal(k1, (B, L, H), dtype=jnp.float32), 'h_lojban': jax.random.normal(k2, (B, S, H), dtype=jnp.float32), 'w_q': jax.random.normal(k3, (H, H), dtype=jnp.float32) * scale, 'w_k': jax.random.normal(k4, (H, H), dtype=jnp.float32) * scale, 'w_v': jax.random.normal(k5, (H, H), dtype=jnp.float32) * scale, 'w_o': jax.random.normal(k6, (H, H), dtype=jnp.float32) * scale, 'alpha': jnp.float32(0.1)}
    _L3_xattn_all = _L3_xattn_setup()
    _L3_xattn_in = {k: v for k, v in _L3_xattn_all.items() if k in ('w_q', 'w_k', 'w_v', 'w_o', 'alpha')}
    del _L3_xattn_all
    return {'x': x, 'ctx_2048': ctx_2048, 'mask_BxS2_ik0': mask_BxS2_ik0, 'L0_xattn_ln1_w': _L0_xattn_in['ln1_w'], 'L0_xattn_ln1_b': _L0_xattn_in['ln1_b'], 'L0_xattn_ln2_w': _L0_xattn_in['ln2_w'], 'L0_xattn_ln2_b': _L0_xattn_in['ln2_b'], 'L0_xattn_maa_x': _L0_xattn_in['maa_x'], 'L0_xattn_maa_w1': _L0_xattn_in['maa_w1'], 'L0_xattn_maa_w2': _L0_xattn_in['maa_w2'], 'L0_xattn_maa_stack': _L0_xattn_in['maa_stack'], 'L0_xattn_time_decay': _L0_xattn_in['time_decay'], 'L0_xattn_decay_w1': _L0_xattn_in['decay_w1'], 'L0_xattn_decay_w2': _L0_xattn_in['decay_w2'], 'L0_xattn_faaaa': _L0_xattn_in['faaaa'], 'L0_xattn_Wr': _L0_xattn_in['Wr'], 'L0_xattn_Wk': _L0_xattn_in['Wk'], 'L0_xattn_Wv': _L0_xattn_in['Wv'], 'L0_xattn_Wg': _L0_xattn_in['Wg'], 'L0_xattn_Wo': _L0_xattn_in['Wo'], 'L0_xattn_gn_w': _L0_xattn_in['gn_w'], 'L0_xattn_gn_b': _L0_xattn_in['gn_b'], 'L0_xattn_ffn_maa_k': _L0_xattn_in['ffn_maa_k'], 'L0_xattn_ffn_maa_r': _L0_xattn_in['ffn_maa_r'], 'L0_xattn_ffn_Wk': _L0_xattn_in['ffn_Wk'], 'L0_xattn_ffn_Wr': _L0_xattn_in['ffn_Wr'], 'L0_xattn_ffn_Wv': _L0_xattn_in['ffn_Wv'], 'L1_xattn_ln1_scale': _L1_xattn_in['ln1_scale'], 'L1_xattn_ln1_offset': _L1_xattn_in['ln1_offset'], 'L1_xattn_wq1': _L1_xattn_in['wq1'], 'L1_xattn_bq1': _L1_xattn_in['bq1'], 'L1_xattn_wk1': _L1_xattn_in['wk1'], 'L1_xattn_bk1': _L1_xattn_in['bk1'], 'L1_xattn_wv1': _L1_xattn_in['wv1'], 'L1_xattn_bv1': _L1_xattn_in['bv1'], 'L1_xattn_wo1': _L1_xattn_in['wo1'], 'L1_xattn_bo1': _L1_xattn_in['bo1'], 'L1_xattn_bias_k1': _L1_xattn_in['bias_k1'], 'L1_xattn_bias_v1': _L1_xattn_in['bias_v1'], 'L1_xattn_ln2_scale': _L1_xattn_in['ln2_scale'], 'L1_xattn_ln2_offset': _L1_xattn_in['ln2_offset'], 'L1_xattn_wq2': _L1_xattn_in['wq2'], 'L1_xattn_bq2': _L1_xattn_in['bq2'], 'L1_xattn_wk2': _L1_xattn_in['wk2'], 'L1_xattn_bk2': _L1_xattn_in['bk2'], 'L1_xattn_wv2': _L1_xattn_in['wv2'], 'L1_xattn_bv2': _L1_xattn_in['bv2'], 'L1_xattn_wo2': _L1_xattn_in['wo2'], 'L1_xattn_bo2': _L1_xattn_in['bo2'], 'L1_xattn_bias_k2': _L1_xattn_in['bias_k2'], 'L1_xattn_bias_v2': _L1_xattn_in['bias_v2'], 'L1_xattn_ln_mlp_scale': _L1_xattn_in['ln_mlp_scale'], 'L1_xattn_ln_mlp_offset': _L1_xattn_in['ln_mlp_offset'], 'L1_xattn_w_fc1': _L1_xattn_in['w_fc1'], 'L1_xattn_b_fc1': _L1_xattn_in['b_fc1'], 'L1_xattn_w_fc2': _L1_xattn_in['w_fc2'], 'L1_xattn_b_fc2': _L1_xattn_in['b_fc2'], 'L2_xattn_q_w': _L2_xattn_in['q_w'], 'L2_xattn_q_b': _L2_xattn_in['q_b'], 'L2_xattn_kv_w': _L2_xattn_in['kv_w'], 'L2_xattn_kv_b': _L2_xattn_in['kv_b'], 'L2_xattn_out_w': _L2_xattn_in['out_w'], 'L2_xattn_out_b': _L2_xattn_in['out_b'], 'L2_xattn_postnorm_w': _L2_xattn_in['postnorm_w'], 'L2_xattn_mlp_w1': _L2_xattn_in['mlp_w1'], 'L2_xattn_mlp_b1': _L2_xattn_in['mlp_b1'], 'L2_xattn_mlp_w2': _L2_xattn_in['mlp_w2'], 'L2_xattn_mlp_b2': _L2_xattn_in['mlp_b2'], 'L3_xattn_w_q': _L3_xattn_in['w_q'], 'L3_xattn_w_k': _L3_xattn_in['w_k'], 'L3_xattn_w_v': _L3_xattn_in['w_v'], 'L3_xattn_w_o': _L3_xattn_in['w_o'], 'L3_xattn_alpha': _L3_xattn_in['alpha']}

def reference(x, ctx_2048, mask_BxS2_ik0, L0_xattn_ln1_w, L0_xattn_ln1_b, L0_xattn_ln2_w, L0_xattn_ln2_b, L0_xattn_maa_x, L0_xattn_maa_w1, L0_xattn_maa_w2, L0_xattn_maa_stack, L0_xattn_time_decay, L0_xattn_decay_w1, L0_xattn_decay_w2, L0_xattn_faaaa, L0_xattn_Wr, L0_xattn_Wk, L0_xattn_Wv, L0_xattn_Wg, L0_xattn_Wo, L0_xattn_gn_w, L0_xattn_gn_b, L0_xattn_ffn_maa_k, L0_xattn_ffn_maa_r, L0_xattn_ffn_Wk, L0_xattn_ffn_Wr, L0_xattn_ffn_Wv, L1_xattn_ln1_scale, L1_xattn_ln1_offset, L1_xattn_wq1, L1_xattn_bq1, L1_xattn_wk1, L1_xattn_bk1, L1_xattn_wv1, L1_xattn_bv1, L1_xattn_wo1, L1_xattn_bo1, L1_xattn_bias_k1, L1_xattn_bias_v1, L1_xattn_ln2_scale, L1_xattn_ln2_offset, L1_xattn_wq2, L1_xattn_bq2, L1_xattn_wk2, L1_xattn_bk2, L1_xattn_wv2, L1_xattn_bv2, L1_xattn_wo2, L1_xattn_bo2, L1_xattn_bias_k2, L1_xattn_bias_v2, L1_xattn_ln_mlp_scale, L1_xattn_ln_mlp_offset, L1_xattn_w_fc1, L1_xattn_b_fc1, L1_xattn_w_fc2, L1_xattn_b_fc2, L2_xattn_q_w, L2_xattn_q_b, L2_xattn_kv_w, L2_xattn_kv_b, L2_xattn_out_w, L2_xattn_out_b, L2_xattn_postnorm_w, L2_xattn_mlp_w1, L2_xattn_mlp_b1, L2_xattn_mlp_w2, L2_xattn_mlp_b2, L3_xattn_w_q, L3_xattn_w_k, L3_xattn_w_v, L3_xattn_w_o, L3_xattn_alpha):
    import jax
    import jax.numpy as jnp

    def _L0_xattn_ref(x, state, ln1_w, ln1_b, ln2_w, ln2_b, maa_x, maa_w1, maa_w2, maa_stack, time_decay, decay_w1, decay_w2, faaaa, Wr, Wk, Wv, Wg, Wo, gn_w, gn_b, ffn_maa_k, ffn_maa_r, ffn_Wk, ffn_Wr, ffn_Wv, i):
        import jax, jax.numpy as jnp
        import numpy as np
        B, L, E, H = (4, 128, 512, 32)
        S = E // H
        EXTRA_MAA, EXTRA_DECAY = (32, 64)
        EPS = 1e-05

        def _ln(x, w, b):
            m = jnp.mean(x, axis=-1, keepdims=True)
            v = jnp.mean((x - m) ** 2, axis=-1, keepdims=True)
            return (x - m) * jax.lax.rsqrt(v + EPS) * w + b

        def _token_shift(xn, prev_row):
            first = (prev_row - xn[:, 0])[:, None]
            rest = xn[:, :-1] - xn[:, 1:]
            return jnp.concatenate([first, rest], axis=1)
        b, l = (x.shape[0], x.shape[1])
        i0 = (2 + S) * i + 0
        i1 = (2 + S) * i + 1
        xn = _ln(x, ln1_w, ln1_b)
        sx = _token_shift(xn, state[:, i1])
        xxx = jnp.tanh((xn + sx * maa_x) @ maa_w1).reshape(b, l, 5, 1, EXTRA_MAA)
        xxx = jnp.matmul(xxx, maa_w2).reshape(b, l, 5, E)
        x5 = xn[:, :, None] + sx[:, :, None] * (maa_stack + xxx)
        w = jnp.exp(-jnp.exp(time_decay + jnp.tanh(x5[:, :, 1] @ decay_w1) @ decay_w2))
        w = w.reshape(b, l, H, S)
        r = (x5[:, :, 3] @ Wr.T).reshape(b, l, H, S)
        k = (x5[:, :, 0] @ Wk.T).reshape(b, l, H, S)
        v = (x5[:, :, 2] @ Wv.T).reshape(b, l, H, S)
        g = jax.nn.silu(x5[:, :, 4] @ Wg.T)
        s0 = state[:, (2 + S) * i + 2:(2 + S) * (i + 1)].reshape(b, H, S, S)
        u = faaaa[None, :, :, None]

        def step(s, rkvw):
            r_t, k_t, v_t, w_t = rkvw
            a = k_t[:, :, :, None] * v_t[:, :, None, :]
            out = jnp.einsum('bhk,bhkd->bhd', r_t, u * a + s)
            return (a + w_t[:, :, :, None] * s, out)
        xs = tuple((jnp.moveaxis(t, 1, 0) for t in (r, k, v, w)))
        _, outs = jax.lax.scan(step, s0, xs)
        att = jnp.moveaxis(outs, 0, 1).reshape(b, l, E)
        a4 = att.reshape(b, l, H, S)
        m = jnp.mean(a4, axis=-1, keepdims=True)
        var = jnp.mean((a4 - m) ** 2, axis=-1, keepdims=True)
        att = ((a4 - m) * jax.lax.rsqrt(var + EPS)).reshape(b, l, E) * gn_w + gn_b
        x = x + att * g @ Wo.T
        xn2 = _ln(x, ln2_w, ln2_b)
        sx2 = _token_shift(xn2, state[:, i0])
        xk = xn2 + sx2 * ffn_maa_k
        xr = xn2 + sx2 * ffn_maa_r
        rr = jax.nn.sigmoid(xr @ ffn_Wr.T)
        kk = jnp.square(jax.nn.relu(xk @ ffn_Wk.T))
        x = x + rr * (kk @ ffn_Wv.T)
        return x

    def _L1_xattn_ref(x, xf_1, xf_2, ln1_scale, ln1_offset, wq1, bq1, wk1, bk1, wv1, bv1, wo1, bo1, bias_k1, bias_v1, ln2_scale, ln2_offset, wq2, bq2, wk2, bk2, wv2, bv2, wo2, bo2, bias_k2, bias_v2, ln_mlp_scale, ln_mlp_offset, w_fc1, b_fc1, w_fc2, b_fc2):
        import jax, jax.numpy as jnp
        import numpy as np
        B, Q, S1, S2 = (4, 64, 512, 512)
        D, H, K, F = (512, 16, 128, 2048)
        LN_EPS = 1e-05

        def _layer_norm(x, scale, offset):
            mu = jnp.mean(x, axis=-1, keepdims=True)
            var = jnp.var(x, axis=-1, keepdims=True)
            return (x - mu) * jax.lax.rsqrt(var + LN_EPS) * scale + offset

        def _cross_attention(q_in, kv_in, wq, bq, wk, bk, wv, bv, wo, bo, bias_k, bias_v):
            b, q_len, _ = q_in.shape
            t = kv_in.shape[1]
            qh = (q_in @ wq + bq).reshape(b, q_len, H, K)
            kh = (kv_in @ wk + bk).reshape(b, t, H, K)
            vh = (kv_in @ wv + bv).reshape(b, t, H, K)
            kh = jnp.concatenate([kh, jnp.broadcast_to(bias_k, (b, 1, H, K))], axis=1)
            vh = jnp.concatenate([vh, jnp.broadcast_to(bias_v, (b, 1, H, K))], axis=1)
            scale = jnp.sqrt(jnp.asarray(K, q_in.dtype))
            logits = jnp.einsum('bqhk,bthk->bhqt', qh, kh) / scale
            weights = jax.nn.softmax(logits, axis=-1)
            ctx = jnp.einsum('bhqt,bthk->bqhk', weights, vh).reshape(b, q_len, H * K)
            return ctx @ wo + bo

        def _forward(x, xf_1, xf_2, ln1_scale, ln1_offset, wq1, bq1, wk1, bk1, wv1, bv1, wo1, bo1, bias_k1, bias_v1, ln2_scale, ln2_offset, wq2, bq2, wk2, bk2, wv2, bv2, wo2, bo2, bias_k2, bias_v2, ln_mlp_scale, ln_mlp_offset, w_fc1, b_fc1, w_fc2, b_fc2):
            res = x
            h = _layer_norm(x, ln1_scale, ln1_offset)
            x = res + _cross_attention(h, xf_1, wq1, bq1, wk1, bk1, wv1, bv1, wo1, bo1, bias_k1, bias_v1)
            res = x
            h = _layer_norm(x, ln2_scale, ln2_offset)
            x = res + _cross_attention(h, xf_2, wq2, bq2, wk2, bk2, wv2, bv2, wo2, bo2, bias_k2, bias_v2)
            h = _layer_norm(x, ln_mlp_scale, ln_mlp_offset)
            h = jax.nn.gelu(h @ w_fc1 + b_fc1, approximate=False) @ w_fc2 + b_fc2
            return x + h
        return _forward(x, xf_1, xf_2, ln1_scale, ln1_offset, wq1, bq1, wk1, bk1, wv1, bv1, wo1, bo1, bias_k1, bias_v1, ln2_scale, ln2_offset, wq2, bq2, wk2, bk2, wv2, bv2, wo2, bo2, bias_k2, bias_v2, ln_mlp_scale, ln_mlp_offset, w_fc1, b_fc1, w_fc2, b_fc2)

    def _L2_xattn_ref(x, latents, attention_mask, q_w, q_b, kv_w, kv_b, out_w, out_b, postnorm_w, mlp_w1, mlp_b1, mlp_w2, mlp_b2):
        import jax, jax.numpy as jnp
        import numpy as np
        B, P, K, H, NH = (4, 512, 64, 512, 16)
        DH = H // NH
        EPS = 1e-06

        def rmsnorm(x, w):
            var = jnp.mean(jnp.square(x), axis=-1, keepdims=True)
            return x * jax.lax.rsqrt(var + EPS) * w
        b, p, _ = x.shape
        k_len = latents.shape[1]
        residual = latents
        h = jnp.concatenate([x, latents], axis=1)
        q = (latents @ q_w + q_b).reshape(b, k_len, NH, DH)
        kv = (h @ kv_w + kv_b).reshape(b, p + k_len, NH, DH, 2)
        kmat, v = (kv[..., 0], kv[..., 1])
        attn = jnp.einsum('bkhd,bnhd->bhkn', q, kmat) / DH
        full_mask = jnp.concatenate([attention_mask.astype(bool), jnp.ones((b, k_len), bool)], axis=-1)
        attn = jnp.where(full_mask[:, None, None, :], attn, -jnp.inf)
        attn = jax.nn.softmax(attn.astype(jnp.float32), axis=-1).astype(q.dtype)
        attn_out = jnp.einsum('bhkn,bnhd->bkhd', attn, v).reshape(b, k_len, H)
        attn_out = attn_out @ out_w + out_b + residual
        out = rmsnorm(attn_out, postnorm_w)
        out = jax.nn.gelu(out @ mlp_w1 + mlp_b1) @ mlp_w2 + mlp_b2
        return out + residual

    def _L3_xattn_ref(h_english, h_lojban, w_q, w_k, w_v, w_o, alpha):
        import jax, jax.numpy as jnp
        import numpy as np
        H = 512
        B, L, S = (4, 1024, 10)
        h = h_english.shape[-1]
        q = jnp.einsum('blh,oh->blo', h_english, w_q)
        k = jnp.einsum('bsh,oh->bso', h_lojban, w_k)
        v = jnp.einsum('bsh,oh->bso', h_lojban, w_v)
        scores = jnp.einsum('blh,bsh->bls', q, k) / jnp.sqrt(jnp.float32(h))
        probs = jax.nn.softmax(scores, axis=-1)
        context = jnp.einsum('bls,bsh->blh', probs, v)
        delta = jnp.einsum('blh,oh->blo', context, w_o)
        return h_english + alpha * delta
    x = _L0_xattn_ref(x, ctx_2048, L0_xattn_ln1_w, L0_xattn_ln1_b, L0_xattn_ln2_w, L0_xattn_ln2_b, L0_xattn_maa_x, L0_xattn_maa_w1, L0_xattn_maa_w2, L0_xattn_maa_stack, L0_xattn_time_decay, L0_xattn_decay_w1, L0_xattn_decay_w2, L0_xattn_faaaa, L0_xattn_Wr, L0_xattn_Wk, L0_xattn_Wv, L0_xattn_Wg, L0_xattn_Wo, L0_xattn_gn_w, L0_xattn_gn_b, L0_xattn_ffn_maa_k, L0_xattn_ffn_maa_r, L0_xattn_ffn_Wk, L0_xattn_ffn_Wr, L0_xattn_ffn_Wv, 0)
    x = _L1_xattn_ref(x, ctx_2048, ctx_2048, L1_xattn_ln1_scale, L1_xattn_ln1_offset, L1_xattn_wq1, L1_xattn_bq1, L1_xattn_wk1, L1_xattn_bk1, L1_xattn_wv1, L1_xattn_bv1, L1_xattn_wo1, L1_xattn_bo1, L1_xattn_bias_k1, L1_xattn_bias_v1, L1_xattn_ln2_scale, L1_xattn_ln2_offset, L1_xattn_wq2, L1_xattn_bq2, L1_xattn_wk2, L1_xattn_bk2, L1_xattn_wv2, L1_xattn_bv2, L1_xattn_wo2, L1_xattn_bo2, L1_xattn_bias_k2, L1_xattn_bias_v2, L1_xattn_ln_mlp_scale, L1_xattn_ln_mlp_offset, L1_xattn_w_fc1, L1_xattn_b_fc1, L1_xattn_w_fc2, L1_xattn_b_fc2)
    x = _L2_xattn_ref(ctx_2048, x, mask_BxS2_ik0, L2_xattn_q_w, L2_xattn_q_b, L2_xattn_kv_w, L2_xattn_kv_b, L2_xattn_out_w, L2_xattn_out_b, L2_xattn_postnorm_w, L2_xattn_mlp_w1, L2_xattn_mlp_b1, L2_xattn_mlp_w2, L2_xattn_mlp_b2)
    x = _L3_xattn_ref(x, ctx_2048, L3_xattn_w_q, L3_xattn_w_k, L3_xattn_w_v, L3_xattn_w_o, L3_xattn_alpha)
    return x

_drawn_inputs = setup_inputs


def setup_inputs(seed=0):
    import zlib

    import numpy as np

    out = dict(_drawn_inputs(seed))
    spreads = {'L0_xattn_ln1_w': (1.0, 0.2),
     'L0_xattn_ln1_b': (0.0, 0.271),
     'L0_xattn_ln2_w': (1.0, 0.6),
     'L0_xattn_ln2_b': (0.0, 0.8),
     'L0_xattn_gn_w': (1.0, 0.6),
     'L0_xattn_gn_b': (0.0, 0.695),
     'L1_xattn_ln1_scale': (1.0, 0.6),
     'L1_xattn_ln1_offset': (0.0, 0.8),
     'L1_xattn_bq1': (0.0, 2.0),
     'L1_xattn_bk1': (0.0, 0.8),
     'L1_xattn_bv1': (0.0, 0.1),
     'L1_xattn_bo1': (0.0, 0.1),
     'L1_xattn_ln2_scale': (1.0, 0.6),
     'L1_xattn_ln2_offset': (0.0, 0.8),
     'L1_xattn_bq2': (0.0, 2.0),
     'L1_xattn_bk2': (0.0, 0.8),
     'L1_xattn_bv2': (0.0, 0.1),
     'L1_xattn_bo2': (0.0, 0.1),
     'L1_xattn_ln_mlp_scale': (1.0, 0.2),
     'L1_xattn_ln_mlp_offset': (0.0, 0.344),
     'L1_xattn_b_fc1': (0.0, 0.1),
     'L1_xattn_b_fc2': (0.0, 0.1),
     'L2_xattn_q_b': (0.0, 0.8),
     'L2_xattn_kv_b': (0.0, 0.8),
     'L2_xattn_out_b': (0.0, 1.1),
     'L2_xattn_postnorm_w': (1.0, 0.2),
     'L2_xattn_mlp_b1': (0.0, 0.1),
     'L2_xattn_mlp_b2': (0.0, 0.1)}
    factors = {'L0_xattn_maa_x': 8.0,
     'L0_xattn_maa_w1': 2.942,
     'L0_xattn_maa_w2': 2.988,
     'L0_xattn_maa_stack': 6.522,
     'L0_xattn_decay_w1': 8.0,
     'L0_xattn_decay_w2': 8.0,
     'L0_xattn_faaaa': 3.012,
     'L0_xattn_ffn_maa_k': 8.0,
     'L0_xattn_ffn_maa_r': 8.0,
     'L0_xattn_ffn_Wr': 4.245,
     'L1_xattn_wq1': 8.0,
     'L1_xattn_wk1': 8.0,
     'L1_xattn_wv1': 2.794,
     'L1_xattn_bias_k1': 33.214,
     'L1_xattn_bias_v1': 8.0,
     'L1_xattn_wq2': 8.0,
     'L1_xattn_wk2': 8.0,
     'L1_xattn_wv2': 2.849,
     'L1_xattn_bias_k2': 25.3,
     'L1_xattn_bias_v2': 8.0,
     'L2_xattn_q_w': 8.0,
     'L2_xattn_kv_w': 6.849,
     'L2_xattn_out_w': 4.914,
     'L3_xattn_w_q': 8.0,
     'L3_xattn_w_k': 8.0,
     'L3_xattn_w_v': 8.0,
     'L3_xattn_w_o': 8.0}
    for name, (base, spread) in spreads.items():
        noise = np.random.default_rng([zlib.crc32(name.encode()), seed]).standard_normal(out[name].shape)
        drawn = base * np.exp(spread * noise) if base else spread * noise
        out[name] = jnp.asarray(drawn.astype(out[name].dtype))
    for name, factor in factors.items():
        out[name] = (out[name] * factor).astype(out[name].dtype)
    return out
```

```python
from contextlib import ExitStack

import numpy as np

import concourse.bass as bass
from concourse import mybir

F32 = mybir.dt.float32
F32R = mybir.dt.float32r
I32 = mybir.dt.int32
ACT = mybir.ActivationFunctionType
ALU = mybir.AluOpType
AX = mybir.AxisListType

P = 128
B, T, D = 8, 112, 512
S = 375
SP = S + 1
C = D // P
NT = B * T
HALF = NT // 2
HB = B // 2
H0, S0 = 32, 16
HK, G = 4, 4
KTILES = [(0, 128), (128, 128), (256, SP - 256)]
KTILES2 = KTILES + [(SP, T)]
SK2 = SP + T
H2, D2 = 16, 32
GAP = -1.0e30
SCALE1 = 128.0 ** -0.5
SCALE2 = 1.0 / D2
SCALE3 = float(D) ** -0.5

VECTORS = [
    ("ln1_w", 4), ("ln1_b", 4), ("maa_x", 4), ("maa_0", 4), ("maa_1", 4), ("maa_2", 4), ("maa_3", 4),
    ("maa_4", 4), ("time_decay", 4), ("u", 4), ("gn_w", 4), ("gn_b", 4), ("ln2_w", 4), ("ln2_b", 4),
    ("ffn_maa_k", 4), ("ffn_maa_r", 4),
    ("a1_s", 4), ("a1_o", 4), ("a2_s", 4), ("a2_o", 4), ("am_s", 4), ("am_o", 4), ("post_w", 4),
    ("q2_b", 4), ("k2_b", 4), ("alpha", 1),
    ("bq1", 16), ("bk1", 16), ("bq2", 16), ("bk2", 16), ("bias_k1", 16), ("bias_k2", 16),
    ("b_fc1", 16), ("mlp_b1", 16),
]
VEC_AT, _n = {}, 0
for _name, _w in VECTORS:
    VEC_AT[_name] = (_n, _w)
    _n += _w
NVEC = _n

ROWS = ["bo1", "bo2", "b_fc2", "v2_b", "out_b", "mlp_b2"]

UNIQUE = (["k", "r", "v", "g", "o", "fr", "fk", "fv"]
          + [f"{w}{layer}_{g}" for layer in (1, 2) for g in range(G) for w in "qkvo"]
          + [f"m1{w}_{g}" for g in range(4) for w in "ab"]
          + ["p_q", "p_k", "p_v", "p_o"]
          + [f"m2{w}_{g}" for g in range(4) for w in "ab"]
          + ["e_q", "e_k", "e_v", "e_o"])
ORDER = ["k", "r", "v", "g", "o"] + UNIQUE
NSLOT = 4


def build(nc, x_in, ctx_in, ctxT_in, prev_in, s0_in, mask_in, w_in, vec_in, rows_in, bv_in,
          maa_w1_in, maa_w2_in, dec_w1_in, dec_w2_in, ident_in, heads_in, place_in, pick_in_dram, out):
    stack = ExitStack()
    phase = [stack.enter_context(ExitStack())]

    def sem(name):
        return stack.enter_context(nc.semaphore(name))

    class Engine:

        def __init__(self, eng, name):
            self.eng, self.sem, self.count, self.seen = eng, sem(name), 0, {}

        def wait(self, *tokens):
            for token in tokens:
                if token is None:
                    continue
                if isinstance(token, list):
                    self.wait(*token)
                    continue
                s, n = token
                if self.seen.get(s.name, 0) < n:
                    self.eng.wait_ge(s, n)
                    self.seen[s.name] = n

        def done(self, instruction):
            self.count += 1
            instruction.then_inc(self.sem, 1)
            return (self.sem, self.count)

        def last(self):
            return (self.sem, self.count) if self.count else None

    pe = Engine(nc.tensor, "pe_done")
    act = Engine(nc.scalar, "act_done")
    dve = Engine(nc.vector, "dve_done")
    pool = Engine(nc.gpsimd, "pool_done")
    sp = Engine(nc.sync, "sp_unused")

    class Stream:

        def __init__(self, name):
            self.sem, self.count = sem(name), 0

        def start(self, dst, src, *after):
            sp.wait((self.sem, self.count) if self.count else None, *after)
            sp.eng.dma_start(dst, src).then_inc(self.sem, 16)
            self.count += 16
            return (self.sem, self.count)

    def sb(name, shape, dt=F32):
        return phase[-1].enter_context(nc.sbuf_tensor(name, shape, dt))

    def new_phase(keep=()):
        tokens = [e.last() for e in (pe, act, dve, pool)] + list(keep)
        for e in (pe, act, dve, pool, sp):
            e.wait(*tokens)
        if len(phase) > 1:
            phase.pop().close()
        phase.append(ExitStack())
        stack.enter_context(phase[-1])

    Wh = sb("W_hi", [P, NSLOT, C, D], F32R)
    Wl = sb("W_lo", [P, NSLOT, C, D], F32R)
    Wraw = sb("W_raw", [P, C, D])
    X = sb("residual", [T, B, D])
    Hh = sb("act_hi", [P, C, NT], F32R)
    Hl = sb("act_lo", [P, C, NT], F32R)
    vec = sb("vectors", [P, NVEC])
    ident = sb("ident", [P, P])
    stats = sb("stats", [T, 2, 6])
    mv = sb("mean_var", [T, 2, 2])
    rstd = sb("rstd", [T, 2, 2])
    minus_half = sb("minus_half", [T, 1])
    bank = [stack.enter_context(nc.psum_tensor(f"bank{i}", [P, 512], F32)) for i in range(8)]

    def V(name, i, n=P):
        return vec[0:n, VEC_AT[name][0] + i:VEC_AT[name][0] + i + 1]

    class Ring:

        def __init__(self, banks):
            self.banks, self.free, self.at = banks, {b: None for b in banks}, 0

        def take(self):
            i = self.banks[self.at % len(self.banks)]
            self.at += 1
            pe.wait(self.free[i])
            return i

    const = sem("const")
    n_const = 0
    for dst, src in ((vec[:], vec_in), (ident[:], ident_in), (X[:], x_in.rearrange("b t d -> t b d"))):
        nc.sync.dma_start(dst, src).then_inc(const, 16)
        n_const += 16
    constants = (const, n_const)
    zeroed = [dve.done(nc.vector.memset(bank[i][:], 0.0)) for i in range(8)]
    t_mh = dve.done(nc.vector.memset(minus_half[:], -0.5))
    for e in (pe, act, dve, pool):
        e.wait(constants, t_mh)
    pe.wait(zeroed)
    act.wait(zeroed)

    w_stream = Stream("w_loaded")
    w_state = {"staged": 0, "split": 0, "raw_free": None, "loaded": None}
    w_ready = {}
    w_free = {}

    def stage_next_weight():
        n = w_state["staged"]
        if n < len(ORDER):
            w_state["loaded"] = w_stream.start(Wraw[:], w_in[UNIQUE.index(ORDER[n])], w_state["raw_free"])
            w_state["staged"] += 1

    def split_weights():
        while w_state["split"] < len(ORDER):
            n = w_state["split"]
            if n >= NSLOT and (n - NSLOT) not in w_free:
                return
            slot, free = n % NSLOT, w_free.get(n - NSLOT)
            act.wait(w_state["loaded"], free)
            his, los = [], []
            for c in range(0, C, 2):
                his.append(act.done(nc.scalar.copy(Wh[:, slot, c:c + 2, :], Wraw[:, c:c + 2, :])))
            pool.wait(w_state["loaded"], free)
            for i, c in enumerate(range(0, C, 2)):
                pool.wait(his[i])
                los.append(pool.done(nc.gpsimd.tensor_tensor(
                    Wl[:, slot, c:c + 2, :], Wraw[:, c:c + 2, :], Wh[:, slot, c:c + 2, :].bitcast(F32),
                    ALU.subtract)))
            w_ready[n] = his + los
            w_state["raw_free"] = his + los
            w_state["split"] += 1
            stage_next_weight()

    w_state["use"] = 0

    class Weight:

        def __init__(self, name):
            self.n = w_state["use"]
            assert ORDER[self.n] == name, (ORDER[self.n], name)
            w_state["use"] += 1
            self.slot = self.n % NSLOT

        def need(self):
            pe.wait(w_ready[self.n])

        def block(self, c, a, n):
            return Wh[:, self.slot, c, a:a + n], Wl[:, self.slot, c, a:a + n]

        def give_up(self):
            w_free[self.n] = [pe.last()]
            split_weights()

    stage_next_weight()
    split_weights()

    def mm3(dst, left, right, first, last):
        nc.tensor.matmul(dst, left[0], right[0], start=first, stop=False)
        nc.tensor.matmul(dst, left[0], right[1], start=False, stop=False)
        return nc.tensor.matmul(dst, left[1], right[0], start=False, stop=last)

    def split_psum(src, hi, lo, ready, free=(), bias=None):
        act.wait(ready, *free)
        if bias is None:
            t_hi = act.done(nc.scalar.copy(hi, src))
        else:
            t_hi = act.done(nc.scalar.activation(hi, src, ACT.Identity, bias=bias))
        dve.wait(ready, t_hi, *free)
        if bias is None:
            t_lo = dve.done(nc.vector.tensor_tensor(lo, src, hi.bitcast(F32), ALU.subtract))
        else:
            t_lo = dve.done(nc.vector.scalar_tensor_tensor(
                out=lo, in0=src, scalar=bias, in1=hi.bitcast(F32), op0=ALU.add, op1=ALU.subtract))
        return [t_hi, t_lo]

    def split_sbuf(src, hi, lo, ready, free=()):
        act.wait(ready, *free)
        t_hi = act.done(nc.scalar.copy(hi, src))
        pool.wait(ready, t_hi, *free)
        t_lo = pool.done(nc.gpsimd.tensor_tensor(lo, src, hi.bitcast(F32), ALU.subtract))
        return [t_hi, t_lo]

    def inverse_root(b, src, eps, ready):
        dve.wait(ready)
        t = dve.done(nc.vector.tensor_scalar(rstd[:, b % 2, 1:2], src, eps, None, ALU.add))
        pool.wait(t)
        return pool.done(nc.gpsimd.tensor_tensor(rstd[:, b % 2, 0:1], rstd[:, b % 2, 1:2],
                                                 minus_half[:], ALU.pow))

    def normalise(b, src, z, ready, z_free, eps=1e-5):
        dve.wait(ready)
        t = dve.done(nc.vector.bn_stats(stats[:, b % 2, :], src))
        dve.wait(t)
        t = dve.done(nc.vector.bn_aggr(mv[:, b % 2, :], stats[:, b % 2, :]))
        t = inverse_root(b, mv[:, b % 2, 1:2], eps, t)
        dve.wait(t, z_free)
        return dve.done(nc.vector.tensor_scalar(z, src, mv[:, b % 2, 0:1], rstd[:, b % 2, 0:1],
                                                ALU.subtract, ALU.mult))

    def turn(ring, z, ready):
        i = ring.take()
        pe.wait(ready)
        for c in range(C):
            m = nc.tensor.transpose(bank[i][:, c * T:(c + 1) * T], z[:, c * P:(c + 1) * P], ident[0:T, 0:T])
        return i, pe.done(m)

    def to_channel_major(ring, b, src, z, scale, offset, dst, ready, z_free, norm=True):
        t = normalise(b, src, z, ready, z_free) if norm else ready
        i, t_turn = turn(ring, z, t)
        act.wait(t_turn)
        ts = []
        for c in range(C):
            ts.append(act.done(nc.scalar.activation(dst(c), bank[i][:, c * T:(c + 1) * T], ACT.Identity,
                                                    scale=V(scale, c), bias=V(offset, c))))
        ring.free[i] = ts
        return ts, t_turn

    new_phase()
    ring = Ring(list(range(8)))
    Z = sb("z", [T, 2, D])
    xn = sb("xn", [P, C, HB, T + 1])
    sx = sb("sx", [P, C, HB, T])
    tmp = sb("tmp", [P, 2, HB, T])
    mx = sb("mx", [P, 2, HB, T])
    x5 = sb("x5", [P, 2, HB, T])
    th = sb("th", [P, HALF])
    th4 = sb("th4", [32, HALF])
    thd = sb("thd", [64, HALF])
    kT = sb("kT", [P, C, HB, T])
    rT = sb("rT", [P, C, HB, T])
    wT = sb("wT", [P, C, HB, T + 1])
    att = sb("att", [P, C, HB, T])
    ab = sb("kv_then_state", [P, 2, HB, T + 1])
    yb = sb("y", [P, 2, HB, T])
    prev = sb("prev", [P, 2, C, B])
    s0 = sb("s0", [P, C, S0, B])
    maa_w1 = sb("maa_w1", [P, C, 160])
    maa_w2 = sb("maa_w2", [P, D])
    maa_w24 = sb("maa_w24", [32, D])
    dec_w1 = sb("dec_w1", [P, C, 64])
    dec_w2 = sb("dec_w2", [64, D])
    heads = sb("heads", [P, P])
    place = sb("place", [P, P + S0 - 1])
    pick_in = sb("pick_row", [P, S0])
    pick = sb("pick", [P, S0, P], F32R)

    c0 = sem("const0")
    n = 0
    for dst, src in ((prev[:], prev_in), (s0[:], s0_in), (maa_w1[:], maa_w1_in), (maa_w2[:], maa_w2_in[0:P]),
                     (maa_w24[:], maa_w2_in[P:P + 32]), (dec_w1[:], dec_w1_in), (dec_w2[:], dec_w2_in),
                     (heads[:], heads_in), (place[:], place_in), (pick_in[:], pick_in_dram)):
        nc.sync.dma_start(dst, src).then_inc(c0, 16)
        n += 16
    for e in (pe, act, dve, pool):
        e.wait((c0, n))
    t_ir = [dve.done(nc.vector.tensor_scalar(pick[:, d, :], heads[:], pick_in[:, d:d + 1], None, ALU.mult))
            for d in range(S0)]
    t_w0 = dve.done(nc.vector.memset(wT[:, :, :, 0:1], 0.0))
    pe.wait(t_ir)
    dve.wait(t_w0)
    Xh = [Hh[:, c, 0:HALF] for c in range(C)]
    Xl = [Hl[:, c, 0:HALF] for c in range(C)]
    vh = [Hh[:, c, HALF:NT] for c in range(C)]
    vl = [Hl[:, c, HALF:NT] for c in range(C)]

    def flat(ap):
        return ap.rearrange("p b t -> p (b t)")

    for half in range(2):
        b0 = half * HB
        half_start = [dve.last(), pool.last(), act.last(), pe.last()]
        for e in (pe, act, dve, pool):
            e.wait(half_start)
        t_xn = []
        z_free = [None, None]
        for i in range(HB):
            b = b0 + i
            ts, z_free[i % 2] = to_channel_major(ring, b, X[:, b, :], Z[:, i % 2, :], "ln1_w", "ln1_b",
                                                 lambda c: xn[:, c, i, 1:T + 1], None, z_free[i % 2])
            t_xn += ts
        t_xn.append(act.done(nc.scalar.copy(xn[:, :, :, 0], prev[:, 1, :, b0:b0 + HB])))
        t_sx = []
        pool.wait(t_xn)
        for c in range(C):
            t_sx.append(pool.done(nc.gpsimd.tensor_tensor(sx[:, c], xn[:, c, :, 0:T], xn[:, c, :, 1:T + 1],
                                                          ALU.subtract)))
        i1, i2 = ring.take(), ring.take()
        mx_free = [None, None]
        dve.wait(t_xn)
        for c in range(C):
            dve.wait(t_sx[c], mx_free[c % 2])
            t = dve.done(nc.vector.scalar_tensor_tensor(out=mx[:, c % 2], in0=sx[:, c], scalar=V("maa_x", c),
                                                        in1=xn[:, c, :, 1:T + 1], op0=ALU.mult, op1=ALU.add))
            pe.wait(t)
            nc.tensor.matmul(bank[i1][:, 0:HALF], maa_w1[:, c, 0:P], flat(mx[:, c % 2]), start=c == 0, stop=c == C - 1)
            mx_free[c % 2] = pe.done(nc.tensor.matmul(bank[i2][0:32, 0:HALF], maa_w1[:, c, P:160], flat(mx[:, c % 2]),
                                                      start=c == 0, stop=c == C - 1))
        act.wait(mx_free[1])
        t_th = [act.done(nc.scalar.activation(th[:], bank[i1][:, 0:HALF], ACT.Tanh))]
        t_th.append(act.done(nc.scalar.activation(th4[:], bank[i2][0:32, 0:HALF], ACT.Tanh)))
        ring.free[i1] = ring.free[i2] = t_th
        pe.wait(t_th)

        state = {"x_free": None, "tmp": [None, None], "x5": [None, None]}

        def mixed(j):
            out_t = []
            for c in range(C):
                i = ring.take()
                if j < 4:
                    left, right = maa_w2[32 * j:32 * j + 32, c * P:(c + 1) * P], th[32 * j:32 * j + 32, :]
                else:
                    left, right = maa_w24[:, c * P:(c + 1) * P], th4[:]
                t = pe.done(nc.tensor.matmul(bank[i][:, 0:HALF], left, right, start=True, stop=True))
                s = c % 2
                dve.wait(t, state["tmp"][s])
                t = dve.done(nc.vector.scalar_tensor_tensor(
                    out=tmp[:, s], in0=bank[i][:, 0:HALF].rearrange("p (b t) -> p b t", b=HB), scalar=V(f"maa_{j}", c),
                    in1=sx[:, c], op0=ALU.add, op1=ALU.mult))
                ring.free[i] = t
                pool.wait(t, state["x5"][s])
                t = pool.done(nc.gpsimd.tensor_tensor(x5[:, s], tmp[:, s], xn[:, c, :, 1:T + 1], ALU.add))
                state["tmp"][s] = t
                ts = split_sbuf(flat(x5[:, s]), Xh[c], Xl[c], t, [state["x_free"]])
                state["x5"][s] = ts
                out_t.append(ts)
            return out_t

        def project(weight, t_in):
            weight.need()
            for o in range(C):
                i = ring.take()
                for c in range(C):
                    pe.wait(t_in[c])
                    m = mm3(bank[i][:, 0:HALF], weight.block(c, o * P, P), (Xh[c], Xl[c]), c == 0, c == C - 1)
                yield o, i, pe.done(m)
            state["x_free"] = pe.last()
            weight.give_up()

        t_in = mixed(1)
        i = ring.take()
        for c in range(C):
            pe.wait(t_in[c])
            nc.tensor.matmul(bank[i][0:64, 0:HALF], dec_w1[:, c, :], Xh[c].bitcast(F32), start=c == 0, stop=False)
            m = nc.tensor.matmul(bank[i][0:64, 0:HALF], dec_w1[:, c, :], Xl[c].bitcast(F32), start=False, stop=c == C - 1)
        state["x_free"] = t = pe.done(m)
        act.wait(t)
        ring.free[i] = t = act.done(nc.scalar.activation(thd[:], bank[i][0:64, 0:HALF], ACT.Tanh))
        pe.wait(t)
        t_w = []
        for c in range(C):
            i = ring.take()
            t = pe.done(nc.tensor.matmul(bank[i][:, 0:HALF], dec_w2[:, c * P:(c + 1) * P], thd[:], start=True, stop=True))
            act.wait(t)
            inner = wT[:, c, :, 1:T + 1]
            ring.free[i] = t = act.done(nc.scalar.activation(
                inner, bank[i][:, 0:HALF].rearrange("p (b t) -> p b t", b=HB), ACT.Exp, bias=V("time_decay", c)))
            act.wait(t)
            t_w.append(act.done(nc.scalar.activation(inner, inner, ACT.Exp, scale=-1.0)))

        t_k, t_r, t_v = [], [], []
        for j, name, dst, ts in ((0, "k", kT, t_k), (3, "r", rT, t_r)):
            for o, i, t in project(Weight(name), mixed(j)):
                act.wait(t)
                ring.free[i] = t = act.done(nc.scalar.copy(flat(dst[:, o]), bank[i][:, 0:HALF]))
                ts.append(t)
        for o, i, t in project(Weight("v"), mixed(2)):
            ts = split_psum(bank[i][:, 0:HALF], vh[o], vl[o], t)
            ring.free[i] = ts
            t_v.append(ts)

        t_att = []
        for o in range(C):
            s = o % 2
            dve.wait(t_k[o], t_r[o], t_v[o], state["tmp"][s], state["x5"][s])
            t = dve.done(nc.vector.scalar_tensor_tensor(out=tmp[:, s], in0=rT[:, o], scalar=V("u", o), in1=kT[:, o],
                                                        op0=ALU.mult, op1=ALU.mult))
            i = ring.take()
            pe.wait(t)
            state["tmp"][s] = t = pe.done(nc.tensor.matmul(bank[i][:, 0:HALF], heads[:], flat(tmp[:, s]), start=True, stop=True))
            dve.wait(t)
            t1 = dve.done(nc.vector.tensor_tensor(flat(att[:, o]), bank[i][:, 0:HALF], vh[o].bitcast(F32), ALU.mult))
            ring.free[i] = t2 = dve.done(nc.vector.tensor_tensor(flat(x5[:, s]), bank[i][:, 0:HALF], vl[o].bitcast(F32), ALU.mult))
            dve.wait(t1, t2)
            t_att.append(dve.done(nc.vector.tensor_tensor(flat(att[:, o]), flat(att[:, o]), flat(x5[:, s]), ALU.add)))
            state["x5"][s] = t_att[-1]

        t_y = [None, None]
        ab_free, yb_free = [None, None], [None, None]
        yring = [ring.take(), ring.take()]
        n_step = 0
        pending = []

        def sum_rows(o, d, s, t):
            j = yring[o % 2]
            pe.wait(t)
            if d == 0 and o >= 2:
                pe.wait(t_y[o % 2])
            yb_free[s] = t = pe.done(nc.tensor.matmul(
                bank[j][:, 0:HALF], place[:, S0 - 1 - d:S0 - 1 - d + P], flat(yb[:, s]),
                start=d == 0, stop=d == S0 - 1))
            if d == S0 - 1:
                dve.wait(t, t_att[o])
                t_y[o % 2] = t_att[o] = dve.done(nc.vector.tensor_tensor(
                    flat(att[:, o]), bank[j][:, 0:HALF], flat(att[:, o]), ALU.add))

        vring = Ring([i for i in range(8) if i not in yring])
        vring.free = {i: ring.free[i] for i in vring.banks}
        for o in range(C):
            pe.wait(t_v[o])
            dve.wait(t_w[o])
            pool.wait(t_r[o])
            for d in range(S0):
                s = n_step % 2
                n_step += 1
                i = vring.take()
                nc.tensor.matmul(bank[i][:, 0:HALF], pick[:, d, :], vh[o], start=True, stop=False)
                t_pick = pe.done(nc.tensor.matmul(bank[i][:, 0:HALF], pick[:, d, :], vl[o], start=False, stop=True))
                pool.wait(ab_free[s])
                t_init = pool.done(nc.gpsimd.tensor_copy(ab[:, s, :, 0], s0[:, o, d, b0:b0 + HB]))
                dve.wait(t_pick, ab_free[s])
                vring.free[i] = t_kv = dve.done(nc.vector.tensor_tensor(
                    ab[:, s, :, 1:T + 1], bank[i][:, 0:HALF].rearrange("p (b t) -> p b t", b=HB), kT[:, o], ALU.mult))
                dve.wait(t_kv, t_init)
                t_scan = dve.done(nc.vector.tensor_tensor_scan(flat(ab[:, s]), flat(wT[:, o]), flat(ab[:, s]), 0.0,
                                                               ALU.mult, ALU.add))
                pool.wait(t_scan, yb_free[s])
                ab_free[s] = t = pool.done(nc.gpsimd.tensor_tensor(yb[:, s], ab[:, s, :, 0:T], rT[:, o], ALU.mult))
                pending.append((o, d, s, t))
                if len(pending) > 1:
                    sum_rows(*pending.pop(0))
        sum_rows(*pending.pop(0))
        for i in vring.banks:
            ring.free[i] = vring.free[i]
        ring.free[yring[0]] = ring.free[yring[1]] = [t_y[0], t_y[1]]

        t_g = []
        for o, i, t in project(Weight("g"), mixed(4)):
            act.wait(t, dve.last())
            ring.free[i] = t = act.done(nc.scalar.activation(flat(kT[:, o]), bank[i][:, 0:HALF], ACT.Silu))
            t_g.append(t)

        t_c = []
        for o in range(C):
            i = ring.take()
            pe.wait(t_att[o])
            t = pe.done(nc.tensor.matmul(bank[i][:, 0:HALF], heads[:], flat(att[:, o]), start=True, stop=True))
            dve.wait(t)
            ring.free[i] = t = dve.done(nc.vector.scalar_tensor_tensor(
                out=flat(att[:, o]), in0=bank[i][:, 0:HALF], scalar=-1.0 / S0, in1=flat(att[:, o]),
                op0=ALU.mult, op1=ALU.add))
            t_c.append(t)
        gt = [None, None]
        t_var = []
        for o in range(C):
            s = o % 2
            pool.wait(t_c[o], gt[s], yb_free[s])
            t = pool.done(nc.gpsimd.tensor_tensor(flat(yb[:, s]), flat(att[:, o]), flat(att[:, o]), ALU.mult))
            i = ring.take()
            pe.wait(t)
            gt[s] = t = pe.done(nc.tensor.matmul(bank[i][:, 0:HALF], heads[:], flat(yb[:, s]), start=True, stop=True))
            dve.wait(t, pool.last())
            ring.free[i] = t = dve.done(nc.vector.tensor_scalar(flat(rT[:, o]), bank[i][:, 0:HALF], 1.0 / S0, 1e-5,
                                                                ALU.mult, ALU.add))
            t_var.append(t)
        t_gn = []
        for o in range(C):
            act.wait(t_var[o])
            t = act.done(nc.scalar.activation(flat(rT[:, o]), flat(rT[:, o]), ACT.Sqrt))
            dve.wait(t)
            t = dve.done(nc.vector.reciprocal(flat(rT[:, o]), flat(rT[:, o])))
            dve.wait(t)
            t = dve.done(nc.vector.scalar_tensor_tensor(out=flat(att[:, o]), in0=flat(att[:, o]), scalar=V("gn_w", o),
                                                        in1=flat(rT[:, o]), op0=ALU.mult, op1=ALU.mult))
            dve.wait(t, t_g[o])
            t = dve.done(nc.vector.scalar_tensor_tensor(out=flat(att[:, o]), in0=flat(att[:, o]), scalar=V("gn_b", o),
                                                        in1=flat(kT[:, o]), op0=ALU.add, op1=ALU.mult))
            t_gn.append(split_sbuf(flat(att[:, o]), Xh[o], Xl[o], t, [state["x_free"]]))
        wo = Weight("o")
        wo.need()
        for i4 in range(HB):
            i = ring.take()
            for c in range(C):
                pe.wait(t_gn[c])
                m = mm3(bank[i][0:T, :], (Xh[c][:, i4 * T:(i4 + 1) * T], Xl[c][:, i4 * T:(i4 + 1) * T]),
                        wo.block(c, 0, D), c == 0, c == C - 1)
            t = pe.done(m)
            dve.wait(t)
            ring.free[i] = dve.done(nc.vector.tensor_tensor(X[:, b0 + i4, :], bank[i][0:T, :], X[:, b0 + i4, :], ALU.add))
        wo.give_up()

    new_phase()
    ring = Ring(list(range(8)))
    Z = sb("z1", [T, 2, D])
    xn = sb("xn1", [P, C, B, T + 1])
    sx = sb("sx1", [P, C, B, T])
    xm = sb("xm1", [P, 2, HB, T])
    rr = sb("rr", [T, B, D])
    kh = sb("kk_hi", [P, C, NT], F32R)
    kl = sb("kk_lo", [P, C, NT], F32R)
    prev = sb("prev1", [P, 2, C, B])
    f_tmp = sb("f_tmp", [T, 2, D])
    prev_stream = Stream("prev_loaded")
    t_prev = prev_stream.start(prev[:], prev_in)
    t_xn = []
    z_free = [None, None]
    for b in range(B):
        ts, z_free[b % 2] = to_channel_major(ring, b, X[:, b, :], Z[:, b % 2, :], "ln2_w", "ln2_b",
                                             lambda c: xn[:, c, b, 1:T + 1], None, z_free[b % 2])
        t_xn += ts
    act.wait(t_prev)
    t_xn.append(act.done(nc.scalar.copy(xn[:, :, :, 0], prev[:, 0, :, :])))
    pool.wait(t_xn)
    t_sx = [pool.done(nc.gpsimd.tensor_tensor(sx[:, c], xn[:, c, :, 0:T], xn[:, c, :, 1:T + 1], ALU.subtract))
            for c in range(C)]
    xm_free = [None, None]
    n_xm = 0

    def ffn_mix(name, h_free):
        nonlocal n_xm
        ts = {}
        for half in range(2):
            for c in range(C):
                s = n_xm % 2
                n_xm += 1
                bs = slice(half * HB, half * HB + HB)
                dve.wait(t_sx[c], t_xn[-1], xm_free[s])
                t = dve.done(nc.vector.scalar_tensor_tensor(out=xm[:, s], in0=sx[:, c, bs], scalar=V(name, c),
                                                            in1=xn[:, c, bs, 1:T + 1], op0=ALU.mult, op1=ALU.add))
                cols = slice(half * HALF, (half + 1) * HALF)
                ts[half, c] = xm_free[s] = split_sbuf(flat(xm[:, s]), Hh[:, c, cols], Hl[:, c, cols], t, [h_free])
        return ts

    t_r = ffn_mix("ffn_maa_r", None)
    w = Weight("fr")
    w.need()
    t_rr = []
    for b in range(B):
        i = ring.take()
        for c in range(C):
            pe.wait(t_r[b // HB, c])
            m = mm3(bank[i][0:T, :], (Hh[:, c, b * T:(b + 1) * T], Hl[:, c, b * T:(b + 1) * T]), w.block(c, 0, D),
                    c == 0, c == C - 1)
        t = pe.done(m)
        act.wait(t)
        ring.free[i] = t = act.done(nc.scalar.activation(rr[:, b, :], bank[i][0:T, :], ACT.Sigmoid))
        t_rr.append(t)
    w.give_up()
    t_k = ffn_mix("ffn_maa_k", pe.last())
    w = Weight("fk")
    w.need()
    t_kk = {}
    for half in range(2):
        for o in range(C):
            i = ring.take()
            for c in range(C):
                pe.wait(t_k[half, c])
                cols = slice(half * HALF, (half + 1) * HALF)
                m = mm3(bank[i][:, 0:HALF], w.block(c, o * P, P), (Hh[:, c, cols], Hl[:, c, cols]), c == 0, c == C - 1)
            t = pe.done(m)
            s = n_xm % 2
            n_xm += 1
            act.wait(t, xm_free[s])
            ring.free[i] = t = act.done(nc.scalar.activation(flat(xm[:, s]), bank[i][:, 0:HALF], ACT.Relu))
            dve.wait(t)
            t = dve.done(nc.vector.tensor_tensor(flat(xm[:, s]), flat(xm[:, s]), flat(xm[:, s]), ALU.mult))
            t_kk[half, o] = xm_free[s] = split_sbuf(flat(xm[:, s]), kh[:, o, cols], kl[:, o, cols], t)
    w.give_up()
    w = Weight("fv")
    w.need()
    ft = [None, None]
    for b in range(B):
        i = ring.take()
        for c in range(C):
            pe.wait(t_kk[b // HB, c])
            m = mm3(bank[i][0:T, :], (kh[:, c, b * T:(b + 1) * T], kl[:, c, b * T:(b + 1) * T]), w.block(c, 0, D),
                    c == 0, c == C - 1)
        t = pe.done(m)
        dve.wait(t, t_rr[b], ft[b % 2])
        ring.free[i] = t = dve.done(nc.vector.tensor_tensor(f_tmp[:, b % 2, :], bank[i][0:T, :], rr[:, b, :], ALU.mult))
        pool.wait(t)
        ft[b % 2] = pool.done(nc.gpsimd.tensor_tensor(X[:, b, :], f_tmp[:, b % 2, :], X[:, b, :], ALU.add))
    w.give_up()

    new_phase()
    Z = sb("z2", [T, 1, D])
    ctx_raw = sb("ctx_raw", [P, C, SP])
    cxh = sb("ctx_hi", [P, 2, C, SP], F32R)
    cxl = sb("ctx_lo", [P, 2, C, SP], F32R)
    qg = sb("q_group", [P, HK, NT])
    qh = sb("q_hi", [P, HK, T], F32R)
    ql = sb("q_lo", [P, HK, T], F32R)
    Kh = sb("K_hi", [P, HK, SP], F32R)
    Kl = sb("K_lo", [P, HK, SP], F32R)
    Vt = sb("V", [P, 3, D])
    Pm = sb("probs", [T, HK, SP])
    PT = sb("probs_T", [P, HK, 3, T])
    oh = sb("o_hi", [P, HK, T], F32R)
    ol = sb("o_lo", [P, HK, T], F32R)
    bv = sb("v_bias", [P, 2, D])
    mxs = sb("max", [T, HK])
    nb = sb("minus_max", [T, HK])
    ssum = sb("sum", [T, HK])
    rsum = sb("inv_sum", [T, HK])
    ctx_stream = Stream("ctx_loaded")
    bv_stream = Stream("bv_loaded")
    row_stream = Stream("row_loaded")
    row = Z[:, 0, :]

    def add_rows(name, ready):
        t_row = row_stream.start(row, rows_in[ROWS.index(name)], ready)
        dve.wait(t_row)
        return [dve.done(nc.vector.tensor_tensor(X[:, b, :], X[:, b, :], row, ALU.add)) for b in range(B)]

    def norm_all(ring, scale, offset, y, x_ready, h_free):
        t_h = [None] * B
        z_free = None
        y_free = [None, None]
        for b in range(B):
            s = b % 2
            act.wait(y_free[s])
            ts, z_free = to_channel_major(ring, b, X[:, b, :], Z[:, 0, :], scale, offset, lambda c: y[:, s, c, :],
                                          x_ready[b] if x_ready else None, z_free)
            cols = slice(b * T, (b + 1) * T)
            t_h[b] = y_free[s] = split_sbuf(y[:, s], Hh[:, :, cols], Hl[:, :, cols], ts, [h_free])
        return t_h

    units = [(layer, g, b) for layer in (1, 2) for g in range(G) for b in range(B)]
    ctx_raw_free = [None]
    ctx_loaded = [None]

    def load_ctx(n):
        if n < len(units):
            ctx_loaded[0] = ctx_stream.start(ctx_raw[:], ctxT_in[units[n][2]], ctx_raw_free[0])

    load_ctx(0)
    cx_free, cx_ready = [None, None], [None, None]

    def split_ctx(n):
        if n < len(units):
            s = n % 2
            ts = []
            for c in range(0, C, 2):
                ts += split_sbuf(ctx_raw[:, c:c + 2, :], cxh[:, s, c:c + 2, :], cxl[:, s, c:c + 2, :],
                                 ctx_loaded[0], [cx_free[s]])
            cx_ready[s] = ctx_raw_free[0] = ts
            load_ctx(n + 1)

    split_ctx(0)
    work = Ring([0, 1, 2, 3])
    t_logit_free = [None] * HK
    t_x = [None] * B
    free = {"K": None, "V": None, "P": None, "PT": None, "o": None, "q": None, "bv": None, "qg": None}

    def tail(u):
        t_p, t_vs, wo_block, b = u["t_p"], u["t_v"], u["wo"], u["b"]
        t_pt = []

        def transposes(h):
            i = work.take()
            pe.wait(t_p[h])
            for j, (k0, kn) in enumerate(KTILES):
                m = nc.tensor.transpose(bank[i][0:kn, j * T:(j + 1) * T], Pm[:, h, k0:k0 + kn], ident[0:T, 0:T])
            t = pe.done(m)
            e, f = (act, nc.scalar.copy) if h % 2 else (dve, nc.vector.tensor_copy)
            e.wait(t, free["PT"])
            work.free[i] = t2 = e.done(f(PT[:, h].rearrange("p j t -> p (j t)"), bank[i][:, 0:3 * T]))
            t_pt.append(t2)
            if h == HK - 1:
                free["P"] = t

        def values():
            i = work.take()
            pe.wait(t_pt, t_vs)
            for h in range(HK):
                for j, (k0, kn) in enumerate(KTILES):
                    m = nc.tensor.matmul(bank[i][:, h * T:(h + 1) * T], Vt[0:kn, j, h * P:(h + 1) * P],
                                         PT[0:kn, h, j, :], start=j == 0, stop=j == 2)
            t = pe.done(m)
            free["V"] = free["PT"] = t
            ts = split_psum(bank[i][:, 0:HK * T], oh[:].rearrange("p h t -> p (h t)"),
                            ol[:].rearrange("p h t -> p (h t)"), t, [free["o"]])
            work.free[i] = ts
            u["t_o"] = ts

        def outputs():
            i = work.take()
            wo_block.need()
            pe.wait(u["t_o"])
            for h in range(HK):
                m = mm3(bank[i][0:T, :], (oh[:, h, :], ol[:, h, :]), wo_block.block(h, 0, D), h == 0, h == HK - 1)
            free["o"] = t = pe.done(m)
            dve.wait(t, t_x[b])
            work.free[i] = t_x[b] = dve.done(nc.vector.tensor_tensor(X[:, b, :], bank[i][0:T, :], X[:, b, :], ALU.add))
            if b == B - 1:
                wo_block.give_up()

        return [lambda: transposes(0), lambda: transposes(1), lambda: transposes(2), lambda: transposes(3),
                values, outputs]

    n_unit = 0
    last_tail = []
    for layer in (1, 2):
        for f in last_tail:
            f()
        last_tail = []
        y = qg[:, 0:2, 0:C * T].rearrange("p s (c t) -> p s c t", c=C)
        act.wait(free["qg"])
        t_h = norm_all(work, f"a{layer}_s", f"a{layer}_o", y, t_x, pe.last())
        t_x = add_rows(f"bo{layer}", [t_h[-1], pe.last()])
        free["qg"] = t_h
        for g in range(G):
            wq = Weight(f"q{layer}_{g}")
            wk = Weight(f"k{layer}_{g}")
            wv = Weight(f"v{layer}_{g}")
            wo = Weight(f"o{layer}_{g}")
            t_bv = bv_stream.start(bv[:], bv_in[(layer - 1) * G + g], free["bv"])
            wq.need()
            t_q = []
            for half in range(2):
                for h in range(HK):
                    cols = slice(half * HALF, (half + 1) * HALF)
                    i = work.take()
                    for c in range(C):
                        pe.wait(t_h[half * HB:half * HB + HB])
                        m = mm3(bank[i][:, 0:HALF], wq.block(c, h * P, P), (Hh[:, c, cols], Hl[:, c, cols]),
                                c == 0, c == C - 1)
                    t = pe.done(m)
                    act.wait(t, free["qg"])
                    work.free[i] = t = act.done(nc.scalar.activation(qg[:, h, cols], bank[i][:, 0:HALF], ACT.Identity,
                                                                     bias=V(f"bq{layer}", g * HK + h)))
                    t_q.append(t)
            wq.give_up()
            bk0 = VEC_AT[f"bias_k{layer}"][0] + g * HK
            learned = vec[:, bk0:bk0 + HK]
            t_lk = split_sbuf(learned, Kh[:, :, S], Kl[:, :, S], None, [free["K"]])
            for b in range(B):
                s = n_unit % 2
                cxr = cx_ready[s]
                steps = last_tail
                u = {"b": b, "wo": wo, "t_v": [], "t_p": []}
                t_qs = split_sbuf(qg[:, :, b * T:(b + 1) * T], qh[:], ql[:], t_q, [free["q"]])
                if b == B - 1:
                    free["qg"] = t_qs
                wk.need()
                pe.wait(cxr)
                t_ks = []
                for h in range(HK):
                    i = work.take()
                    for c in range(C):
                        m = mm3(bank[i][:, 0:SP], wk.block(c, h * P, P), (cxh[:, s, c, :], cxl[:, s, c, :]),
                                c == 0, c == C - 1)
                    t = pe.done(m)
                    ts = split_psum(bank[i][:, 0:S], Kh[:, h, 0:S], Kl[:, h, 0:S], t, [free["K"]],
                                    bias=V(f"bk{layer}", g * HK + h))
                    work.free[i] = ts
                    t_ks.append(ts)
                    if h >= 1 and steps:
                        steps.pop(0)()
                        if h >= 3:
                            steps.pop(0)()
                if b == B - 1:
                    wk.give_up()
                wv.need()
                for j, (k0, kn) in enumerate(KTILES):
                    i = work.take()
                    for c in range(C):
                        m = mm3(bank[i][0:kn, :], (cxh[:, s, c, k0:k0 + kn], cxl[:, s, c, k0:k0 + kn]),
                                wv.block(c, 0, D), c == 0, c == C - 1)
                    t = pe.done(m)
                    if steps and j == 0:
                        steps.pop(0)()
                    dve.wait(t, t_bv, free["V"])
                    work.free[i] = t = dve.done(nc.vector.tensor_tensor(Vt[0:kn, j, :], bank[i][0:kn, :],
                                                                        bv[0:kn, j // 2, :], ALU.add))
                    u["t_v"].append(t)
                    if steps and j == 1:
                        steps.pop(0)()
                cx_free[s] = pe.last()
                free["bv"] = dve.last()
                if b == B - 1:
                    wv.give_up()
                pe.wait(t_qs, t_lk)
                t_e, t_m = [], []
                for h in range(HK):
                    pe.wait(t_ks[h], t_logit_free[h])
                    t = pe.done(mm3(bank[4 + h][0:T, 0:SP], (qh[:, h, :], ql[:, h, :]), (Kh[:, h, :], Kl[:, h, :]),
                                    True, True))
                    dve.wait(t)
                    t_m.append(dve.done(nc.vector.tensor_reduce(mxs[:, h:h + 1], bank[4 + h][0:T, 0:SP], AX.X, ALU.max)))
                free["K"] = free["q"] = pe.last()
                n_unit += 1
                split_ctx(n_unit)
                dve.wait(t_m)
                t = dve.done(nc.vector.tensor_scalar(nb[:], mxs[:], -SCALE1, None, ALU.mult))
                act.wait(t, free["P"])
                for h in range(HK):
                    t_logit_free[h] = t = act.done(nc.scalar.activation(
                        Pm[:, h, :], bank[4 + h][0:T, 0:SP], ACT.Exp, bias=nb[:, h:h + 1], scale=SCALE1,
                        accum_out=ssum[:, h:h + 1]))
                    t_e.append(t)
                dve.wait(t_e)
                t = dve.done(nc.vector.reciprocal(rsum[:], ssum[:]))
                pool.wait(t)
                for h in range(HK):
                    u["t_p"].append(pool.done(nc.gpsimd.tensor_scalar(Pm[:, h, :], Pm[:, h, :], rsum[:, h:h + 1], 1.0,
                                                                      ALU.mult, ALU.mult)))
                assert not steps
                last_tail = tail(u)
    for f in last_tail:
        f()

    def mlp(tag, bias, func, t_h, t_x):
        Gf = sb(f"g_{tag}", [P, 2, HALF])
        Gh = sb(f"g_hi_{tag}", [P, C, NT], F32R)
        Gl = sb(f"g_lo_{tag}", [P, C, NT], F32R)
        gf_free = [None, None]
        gh_free = [None, None]
        n = 0
        for g in range(4):
            w1 = Weight(f"m{tag}a_{g}")
            w2 = Weight(f"m{tag}b_{g}")
            w1.need()
            t_g = {}
            for half in range(2):
                cols = slice(half * HALF, (half + 1) * HALF)
                pe.wait(t_h[half * HB:half * HB + HB])
                for o in range(C):
                    i = ring.take()
                    for c in range(C):
                        m = mm3(bank[i][:, 0:HALF], w1.block(c, o * P, P), (Hh[:, c, cols], Hl[:, c, cols]),
                                c == 0, c == C - 1)
                    t = pe.done(m)
                    s = n % 2
                    n += 1
                    act.wait(t, gf_free[s])
                    ring.free[i] = t = act.done(nc.scalar.activation(Gf[:, s], bank[i][:, 0:HALF], func,
                                                                     bias=V(bias, g * C + o)))
                    t_g[half, o] = gf_free[s] = split_sbuf(Gf[:, s], Gh[:, o, cols], Gl[:, o, cols], t, [gh_free[half]])
            w1.give_up()
            w2.need()
            for b in range(B):
                i = ring.take()
                for o in range(C):
                    pe.wait(t_g[b // HB, o])
                    m = mm3(bank[i][0:T, :], (Gh[:, o, b * T:(b + 1) * T], Gl[:, o, b * T:(b + 1) * T]),
                            w2.block(o, 0, D), o == 0, o == C - 1)
                t = pe.done(m)
                gh_free[b // HB] = t
                dve.wait(t, t_x[b])
                ring.free[i] = t_x[b] = dve.done(nc.vector.tensor_tensor(X[:, b, :], bank[i][0:T, :], X[:, b, :], ALU.add))
            w2.give_up()
        return t_x

    new_phase()
    ring = Ring(list(range(8)))
    Z = sb("z3", [T, 1, D])
    row = Z[:, 0, :]
    y = sb("y3", [P, 2, C, T])
    t_h = norm_all(ring, "am_s", "am_o", y, None, None)
    t_x = add_rows("b_fc2", [t_h[-1], pe.last()])
    mlp("1", "b_fc1", ACT.Gelu, t_h, t_x)

    new_phase()
    ring = Ring([0, 1, 2, 3])
    ctx_raw = sb("ctx_raw2", [P, C, SP])
    cxh = sb("ctx_hi2", [P, 1, C, SP], F32R)
    cxl = sb("ctx_lo2", [P, 1, C, SP], F32R)
    q2 = sb("q2", [P, C, NT])
    qh = sb("q2_hi", [P, C, T], F32R)
    ql = sb("q2_lo", [P, C, T], F32R)
    Kh = sb("K2_hi", [P, C, SK2], F32R)
    Kl = sb("K2_lo", [P, C, SK2], F32R)
    Vt = sb("V2", [P, 4, D])
    Pm = sb("probs2", [T, 4, SK2])
    PT = sb("probs2_T", [P, 4, T])
    mask_i = sb("mask_int", [T, SP], I32)
    mask = sb("mask_bias", [T, SK2])
    v_row = sb("v2_bias", [P, D])
    o_row = sb("out_bias", [T, D])
    A = sb("attended", [T, D])
    mxs = sb("max2", [T, H2])
    nb = sb("minus_max2", [T, H2])
    ssum = sb("sum2", [T, H2])
    rsum = sb("inv_sum2", [T, H2])
    rows2 = sem("rows2")
    nc.sync.dma_start(v_row[0:T], rows_in[ROWS.index("v2_b")]).then_inc(rows2, 16)
    nc.sync.dma_start(v_row[T:P], rows_in[ROWS.index("v2_b")][0:P - T]).then_inc(rows2, 16)
    nc.sync.dma_start(o_row[:], rows_in[ROWS.index("out_b")]).then_inc(rows2, 16)
    t_rows2 = (rows2, 48)
    mask_stream = Stream("mask_loaded")
    ctx2_stream = Stream("ctx2_loaded")
    t_ctx = ctx2_stream.start(ctx_raw[:], ctxT_in[0])
    t_mask_in = mask_stream.start(mask_i[:], mask_in[0])
    t_mz = dve.done(nc.vector.memset(mask[:, SP:SK2], 0.0))

    t_h = []
    for b in range(B):
        i, t = turn(ring, X[:, b, :], None)
        cols = slice(b * T, (b + 1) * T)
        ts = split_psum(bank[i][:, 0:C * T].rearrange("p (c t) -> p c t", c=C), Hh[:, :, cols], Hl[:, :, cols], t)
        ring.free[i] = ts
        t_h.append(ts)
    w = Weight("p_q")
    w.need()
    t_q = []
    for half in range(2):
        cols = slice(half * HALF, (half + 1) * HALF)
        pe.wait(t_h[half * HB:half * HB + HB])
        for o in range(C):
            i = ring.take()
            for c in range(C):
                m = mm3(bank[i][:, 0:HALF], w.block(c, o * P, P), (Hh[:, c, cols], Hl[:, c, cols]), c == 0, c == C - 1)
            t = pe.done(m)
            act.wait(t)
            ring.free[i] = t = act.done(nc.scalar.activation(q2[:, o, cols], bank[i][:, 0:HALF], ACT.Identity,
                                                             bias=V("q2_b", o)))
            t_q.append(t)
    w.give_up()
    wk, wv, wo = Weight("p_k"), Weight("p_v"), Weight("p_o")
    cx_free = qf = kf = vf = pf = ptf = mf = af = None
    lf = [None] * 4
    t_h2 = []
    for b in range(B):
        cols = slice(b * T, (b + 1) * T)
        t_cx = []
        for c in range(0, C, 2):
            t_cx += split_sbuf(ctx_raw[:, c:c + 2], cxh[:, 0, c:c + 2], cxl[:, 0, c:c + 2], t_ctx, [cx_free])
        if b + 1 < B:
            t_ctx = ctx2_stream.start(ctx_raw[:], ctxT_in[b + 1], t_cx)
        t_qs = split_sbuf(q2[:, :, cols], qh[:], ql[:], t_q, [qf])
        dve.wait(t_mask_in, mf)
        t_mask = dve.done(nc.vector.tensor_scalar(mask[:, 0:SP], mask_i[:], 0.0, GAP, ALU.is_equal, ALU.mult))
        if b + 1 < B:
            t_mask_in = mask_stream.start(mask_i[:], mask_in[b + 1], t_mask)
        wk.need()
        pe.wait(t_cx, t_h[b])
        t_ks = []
        for o in range(C):
            i = ring.take()
            for c in range(C):
                mm3(bank[i][:, 0:SP], wk.block(c, o * P, P), (cxh[:, 0, c, :], cxl[:, 0, c, :]), c == 0, c == C - 1)
            for c in range(C):
                m = nc.tensor.matmul(bank[i][:, SP:SK2], Wh[:, wk.slot, c, o * P:(o + 1) * P], Hh[:, c, cols], start=False, stop=False, skip_group_check=True)
                m = nc.tensor.matmul(bank[i][:, SP:SK2], Wh[:, wk.slot, c, o * P:(o + 1) * P], Hl[:, c, cols], start=False, stop=False, skip_group_check=True)
                m = nc.tensor.matmul(bank[i][:, SP:SK2], Wl[:, wk.slot, c, o * P:(o + 1) * P], Hh[:, c, cols], start=False, stop=c == C - 1, skip_group_check=True)
            t = pe.done(m)
            ts = split_psum(bank[i][:, 0:SK2], Kh[:, o, :], Kl[:, o, :], t, [kf], bias=V("k2_b", o))
            ring.free[i] = ts
            t_ks.append(ts)
        wv.need()
        t_vs = []
        for j, (k0, kn) in enumerate(KTILES2):
            i = ring.take()
            for c in range(C):
                left = ((cxh[:, 0, c, k0:k0 + kn], cxl[:, 0, c, k0:k0 + kn]) if j < 3 else (Hh[:, c, cols], Hl[:, c, cols]))
                m = mm3(bank[i][0:kn, :], left, wv.block(c, 0, D), c == 0, c == C - 1)
            t = pe.done(m)
            dve.wait(t, t_rows2, vf)
            ring.free[i] = t = dve.done(nc.vector.tensor_tensor(Vt[0:kn, j, :], bank[i][0:kn, :], v_row[0:kn, :], ALU.add))
            t_vs.append(t)
        cx_free = pe.last()
        o_bank = ring.take()
        pe.wait(t_qs)
        pv_last = None
        for o in range(C):
            pe.wait(t_ks[o])
            t_m = []
            for k in range(4):
                pe.wait(lf[k])
                rows = slice(32 * k, 32 * k + 32)
                t = pe.done(mm3(bank[4 + k][0:T, 0:SK2], (qh[rows, o, :], ql[rows, o, :]), (Kh[rows, o, :], Kl[rows, o, :]),
                                True, True))
                dve.wait(t, t_mask, t_mz, pf)
                t = dve.done(nc.vector.tensor_tensor(Pm[:, k, :], bank[4 + k][0:T, 0:SK2], mask[:], ALU.add))
                lf[k] = t
                dve.wait(t)
                t_m.append(dve.done(nc.vector.tensor_reduce(mxs[:, 4 * o + k:4 * o + k + 1], Pm[:, k, :], AX.X, ALU.max)))
            dve.wait(t_m)
            t = dve.done(nc.vector.tensor_scalar(nb[:, 4 * o:4 * o + 4], mxs[:, 4 * o:4 * o + 4], -SCALE2, None, ALU.mult))
            act.wait(t, af)
            for k in range(4):
                h = 4 * o + k
                t_e = act.done(nc.scalar.activation(Pm[:, k, :], Pm[:, k, :], ACT.Exp, bias=nb[:, h:h + 1],
                                                    scale=SCALE2, accum_out=ssum[:, h:h + 1]))
                i = ring.take()
                if i == o_bank:
                    i = ring.take()
                pe.wait(t_e)
                for j, (k0, kn) in enumerate(KTILES2):
                    m = nc.tensor.transpose(bank[i][0:kn, j * T:(j + 1) * T], Pm[:, k, k0:k0 + kn], ident[0:T, 0:T])
                pf = t = pe.done(m)
                dve.wait(t, ptf)
                ring.free[i] = t = dve.done(nc.vector.tensor_copy(PT[:].rearrange("p j t -> p (j t)"), bank[i][:, 0:4 * T]))
                pe.wait(t, t_vs)
                for j, (k0, kn) in enumerate(KTILES2):
                    m = nc.tensor.matmul(bank[o_bank][0:T, h * D2:(h + 1) * D2], PT[0:kn, j, :],
                                         Vt[0:kn, j, h * D2:(h + 1) * D2], start=j == 0, stop=j == 3)
                ptf = pv_last = pe.done(m)
            t_exp = act.last()
        qf = kf = vf = pv_last
        mf = dve.last()
        dve.wait(t_exp, pv_last)
        t = dve.done(nc.vector.reciprocal(rsum[:], ssum[:]))
        dve.wait(t)
        af = ring.free[o_bank] = t = dve.done(nc.vector.tensor_tensor(
            A[:].rearrange("q (h d) -> q h d", h=H2), bank[o_bank][0:T, :].rearrange("q (h d) -> q h d", h=H2),
            rsum[:].unsqueeze(2).broadcast_to([T, H2, D2]), ALU.mult))
        i, t = turn(ring, A[:], t)
        ts = split_psum(bank[i][:, 0:C * T].rearrange("p (c t) -> p c t", c=C), qh[:], ql[:], t, [qf])
        ring.free[i] = ts
        wo.need()
        i = ring.take()
        pe.wait(ts)
        for c in range(C):
            m = mm3(bank[i][0:T, :], (qh[:, c, :], ql[:, c, :]), wo.block(c, 0, D), c == 0, c == C - 1)
        qf = t = pe.done(m)
        dve.wait(t, t_rows2)
        ring.free[i] = t = dve.done(nc.vector.tensor_tensor(A[:], bank[i][0:T, :], o_row[:], ALU.add))
        dve.wait(t)
        t = dve.done(nc.vector.tensor_tensor(A[:], A[:], X[:, b, :], ALU.add))
        dve.wait(t)
        t = dve.done(nc.vector.bn_stats(stats[:, b % 2, :], A[:]))
        dve.wait(t)
        t = dve.done(nc.vector.bn_aggr(mv[:, b % 2, :], stats[:, b % 2, :]))
        dve.wait(t)
        t = dve.done(nc.vector.scalar_tensor_tensor(out=mv[:, b % 2, 1:2], in0=mv[:, b % 2, 0:1], scalar=mv[:, b % 2, 0:1],
                                                    in1=mv[:, b % 2, 1:2], op0=ALU.mult, op1=ALU.add))
        t = inverse_root(b, mv[:, b % 2, 1:2], 1e-6, t)
        dve.wait(t)
        t = dve.done(nc.vector.tensor_scalar(A[:], A[:], rstd[:, b % 2, 0:1], None, ALU.mult))
        i, t = turn(ring, A[:], t)
        af = t
        ts = []
        act.wait(t)
        for c in range(C):
            act.wait(None)
            ts.append(act.done(nc.scalar.activation(q2[:, c, cols], bank[i][:, c * T:(c + 1) * T], ACT.Copy,
                                                    scale=V("post_w", c))))
        ring.free[i] = ts
        t_h2.append(split_sbuf(q2[:, :, cols], Hh[:, :, cols], Hl[:, :, cols], ts, [pv_last]))
    wk.give_up()
    wv.give_up()
    wo.give_up()

    new_phase()
    ring = Ring(list(range(8)))
    Z = sb("z4", [T, 1, D])
    row = Z[:, 0, :]
    t_x = add_rows("mlp_b2", None)
    mlp("2", "mlp_b1", ACT.Gelu_apprx_tanh, t_h2, t_x)

    new_phase()
    ring = Ring([0, 1, 2, 3, 4, 5, 6, 7])
    ctx_raw = sb("ctx_raw3", [P, C, SP])
    cxh = sb("ctx_hi3", [P, 1, C, SP], F32R)
    cxl = sb("ctx_lo3", [P, 1, C, SP], F32R)
    ctx_n = sb("ctx_rows", [P, 3, D])
    Qh = sb("Q_hi", [P, C, NT], F32R)
    Ql = sb("Q_lo", [P, C, NT], F32R)
    Rh = sb("QK_hi", [P, C, NT], F32R)
    Rl = sb("QK_lo", [P, C, NT], F32R)
    Pm = sb("probs3", [T, 2, SP])
    PT = sb("probs3_T", [P, 3, T])
    A = sb("attended3", [T, D])
    mxs = sb("max3", [T, B])
    nb = sb("minus_max3", [T, B])
    ssum = sb("sum3", [T, B])
    rsum = sb("inv_sum3", [T, B])
    O = sb("out_tile", [T, 2, D])
    ctx3_stream = Stream("ctx3_loaded")
    rows3 = sem("rows3")
    n_rows3 = 0
    t_ctx = ctx3_stream.start(ctx_raw[:], ctxT_in[0])

    def load_rows(b, after):
        nonlocal n_rows3
        sp.wait((rows3, n_rows3) if n_rows3 else None, after)
        sp.eng.dma_start(ctx_n[:, 0:2, :], ctx_in[b, 0:2 * P].rearrange("(j p) d -> p j d", p=P)).then_inc(rows3, 16)
        sp.eng.dma_start(ctx_n[0:S - 2 * P, 2, :], ctx_in[b, 2 * P:S]).then_inc(rows3, 16)
        n_rows3 += 32
        return (rows3, n_rows3)

    t_rows = load_rows(0, None)
    t_h = []
    for b in range(B):
        i, t = turn(ring, X[:, b, :], None)
        cols = slice(b * T, (b + 1) * T)
        ts = split_psum(bank[i][:, 0:C * T].rearrange("p (c t) -> p c t", c=C), Hh[:, :, cols], Hl[:, :, cols], t)
        ring.free[i] = ts
        t_h.append(ts)

    def project3(name, src, dst, ready, free=()):
        w = Weight(name)
        w.need()
        out_t = []
        for half in range(2):
            cols = slice(half * HALF, (half + 1) * HALF)
            pe.wait(ready[half])
            ts_half = []
            for o in range(C):
                i = ring.take()
                for c in range(C):
                    m = mm3(bank[i][:, 0:HALF], w.block(c, o * P, P), (src[0][:, c, cols], src[1][:, c, cols]),
                            c == 0, c == C - 1)
                t = pe.done(m)
                ts = split_psum(bank[i][:, 0:HALF], dst[0][:, o, cols], dst[1][:, o, cols], t, free)
                ring.free[i] = ts
                ts_half.append(ts)
            out_t.append(ts_half)
        w.give_up()
        return out_t

    Hs, Qs, Rs = (Hh, Hl), (Qh, Ql), (Rh, Rl)
    t_q = project3("e_q", Hs, Qs, [t_h[0:HB], t_h[HB:B]])
    t_qk = project3("e_k", Qs, Rs, t_q)
    h_free = pe.last()
    cx_free = pt_free = cn_free = a_free = None
    p_free = [None, None]
    t_pc = []
    for b in range(B):
        cols = slice(b * T, (b + 1) * T)
        t_cx = []
        for c in range(0, C, 2):
            t_cx += split_sbuf(ctx_raw[:, c:c + 2], cxh[:, 0, c:c + 2], cxl[:, 0, c:c + 2], t_ctx, [cx_free])
        if b + 1 < B:
            t_ctx = ctx3_stream.start(ctx_raw[:], ctxT_in[b + 1], t_cx)
        i = ring.take()
        pe.wait(t_cx, t_qk[b // HB])
        for c in range(C):
            m = mm3(bank[i][0:T, 0:SP], (Rh[:, c, cols], Rl[:, c, cols]), (cxh[:, 0, c, :], cxl[:, 0, c, :]), c == 0, c == C - 1)
        cx_free = t = pe.done(m)
        s = b % 2
        dve.wait(t)
        t = dve.done(nc.vector.tensor_reduce(mxs[:, b:b + 1], bank[i][0:T, 0:S], AX.X, ALU.max))
        dve.wait(t)
        t = dve.done(nc.vector.tensor_scalar(nb[:, b:b + 1], mxs[:, b:b + 1], -SCALE3, None, ALU.mult))
        act.wait(t, p_free[s])
        ring.free[i] = t = act.done(nc.scalar.activation(Pm[:, s, 0:S], bank[i][0:T, 0:S], ACT.Exp, bias=nb[:, b:b + 1],
                                                         scale=SCALE3, accum_out=ssum[:, b:b + 1]))
        dve.wait(t)
        t_rs = dve.done(nc.vector.reciprocal(rsum[:, b:b + 1], ssum[:, b:b + 1]))
        i = ring.take()
        pe.wait(t)
        for j, (k0, kn) in enumerate(KTILES):
            kn = min(kn, S - k0)
            m = nc.tensor.transpose(bank[i][0:kn, j * T:(j + 1) * T], Pm[:, s, k0:k0 + kn], ident[0:T, 0:T])
        p_free[s] = t = pe.done(m)
        dve.wait(t, pt_free)
        ring.free[i] = t = dve.done(nc.vector.tensor_copy(PT[:].rearrange("p j t -> p (j t)"), bank[i][:, 0:3 * T]))
        i = ring.take()
        pe.wait(t, t_rows)
        for j, (k0, kn) in enumerate(KTILES):
            kn = min(kn, S - k0)
            m = nc.tensor.matmul(bank[i][0:T, :], PT[0:kn, j, :], ctx_n[0:kn, j, :], start=j == 0, stop=j == 2)
        pt_free = t = pe.done(m)
        if b + 1 < B:
            t_rows = load_rows(b + 1, t)
        dve.wait(t, t_rs, a_free)
        ring.free[i] = t = dve.done(nc.vector.tensor_scalar(A[:], bank[i][0:T, :], rsum[:, b:b + 1], None, ALU.mult))
        i, t = turn(ring, A[:], t)
        a_free = t
        ts = split_psum(bank[i][:, 0:C * T].rearrange("p (c t) -> p c t", c=C), Hh[:, :, cols], Hl[:, :, cols], t, [h_free])
        ring.free[i] = ts
        t_pc.append(ts)
    q_free = pe.last()
    t_c = project3("e_v", Hs, Qs, [t_pc[0:HB], t_pc[HB:B]], [q_free])
    w = Weight("e_o")
    w.need()
    out_sems = [sem("stored0"), sem("stored1")]
    stored = [0, 0]
    for b in range(B):
        i = ring.take()
        pe.wait(t_c[b // HB])
        for c in range(C):
            m = mm3(bank[i][0:T, :], (Qh[:, c, b * T:(b + 1) * T], Ql[:, c, b * T:(b + 1) * T]), w.block(c, 0, D),
                    c == 0, c == C - 1)
        t = pe.done(m)
        s = b % 2
        dve.wait(t, (out_sems[s], stored[s]) if stored[s] else None)
        ring.free[i] = t = dve.done(nc.vector.scalar_tensor_tensor(
            out=O[:, s, :], in0=bank[i][0:T, :], scalar=V("alpha", 0, T), in1=X[:, b, :], op0=ALU.mult, op1=ALU.add))
        sp.wait(t)
        sp.eng.dma_start(out[b], O[:, s, :]).then_inc(out_sems[s], 16)
        stored[s] += 16
    w.give_up()
    for s in range(2):
        sp.wait((out_sems[s], stored[s]))
    while len(phase) > 1:
        phase.pop().close()
    stack.close()


def _chunked(w):
    return np.ascontiguousarray(w.reshape(C, P, w.shape[1]).transpose(1, 0, 2))


def kernel(**inputs):
    import concourse.bacc as _bacc
    from concourse.bass_utils import run_bass_kernel_spmd as _run

    i = {k: np.asarray(v) for k, v in inputs.items()}
    l0 = {k[9:]: v for k, v in i.items() if k.startswith("L0_")}
    l1 = {k[9:]: v for k, v in i.items() if k.startswith("L1_")}
    l2 = {k[9:]: v for k, v in i.items() if k.startswith("L2_")}
    l3 = {k[9:]: v for k, v in i.items() if k.startswith("L3_")}
    ctx = i["ctx_2048"]

    ctxT = np.zeros((B, D, SP), ctx.dtype)
    ctxT[:, :, :S] = ctx.transpose(0, 2, 1)
    ctxT = np.ascontiguousarray(ctxT.reshape(B, C, P, SP).transpose(0, 2, 1, 3))
    prev = np.ascontiguousarray(ctx[:, 0:2].reshape(B, 2, C, P).transpose(3, 1, 2, 0))
    s0 = ctx[:, 2:2 + S0].reshape(B, C, 8, S0, S0).transpose(2, 3, 1, 4, 0).reshape(P, C, S0, B)
    mask = np.zeros((B, SP), i["mask_BxS2_ik0"].dtype)
    mask[:, :S] = i["mask_BxS2_ik0"]
    mask = np.repeat(mask[:, None, :], T, 1)

    blocks = {"k": l0["Wk"].T, "r": l0["Wr"].T, "v": l0["Wv"].T, "g": l0["Wg"].T, "o": l0["Wo"].T,
              "fr": l0["ffn_Wr"].T, "fk": l0["ffn_Wk"].T, "fv": l0["ffn_Wv"].T,
              "p_q": l2["q_w"], "p_k": l2["kv_w"][:, 0::2], "p_v": l2["kv_w"][:, 1::2], "p_o": l2["out_w"],
              "e_q": l3["w_q"].T, "e_k": l3["w_k"], "e_v": l3["w_v"].T, "e_o": l3["w_o"].T}
    for g in range(4):
        at = slice(g * D, (g + 1) * D)
        for layer in (1, 2):
            for w in "qkv":
                blocks[f"{w}{layer}_{g}"] = l1[f"w{w}{layer}"][:, at]
            blocks[f"o{layer}_{g}"] = l1[f"wo{layer}"][at]
        blocks[f"m1a_{g}"], blocks[f"m1b_{g}"] = l1["w_fc1"][:, at], l1["w_fc2"][at]
        blocks[f"m2a_{g}"], blocks[f"m2b_{g}"] = l2["mlp_w1"][:, at], l2["mlp_w2"][at]
    weights = np.stack([_chunked(blocks[n]) for n in UNIQUE])

    vectors = {"ln1_w": l0["ln1_w"], "ln1_b": l0["ln1_b"], "maa_x": l0["maa_x"], "time_decay": l0["time_decay"],
               "u": l0["faaaa"].reshape(-1), "gn_w": l0["gn_w"], "gn_b": l0["gn_b"], "ln2_w": l0["ln2_w"],
               "ln2_b": l0["ln2_b"], "ffn_maa_k": l0["ffn_maa_k"], "ffn_maa_r": l0["ffn_maa_r"],
               "a1_s": l1["ln1_scale"], "a1_o": l1["ln1_offset"], "a2_s": l1["ln2_scale"], "a2_o": l1["ln2_offset"],
               "am_s": l1["ln_mlp_scale"], "am_o": l1["ln_mlp_offset"], "post_w": l2["postnorm_w"],
               "q2_b": l2["q_b"], "k2_b": l2["kv_b"][0::2], "alpha": np.repeat(l3["alpha"].reshape(1), P),
               "bq1": l1["bq1"], "bk1": l1["bk1"], "bq2": l1["bq2"], "bk2": l1["bk2"],
               "bias_k1": l1["bias_k1"].reshape(-1), "bias_k2": l1["bias_k2"].reshape(-1),
               "b_fc1": l1["b_fc1"], "mlp_b1": l2["mlp_b1"]}
    for j in range(5):
        vectors[f"maa_{j}"] = l0["maa_stack"][j]
    vec = np.ascontiguousarray(np.concatenate([vectors[n].reshape(w, P) for n, w in VECTORS]).T)
    rows = {"bo1": l1["bo1"], "bo2": l1["bo2"], "b_fc2": l1["b_fc2"], "v2_b": l2["kv_b"][1::2],
            "out_b": l2["out_b"], "mlp_b2": l2["mlp_b2"]}
    rows = np.stack([np.repeat(rows[n][None], T, 0) for n in ROWS])
    bv = []
    for layer in (1, 2):
        for g in range(G):
            both = np.repeat(l1[f"bv{layer}"][None, None, g * D:(g + 1) * D], P, 0).repeat(2, 1)
            both[S - 2 * P, 1] = l1[f"bias_v{layer}"].reshape(-1)[g * D:(g + 1) * D]
            bv.append(both)
    bv = np.stack(bv)

    lane = np.arange(P)
    ident = np.eye(P, dtype=np.float32)
    heads = (lane[:, None] // S0 == lane[None, :] // S0).astype(np.float32)
    place = np.zeros((P, P + S0 - 1), np.float32)
    place[lane, S0 - 1 + S0 * (lane // S0)] = 1.0
    pick = (lane[:, None] % S0 == np.arange(S0)[None, :]).astype(np.float32)

    arrays = {"x": i["x"], "ctx": ctx, "ctxT": ctxT, "prev": prev, "s0": s0, "mask": mask, "weights": weights,
              "vec": vec, "rows": rows, "bv": bv, "maa_w1": _chunked(l0["maa_w1"]),
              "maa_w2": l0["maa_w2"].reshape(5 * 32, D), "dec_w1": _chunked(l0["decay_w1"]), "dec_w2": l0["decay_w2"],
              "ident": ident, "heads": heads, "place": place, "pick": pick}
    nc = _bacc.Bacc("TRN2", target_bir_lowering=False, num_devices=1)
    feeds, args = {}, []
    for name, a in arrays.items():
        a = np.ascontiguousarray(a)
        feeds[f"in_{name}"] = a
        args.append(nc.dram_tensor(f"in_{name}", a.shape, mybir.dt.from_np(a.dtype), kind="ExternalInput").ap())
    args.append(nc.dram_tensor("out_y", (B, T, D), F32, kind="ExternalOutput").ap())
    build(nc, *args)
    r = _run(nc, [feeds], core_ids=[0])
    return r.results[0]["out_y"]
```

```python
from contextlib import ExitStack

import numpy as np

import concourse.bass as bass
from concourse import mybir

F32 = mybir.dt.float32
F32R = mybir.dt.float32r
I32 = mybir.dt.int32
ACT = mybir.ActivationFunctionType
ALU = mybir.AluOpType
AX = mybir.AxisListType

P = 128
B, T, D = 8, 112, 512
S = 375
SP = S + 1
C = D // P
NT = B * T
HALF = NT // 2
HB = B // 2
H0, S0 = 32, 16
HK, G = 4, 4
KTILES = [(0, 128), (128, 128), (256, SP - 256)]
KTILES2 = KTILES + [(SP, T)]
SK2 = SP + T
H2, D2 = 16, 32
GAP = -1.0e30
SCALE1 = 128.0 ** -0.5
SCALE2 = 1.0 / D2
SCALE3 = float(D) ** -0.5

VECTORS = [
    ("ln1_w", 4), ("ln1_b", 4), ("maa_x", 4), ("maa_0", 4), ("maa_1", 4), ("maa_2", 4), ("maa_3", 4),
    ("maa_4", 4), ("time_decay", 4), ("u", 4), ("gn_w", 4), ("gn_b", 4), ("ln2_w", 4), ("ln2_b", 4),
    ("ffn_maa_k", 4), ("ffn_maa_r", 4),
    ("a1_s", 4), ("a1_o", 4), ("a2_s", 4), ("a2_o", 4), ("am_s", 4), ("am_o", 4), ("post_w", 4),
    ("q2_b", 4), ("k2_b", 4), ("v2_b", 4), ("alpha", 1),
    ("bq1", 16), ("bk1", 16), ("bq2", 16), ("bk2", 16), ("bias_k1", 16), ("bias_k2", 16),
    ("b_fc1", 16), ("mlp_b1", 16),
]
VEC_AT, _n = {}, 0
for _name, _w in VECTORS:
    VEC_AT[_name] = (_n, _w)
    _n += _w
NVEC = _n

ROWS = ["bo1", "bo2", "b_fc2", "out_b", "mlp_b2"]

UNIQUE = (["k", "r", "v", "g", "o", "fr", "fk", "fv"]
          + [f"{w}{layer}_{g}" for layer in (1, 2) for g in range(G) for w in "qkvo"]
          + [f"m1{w}_{g}" for g in range(4) for w in "ab"]
          + ["p_q", "p_k", "p_v", "p_o"]
          + [f"m2{w}_{g}" for g in range(4) for w in "ab"]
          + ["e_q", "e_k", "e_v", "e_o"])
ORDER = ["k", "r", "v", "g", "o"] + UNIQUE
NSLOT = 4


def build(nc, x_in, ctx_in, ctxT_in, prev_in, s0_in, mask_in, w_in, vec_in, rows_in, bv_in,
          maa_w1_in, maa_w2_in, dec_w1_in, dec_w2_in, ident_in, heads_in, place_in, pick_in_dram, out):
    stack = ExitStack()
    phase = [stack.enter_context(ExitStack())]

    def sem(name):
        return stack.enter_context(nc.semaphore(name))

    class Engine:

        def __init__(self, eng, name):
            self.eng, self.sem, self.count, self.seen = eng, sem(name), 0, {}

        def wait(self, *tokens):
            for token in tokens:
                if token is None:
                    continue
                if isinstance(token, list):
                    self.wait(*token)
                    continue
                s, n = token
                if self.seen.get(s.name, 0) < n:
                    self.eng.wait_ge(s, n)
                    self.seen[s.name] = n

        def done(self, instruction):
            self.count += 1
            instruction.then_inc(self.sem, 1)
            return (self.sem, self.count)

        def last(self):
            return (self.sem, self.count) if self.count else None

    pe = Engine(nc.tensor, "pe_done")
    act = Engine(nc.scalar, "act_done")
    dve = Engine(nc.vector, "dve_done")
    pool = Engine(nc.gpsimd, "pool_done")
    sp = Engine(nc.sync, "sp_unused")

    class Stream:

        def __init__(self, name):
            self.sem, self.count = sem(name), 0

        def start(self, dst, src, *after):
            sp.wait((self.sem, self.count) if self.count else None, *after)
            sp.eng.dma_start(dst, src).then_inc(self.sem, 16)
            self.count += 16
            return (self.sem, self.count)

    def sb(name, shape, dt=F32):
        return phase[-1].enter_context(nc.sbuf_tensor(name, shape, dt))

    def new_phase(keep=()):
        tokens = [e.last() for e in (pe, act, dve, pool)] + list(keep)
        for e in (pe, act, dve, pool, sp):
            e.wait(*tokens)
        if len(phase) > 1:
            phase.pop().close()
        phase.append(ExitStack())
        stack.enter_context(phase[-1])

    Wh = sb("W_hi", [P, NSLOT, C, D], F32R)
    Wl = sb("W_lo", [P, NSLOT, C, D], F32R)
    Wraw = sb("W_raw", [P, C, D])
    X = sb("residual", [T, B, D])
    Hh = sb("act_hi", [P, C, NT], F32R)
    Hl = sb("act_lo", [P, C, NT], F32R)
    vec = sb("vectors", [P, NVEC])
    ident = sb("ident", [P, P])
    stats = sb("stats", [T, HB, 6])
    mv = sb("mean_var", [T, HB, 2])
    rstd = sb("rstd", [T, HB, 2])
    minus_half = sb("minus_half", [T, HB])
    Z = sb("normalised", [T, D])
    row = sb("bias_row", [T, D])
    bank = [stack.enter_context(nc.psum_tensor(f"bank{i}", [P, 512], F32)) for i in range(8)]

    def V(name, i, n=P):
        return vec[0:n, VEC_AT[name][0] + i:VEC_AT[name][0] + i + 1]

    class Ring:

        def __init__(self, banks):
            self.banks, self.free, self.at = banks, {b: None for b in banks}, 0

        def take(self):
            i = self.banks[self.at % len(self.banks)]
            self.at += 1
            pe.wait(self.free[i])
            return i

    const = sem("const")
    n_const = 0
    for dst, src in ((X[:], x_in.rearrange("b t d -> t b d")), (vec[:], vec_in), (ident[:], ident_in)):
        nc.sync.dma_start(dst, src).then_inc(const, 16)
        n_const += 16
    constants = (const, n_const)
    zeroed = [dve.done(nc.vector.memset(bank[i][:], 0.0)) for i in range(8)]
    t_mh = dve.done(nc.vector.memset(minus_half[:], -0.5))
    for e in (pe, act, dve, pool):
        e.wait(constants, t_mh)
    pe.wait(zeroed)
    act.wait(zeroed)

    w_stream = Stream("w_loaded")
    w_state = {"staged": 0, "split": 0, "raw_free": None, "loaded": None}
    w_ready = {}
    w_free = {}

    def stage_next_weight():
        n = w_state["staged"]
        if n < len(ORDER):
            w_state["loaded"] = w_stream.start(Wraw[:], w_in[UNIQUE.index(ORDER[n])], w_state["raw_free"])
            w_state["staged"] += 1

    def feed_weights():
        n = w_state["split"]
        if n == len(ORDER) or n >= NSLOT and (n - NSLOT) not in w_free:
            return
        slot, free = n % NSLOT, w_free.get(n - NSLOT)
        act.wait(w_state["loaded"], free)
        his, los = [], []
        for c in range(0, C, 2):
            his.append(act.done(nc.scalar.copy(Wh[:, slot, c:c + 2, :], Wraw[:, c:c + 2, :])))
        pool.wait(w_state["loaded"], free)
        for i, c in enumerate(range(0, C, 2)):
            pool.wait(his[i])
            los.append(pool.done(nc.gpsimd.tensor_tensor(
                Wl[:, slot, c:c + 2, :], Wraw[:, c:c + 2, :], Wh[:, slot, c:c + 2, :].bitcast(F32),
                ALU.subtract)))
        w_ready[n] = his + los
        w_state["raw_free"] = his + los
        w_state["split"] += 1
        stage_next_weight()

    w_state["use"] = 0

    class Weight:

        def __init__(self, name):
            self.n = w_state["use"]
            assert ORDER[self.n] == name, (ORDER[self.n], name)
            w_state["use"] += 1
            self.slot = self.n % NSLOT

        def need(self):
            while w_state["split"] <= self.n:
                feed_weights()
            pe.wait(w_ready[self.n])

        def block(self, c, a, n):
            return Wh[:, self.slot, c, a:a + n], Wl[:, self.slot, c, a:a + n]

        def give_up(self):
            w_free[self.n] = [pe.last()]

    def mm3(dst, left, right, first, last):
        nc.tensor.matmul(dst, left[0], right[0], start=first, stop=False)
        nc.tensor.matmul(dst, left[0], right[1], start=False, stop=False)
        return nc.tensor.matmul(dst, left[1], right[0], start=False, stop=last)

    def split_psum(src, hi, lo, ready, free=(), bias=None):
        act.wait(ready, *free)
        if bias is None:
            t_hi = act.done(nc.scalar.copy(hi, src))
        else:
            t_hi = act.done(nc.scalar.activation(hi, src, ACT.Identity, bias=bias))
        dve.wait(ready, t_hi, *free)
        if bias is None:
            t_lo = dve.done(nc.vector.tensor_tensor(lo, src, hi.bitcast(F32), ALU.subtract))
        else:
            t_lo = dve.done(nc.vector.scalar_tensor_tensor(
                out=lo, in0=src, scalar=bias, in1=hi.bitcast(F32), op0=ALU.add, op1=ALU.subtract))
        return [t_hi, t_lo]

    def split_sbuf(src, hi, lo, ready, free=()):
        act.wait(ready, *free)
        t_hi = act.done(nc.scalar.copy(hi, src))
        pool.wait(ready, t_hi, *free)
        t_lo = pool.done(nc.gpsimd.tensor_tensor(lo, src, hi.bitcast(F32), ALU.subtract))
        return [t_hi, t_lo]

    def inverse_root(n, src, eps, ready):
        dve.wait(ready)
        t = dve.done(nc.vector.tensor_scalar(rstd[:, 0:n, 1], src, eps, None, ALU.add))
        pool.wait(t)
        return pool.done(nc.gpsimd.tensor_tensor(rstd[:, 0:n, 0], rstd[:, 0:n, 1], minus_half[:, 0:n], ALU.pow))

    def moments(srcs, ready):
        for k, src in enumerate(srcs):
            dve.wait(ready[k])
            t = dve.done(nc.vector.bn_stats(stats[:, k, :], src))
        for k, src in enumerate(srcs):
            dve.wait(t)
            t = dve.done(nc.vector.bn_aggr(mv[:, k, :], stats[:, k, :]))
        return inverse_root(len(srcs), mv[:, 0:len(srcs), 1], 1e-5, t)

    def turn(ring, z, ready):
        i = ring.take()
        pe.wait(ready)
        for c in range(C):
            m = nc.tensor.transpose(bank[i][:, c * T:(c + 1) * T], z[:, c * P:(c + 1) * P], ident[0:T, 0:T])
        return i, pe.done(m)

    z_read = [None]

    def normalised_turn(ring, src, k, t_root):
        dve.wait(t_root, z_read[0])
        t = dve.done(nc.vector.tensor_scalar(Z[:], src, mv[:, k, 0:1], rstd[:, k, 0:1], ALU.subtract, ALU.mult))
        i, z_read[0] = turn(ring, Z[:], t)
        return i, z_read[0], t

    def norm_split(ring, bs, scale, offset, ready, h_free, t_row):
        t_root = moments([X[:, b, :] for b in bs], ready)
        out_t = {}
        for k, b in enumerate(bs):
            i, t_turn, t_z = normalised_turn(ring, X[:, b, :], k, t_root)
            act.wait(t_turn)
            ts = []
            for c in range(C):
                at = bank[i][:, c * T:(c + 1) * T]
                ts.append(act.done(nc.scalar.activation(at, at, ACT.Identity, scale=V(scale, c), bias=V(offset, c))))
            cols = slice(b * T, (b + 1) * T)
            ts = split_psum(bank[i][:, 0:C * T].rearrange("p (c t) -> p c t", c=C), Hh[:, :, cols], Hl[:, :, cols],
                            ts, [h_free])
            ring.free[i] = ts
            dve.wait(t_row, t_z)
            out_t[b] = ts, dve.done(nc.vector.tensor_tensor(X[:, b, :], X[:, b, :], row[:], ALU.add))
        return out_t

    row_stream = Stream("row_loaded")

    def load_row(name, *after):
        return row_stream.start(row[:], rows_in[ROWS.index(name)], *after)

    phase.append(ExitStack())
    stack.enter_context(phase[-1])
    ring = Ring([0, 1, 2, 3, 4, 5])
    y_banks = [6, 7]
    xn = sb("xn", [P, C, HB, T + 1])
    sx = sb("sx", [P, C, HB, T])
    tmp = sb("tmp", [P, 2, HB, T + 1])
    mx = sb("mx", [P, 2, HB, T])
    x5 = sb("x5", [P, 2, HB, T])
    th = sb("th", [P, HALF])
    th4 = sb("th4", [32, HALF])
    thd = sb("thd", [64, HALF])
    kT = sb("kT", [P, C, HB, T])
    rT = sb("rT", [P, C, HB, T])
    wT = sb("wT", [P, C, HB, T + 1])
    att = sb("att", [P, C, HB, T])
    ab2 = sb("kv_then_state", [P, 2, HB, T + 1])
    yb2 = sb("y", [P, 2, HB, T])
    prev = sb("prev", [P, 2, C, B])
    s0 = sb("s0", [P, C, S0, B])
    maa_w1 = sb("maa_w1", [P, C, 160])
    maa_w2 = sb("maa_w2", [P, D])
    maa_w24 = sb("maa_w24", [32, D])
    dec_w1 = sb("dec_w1", [P, C, 64])
    dec_w2 = sb("dec_w2", [64, D])
    heads = sb("heads", [P, P])
    place = sb("place", [P, P + S0 - 1])
    pick_in = sb("pick_row", [P, S0])
    pick = sb("pick", [P, S0, P], F32R)
    AB = [ab2[:, 0], ab2[:, 1], tmp[:, 0], tmp[:, 1]]
    YB = [yb2[:, 0], yb2[:, 1], x5[:, 0], x5[:, 1]]
    NB = 4

    c0 = sem("const0")
    n = 0
    for dst, src in ((prev[:], prev_in), (maa_w1[:], maa_w1_in), (maa_w2[:], maa_w2_in[0:P]),
                     (maa_w24[:], maa_w2_in[P:P + 32]), (dec_w1[:], dec_w1_in), (dec_w2[:], dec_w2_in),
                     (heads[:], heads_in), (place[:], place_in), (pick_in[:], pick_in_dram), (s0[:], s0_in)):
        nc.sync.dma_start(dst, src).then_inc(c0, 16)
        n += 16
    consts0 = (c0, n)
    stage_next_weight()

    def flat(ap):
        return ap.rearrange("p b t -> p (b t)")

    def by_batch(ap):
        return ap.rearrange("p (b t) -> p b t", b=HB)

    Xs = [([Hh[:, c, k * HALF:(k + 1) * HALF] for c in range(C)], [Hl[:, c, k * HALF:(k + 1) * HALF] for c in range(C)])
          for k in range(2)]
    xs_read = [None, None]
    vh, vl = Xs[0]
    last_mix = None
    scratch = {"tmp": [None, None], "x5": [None, None], "mx": [None, None]}
    t_prep = {}

    def prepare(half):
        b0 = half * HB
        t_xn, t_sx = [], []
        got = t_prep[half] = {"xn": t_xn, "sx": t_sx}

        def first():
            got["root"] = moments([X[:, b0 + k, :] for k in range(HB)], [constants] * HB)

        def norm(k):
            i, t, _ = normalised_turn(ring, X[:, b0 + k, :], k, got["root"])
            act.wait(t, last_mix)
            ts = [act.done(nc.scalar.activation(xn[:, c, k, 1:T + 1], bank[i][:, c * T:(c + 1) * T], ACT.Identity,
                                                scale=V("ln1_w", c), bias=V("ln1_b", c))) for c in range(C)]
            ring.free[i] = ts
            t_xn.extend(ts)

        def shift():
            act.wait(consts0, last_mix)
            t_xn.append(act.done(nc.scalar.copy(xn[:, :, :, 0], prev[:, 1, :, b0:b0 + HB])))
            pool.wait(t_xn, last_mix)
            for c in range(C):
                t_sx.append(pool.done(nc.gpsimd.tensor_tensor(sx[:, c], xn[:, c, :, 0:T], xn[:, c, :, 1:T + 1],
                                                              ALU.subtract)))

        def low_rank():
            i1, i2 = ring.take(), ring.take()
            pe.wait(consts0)
            for c in range(C):
                dve.wait(t_xn, t_sx[c], scratch["mx"][c % 2])
                t = dve.done(nc.vector.scalar_tensor_tensor(out=mx[:, c % 2], in0=sx[:, c], scalar=V("maa_x", c),
                                                            in1=xn[:, c, :, 1:T + 1], op0=ALU.mult, op1=ALU.add))
                pe.wait(t)
                nc.tensor.matmul(bank[i1][:, 0:HALF], maa_w1[:, c, 0:P], flat(mx[:, c % 2]), start=c == 0, stop=c == C - 1)
                scratch["mx"][c % 2] = pe.done(nc.tensor.matmul(
                    bank[i2][0:32, 0:HALF], maa_w1[:, c, P:160], flat(mx[:, c % 2]), start=c == 0, stop=c == C - 1))
            act.wait(scratch["mx"][1], last_mix)
            got["th"] = [act.done(nc.scalar.activation(th[:], bank[i1][:, 0:HALF], ACT.Tanh)),
                         act.done(nc.scalar.activation(th4[:], bank[i2][0:32, 0:HALF], ACT.Tanh))]
            ring.free[i1] = ring.free[i2] = got["th"]

        return [first, lambda: norm(0), lambda: norm(1), lambda: norm(2), lambda: norm(3), shift, low_rank]

    def mixed(half, j, k):
        got = t_prep[half]
        out_t = []
        pe.wait(got["th"])
        for c in range(C):
            i = ring.take()
            if j < 4:
                left, right = maa_w2[32 * j:32 * j + 32, c * P:(c + 1) * P], th[32 * j:32 * j + 32, :]
            else:
                left, right = maa_w24[:, c * P:(c + 1) * P], th4[:]
            t = pe.done(nc.tensor.matmul(bank[i][:, 0:HALF], left, right, start=True, stop=True))
            s = c % 2
            dve.wait(t, scratch["tmp"][s], got["sx"])
            t = dve.done(nc.vector.scalar_tensor_tensor(
                out=tmp[:, s, :, 0:T], in0=by_batch(bank[i][:, 0:HALF]), scalar=V(f"maa_{j}", c),
                in1=sx[:, c], op0=ALU.add, op1=ALU.mult))
            ring.free[i] = t
            pool.wait(t, scratch["x5"][s], got["xn"])
            t = pool.done(nc.gpsimd.tensor_tensor(x5[:, s], tmp[:, s, :, 0:T], xn[:, c, :, 1:T + 1], ALU.add))
            scratch["tmp"][s] = t
            ts = split_sbuf(flat(x5[:, s]), Xs[k][0][c], Xs[k][1][c], t, [xs_read[k]])
            scratch["x5"][s] = ts
            out_t.append(ts)
        return out_t

    def project_block(weight, o, k, t_in):
        i = ring.take()
        for c in range(C):
            pe.wait(t_in[c])
            m = mm3(bank[i][:, 0:HALF], weight.block(c, o * P, P), (Xs[k][0][c], Xs[k][1][c]), c == 0, c == C - 1)
        xs_read[k] = t = pe.done(m)
        return i, t

    first_steps = prepare(0)
    first_steps[0]()
    feed_weights()
    for f in first_steps[1:]:
        f()
    dve.wait(consts0)
    t_pick_made = [dve.done(nc.vector.tensor_scalar(pick[:, d, :], heads[:], pick_in[:, d:d + 1], None, ALU.mult))
                   for d in range(S0)]
    t_w0 = dve.done(nc.vector.memset(wT[:, :, :, 0:1], 0.0))
    pool.wait(consts0)
    ab_free, yb_free = [None] * NB, [None] * NB
    att_read = None

    for half in range(2):
        b0 = half * HB
        t_in1 = mixed(half, 1, 0)
        feed_weights()
        t_in0 = mixed(half, 0, 1)
        i = ring.take()
        for c in range(C):
            pe.wait(t_in1[c])
            nc.tensor.matmul(bank[i][0:64, 0:HALF], dec_w1[:, c, :], Xs[0][0][c].bitcast(F32), start=c == 0, stop=False)
            m = nc.tensor.matmul(bank[i][0:64, 0:HALF], dec_w1[:, c, :], Xs[0][1][c].bitcast(F32), start=False, stop=c == C - 1)
        xs_read[0] = t = pe.done(m)
        act.wait(t)
        ring.free[i] = t_thd = act.done(nc.scalar.activation(thd[:], bank[i][0:64, 0:HALF], ACT.Tanh))
        t_in3 = mixed(half, 3, 0)
        feed_weights()
        pe.wait(t_thd)
        t_w = []
        for c in range(C):
            i = ring.take()
            t = pe.done(nc.tensor.matmul(bank[i][:, 0:HALF], dec_w2[:, c * P:(c + 1) * P], thd[:], start=True, stop=True))
            act.wait(t, t_w0)
            inner = wT[:, c, :, 1:T + 1]
            ring.free[i] = t = act.done(nc.scalar.activation(
                inner, by_batch(bank[i][:, 0:HALF]), ACT.Exp, bias=V("time_decay", c)))
            act.wait(t)
            t_w.append(act.done(nc.scalar.activation(inner, inner, ACT.Exp, scale=-1.0)))

        t_k, t_r, t_v = [], [], []
        wk = Weight("k")
        wk.need()
        for o in range(C):
            i, t = project_block(wk, o, 1, t_in0)
            act.wait(t)
            ring.free[i] = t = act.done(nc.scalar.copy(flat(kT[:, o]), bank[i][:, 0:HALF]))
            t_k.append(t)
        wk.give_up()
        feed_weights()
        t_in2 = mixed(half, 2, 1)
        wr = Weight("r")
        wr.need()
        for o in range(C):
            i, t = project_block(wr, o, 0, t_in3)
            act.wait(t)
            ring.free[i] = t = act.done(nc.scalar.copy(flat(rT[:, o]), bank[i][:, 0:HALF]))
            t_r.append(t)
        wr.give_up()
        feed_weights()
        wv = Weight("v")
        wv.need()
        for o in range(C):
            i, t = project_block(wv, o, 1, t_in2)
            ts = split_psum(bank[i][:, 0:HALF], vh[o], vl[o], t, [xs_read[0]])
            ring.free[i] = ts
            t_v.append(ts)
        wv.give_up()
        feed_weights()
        t_in4 = mixed(half, 4, 1)
        last_mix = [pool.last(), pe.last(), dve.last()]

        t_att = []
        for o in range(C):
            s = o % 2
            dve.wait(t_k[o], t_r[o], t_v[o], scratch["tmp"][s], scratch["x5"][s], att_read)
            t = dve.done(nc.vector.scalar_tensor_tensor(out=tmp[:, s, :, 0:T], in0=rT[:, o], scalar=V("u", o), in1=kT[:, o],
                                                        op0=ALU.mult, op1=ALU.mult))
            i = ring.take()
            pe.wait(t)
            scratch["tmp"][s] = t = pe.done(nc.tensor.matmul(bank[i][:, 0:HALF], heads[:], tmp[:, s, :, 0:T], start=True, stop=True))
            dve.wait(t)
            t1 = dve.done(nc.vector.tensor_tensor(flat(att[:, o]), bank[i][:, 0:HALF], vh[o].bitcast(F32), ALU.mult))
            ring.free[i] = t2 = dve.done(nc.vector.tensor_tensor(flat(x5[:, s]), bank[i][:, 0:HALF], vl[o].bitcast(F32), ALU.mult))
            dve.wait(t1, t2)
            t_att.append(dve.done(nc.vector.tensor_tensor(flat(att[:, o]), flat(att[:, o]), flat(x5[:, s]), ALU.add)))
            scratch["x5"][s] = t_att[-1]
        ab_free[2:4], yb_free[2:4] = scratch["tmp"], scratch["x5"]

        wg = Weight("g")
        sums = []
        t_c, t_g = {}, {}
        t_kv_of, t_y_of = {}, {}
        steps = [(o, d) for o in range(C) for d in range(S0)]
        picked = {}
        var_read = [None, None]

        def spread(n):
            if n < len(steps):
                o, d = steps[n]
                i = pick_ring.take()
                pe.wait(t_v[o], t_pick_made)
                nc.tensor.matmul(bank[i][:, 0:HALF], pick[:, d, :], vh[o], start=True, stop=False)
                picked[n] = i, pe.done(nc.tensor.matmul(bank[i][:, 0:HALF], pick[:, d, :], vl[o], start=False, stop=True))

        def sum_rows(n, t):
            o, d = steps[n]
            j = y_banks[o % 2]
            pe.wait(t)
            if d == 0:
                pe.wait(ring.free.get(j))
            yb_free[n % NB] = t = pe.done(nc.tensor.matmul(
                bank[j][:, 0:HALF], place[:, S0 - 1 - d:S0 - 1 - d + P], flat(YB[n % NB]),
                start=d == 0, stop=d == S0 - 1))
            if d == S0 - 1:
                dve.wait(t, t_att[o])
                ring.free[j] = t_att[o] = dve.done(nc.vector.tensor_tensor(
                    flat(att[:, o]), bank[j][:, 0:HALF], flat(att[:, o]), ALU.add))

        def gate(o):
            wg.need()
            i, t = project_block(wg, o, 1, t_in4)
            act.wait(t, t_kv_of[o])
            ring.free[i] = t_g[o] = act.done(nc.scalar.activation(flat(kT[:, o]), bank[i][:, 0:HALF], ACT.Silu))

        def centre(o):
            i = ring.take()
            pe.wait(t_att[o])
            t = pe.done(nc.tensor.matmul(bank[i][:, 0:HALF], heads[:], flat(att[:, o]), start=True, stop=True))
            dve.wait(t)
            ring.free[i] = t_c[o] = dve.done(nc.vector.scalar_tensor_tensor(
                out=flat(att[:, o]), in0=bank[i][:, 0:HALF], scalar=-1.0 / S0, in1=flat(att[:, o]),
                op0=ALU.mult, op1=ALU.add))

        def variance(o):
            s = o % 2
            pool.wait(t_c[o], scratch["mx"][s])
            t = pool.done(nc.gpsimd.tensor_tensor(flat(mx[:, s]), flat(att[:, o]), flat(att[:, o]), ALU.mult))
            i = ring.take()
            pe.wait(t)
            scratch["mx"][s] = t = pe.done(nc.tensor.matmul(bank[i][:, 0:HALF], heads[:], flat(mx[:, s]), start=True, stop=True))
            dve.wait(t, t_y_of[o])
            ring.free[i] = t_c[o] = dve.done(nc.vector.tensor_scalar(flat(rT[:, o]), bank[i][:, 0:HALF], 1.0 / S0, 1e-5,
                                                                     ALU.mult, ALU.add))

        prep = prepare(1) if half == 0 else []
        ahead, lag = 3, 2
        pick_ring = Ring([0, 1, 2, 3])
        pick_ring.free = ring.free
        ring.banks = [4, 5]
        for n in range(ahead):
            spread(n)
        for n, (o, d) in enumerate(steps):
            s = n % NB
            spread(n + ahead)
            i, t = picked.pop(n)
            pool.wait(ab_free[s])
            t_init = pool.done(nc.gpsimd.tensor_copy(AB[s][:, :, 0], s0[:, o, d, b0:b0 + HB]))
            dve.wait(t, ab_free[s], t_k[o])
            ring.free[i] = t_kv_of[o] = t = dve.done(nc.vector.tensor_tensor(
                AB[s][:, :, 1:T + 1], by_batch(bank[i][:, 0:HALF]), kT[:, o], ALU.mult))
            dve.wait(t, t_init, t_w[o])
            t = dve.done(nc.vector.tensor_tensor_scan(flat(AB[s]), flat(wT[:, o]), flat(AB[s]), 0.0, ALU.mult, ALU.add))
            pool.wait(t, yb_free[s], t_r[o])
            ab_free[s] = t_y_of[o] = t = pool.done(nc.gpsimd.tensor_tensor(YB[s], AB[s][:, :, 0:T], rT[:, o], ALU.mult))
            sums.append((n, t))
            if len(sums) > lag:
                sum_rows(*sums.pop(0))
            if o > 0 and d == 4:
                gate(o - 1)
            if o > 0 and d == 7:
                centre(o - 1)
            if o > 0 and d == 10:
                variance(o - 1)
            if prep and d in (2, 12):
                prep.pop(0)()
            if n in (20, 40):
                feed_weights()
        for x in sums:
            sum_rows(*x)
        ring.banks = [0, 1, 2, 3, 4, 5]
        gate(C - 1)
        wg.give_up()
        centre(C - 1)
        variance(C - 1)
        scratch["tmp"], scratch["x5"] = ab_free[2:4], yb_free[2:4]
        t_gn = []
        for f in prep:
            f()
        t_root = []
        for o in range(C):
            act.wait(t_c[o])
            t_root.append(act.done(nc.scalar.activation(flat(rT[:, o]), flat(rT[:, o]), ACT.Sqrt)))
        for o in range(C):
            dve.wait(t_root[o])
            t = dve.done(nc.vector.reciprocal(flat(rT[:, o]), flat(rT[:, o])))
            dve.wait(t)
            t = dve.done(nc.vector.scalar_tensor_tensor(out=flat(att[:, o]), in0=flat(att[:, o]), scalar=V("gn_w", o),
                                                        in1=flat(rT[:, o]), op0=ALU.mult, op1=ALU.mult))
            dve.wait(t, t_g[o])
            t = dve.done(nc.vector.scalar_tensor_tensor(out=flat(att[:, o]), in0=flat(att[:, o]), scalar=V("gn_b", o),
                                                        in1=flat(kT[:, o]), op0=ALU.add, op1=ALU.mult))
            t_gn.append(split_sbuf(flat(att[:, o]), Xs[0][0][o], Xs[0][1][o], t, [pe.last()]))
        att_read = t_gn
        wo = Weight("o")
        wo.need()
        for i4 in range(HB):
            i = ring.take()
            for c in range(C):
                pe.wait(t_gn[c])
                m = mm3(bank[i][0:T, :], (Xs[0][0][c][:, i4 * T:(i4 + 1) * T], Xs[0][1][c][:, i4 * T:(i4 + 1) * T]),
                        wo.block(c, 0, D), c == 0, c == C - 1)
            xs_read[0] = t = pe.done(m)
            dve.wait(t)
            ring.free[i] = dve.done(nc.vector.tensor_tensor(X[:, b0 + i4, :], bank[i][0:T, :], X[:, b0 + i4, :], ALU.add))
        wo.give_up()
        feed_weights()

    new_phase()
    ring = Ring(list(range(8)))
    xn = sb("xn1", [P, C, B, T + 1])
    sx = sb("sx1", [P, C, B, T])
    xm = sb("xm1", [P, 2, HB, T])
    rr = sb("rr", [T, B, D])
    kh = sb("kk_hi", [P, C, NT], F32R)
    kl = sb("kk_lo", [P, C, NT], F32R)
    prev = sb("prev1", [P, 2, C, B])
    f_tmp = sb("f_tmp", [T, 2, D])
    prev_stream = Stream("prev_loaded")
    t_prev = prev_stream.start(prev[:], prev_in)
    t_row = load_row("bo1")
    t_xn, t_sx = {}, {}
    act.wait(t_prev)
    t_p = act.done(nc.scalar.copy(xn[:, :, :, 0], prev[:, 0, :, :]))
    xm_free = [None, None]
    n_xm = 0

    def ffn_norm(half):
        bs = range(half * HB, half * HB + HB)
        t_root = moments([X[:, b, :] for b in bs], [None] * HB)
        ts = [t_p]
        for k, b in enumerate(bs):
            i, t, _ = normalised_turn(ring, X[:, b, :], k, t_root)
            act.wait(t)
            for c in range(C):
                ring.free[i] = t = act.done(nc.scalar.activation(
                    xn[:, c, b, 1:T + 1], bank[i][:, c * T:(c + 1) * T], ACT.Identity, scale=V("ln2_w", c),
                    bias=V("ln2_b", c)))
            ts.append(t)
        t_xn[half] = ts
        pool.wait(ts)
        for c in range(C):
            h = slice(half * HB, half * HB + HB)
            t_sx[half, c] = pool.done(nc.gpsimd.tensor_tensor(sx[:, c, h], xn[:, c, h, 0:T], xn[:, c, h, 1:T + 1],
                                                              ALU.subtract))

    def ffn_mix(name, half, hi, lo):
        nonlocal n_xm
        ts = []
        for c in range(C):
            s = n_xm % 2
            n_xm += 1
            bs = slice(half * HB, half * HB + HB)
            dve.wait(t_sx[half, c], t_xn[half], xm_free[s])
            t = dve.done(nc.vector.scalar_tensor_tensor(out=xm[:, s], in0=sx[:, c, bs], scalar=V(name, c),
                                                        in1=xn[:, c, bs, 1:T + 1], op0=ALU.mult, op1=ALU.add))
            cols = slice(half * HALF, (half + 1) * HALF)
            xm_free[s] = split_sbuf(flat(xm[:, s]), hi[:, c, cols], lo[:, c, cols], t)
            ts.append(xm_free[s])
        return ts

    wr = Weight("fr")
    wk = Weight("fk")
    wv = Weight("fv")
    t_rr = {}
    t_kk = {}
    t_km = {}

    def receptance(half, t_in):
        wr.need()
        for b in range(half * HB, half * HB + HB):
            i = ring.take()
            for c in range(C):
                pe.wait(t_in[c])
                m = mm3(bank[i][0:T, :], (kh[:, c, b * T:(b + 1) * T], kl[:, c, b * T:(b + 1) * T]), wr.block(c, 0, D),
                        c == 0, c == C - 1)
            t = pe.done(m)
            act.wait(t)
            ring.free[i] = t_rr[b] = act.done(nc.scalar.activation(rr[:, b, :], bank[i][0:T, :], ACT.Sigmoid))
        return pe.last()

    def ffn_keys(half, kh_free):
        nonlocal n_xm
        wk.need()
        cols = slice(half * HALF, (half + 1) * HALF)
        for o in range(C):
            i = ring.take()
            for c in range(C):
                pe.wait(t_km[half][c])
                m = mm3(bank[i][:, 0:HALF], wk.block(c, o * P, P), (Hh[:, c, cols], Hl[:, c, cols]), c == 0, c == C - 1)
            t = pe.done(m)
            s = n_xm % 2
            n_xm += 1
            act.wait(t, xm_free[s])
            ring.free[i] = t = act.done(nc.scalar.activation(flat(xm[:, s]), bank[i][:, 0:HALF], ACT.Relu))
            dve.wait(t)
            t = dve.done(nc.vector.tensor_tensor(flat(xm[:, s]), flat(xm[:, s]), flat(xm[:, s]), ALU.mult))
            t_kk[half, o] = xm_free[s] = split_sbuf(flat(xm[:, s]), kh[:, o, cols], kl[:, o, cols], t, [kh_free])

    ffn_norm(0)
    t_r0 = ffn_mix("ffn_maa_r", 0, kh, kl)
    t_km[0] = ffn_mix("ffn_maa_k", 0, Hh, Hl)
    ffn_norm(1)
    r0_read = receptance(0, t_r0)
    t_r1 = ffn_mix("ffn_maa_r", 1, kh, kl)
    t_km[1] = ffn_mix("ffn_maa_k", 1, Hh, Hl)
    feed_weights()
    ffn_keys(0, r0_read)
    r1_read = receptance(1, t_r1)
    wr.give_up()
    ffn_keys(1, r1_read)
    wk.give_up()
    wv.need()
    ft = [None, None]
    t_x = [None] * B
    h_read = pe.last()
    normed = {}
    for b in range(B):
        i = ring.take()
        for c in range(C):
            pe.wait(t_kk[b // HB, c])
            m = mm3(bank[i][0:T, :], (kh[:, c, b * T:(b + 1) * T], kl[:, c, b * T:(b + 1) * T]), wv.block(c, 0, D),
                    c == 0, c == C - 1)
        t = pe.done(m)
        dve.wait(t, t_rr[b], ft[b % 2])
        ring.free[i] = t = dve.done(nc.vector.tensor_tensor(f_tmp[:, b % 2, :], bank[i][0:T, :], rr[:, b, :], ALU.mult))
        pool.wait(t)
        t_x[b] = ft[b % 2] = pool.done(nc.gpsimd.tensor_tensor(X[:, b, :], f_tmp[:, b % 2, :], X[:, b, :], ALU.add))
        if b >= 2:
            normed |= norm_split(ring, [b - 2], "a1_s", "a1_o", [t_x[b - 2]], h_read, t_row)
        if b % 3 == 0:
            feed_weights()
    wv.give_up()
    normed |= norm_split(ring, [B - 2, B - 1], "a1_s", "a1_o", t_x[B - 2:B], h_read, t_row)

    new_phase()
    ctx_raw = sb("ctx_raw", [P, C, SP])
    cxh = sb("ctx_hi", [P, 2, C, SP], F32R)
    cxl = sb("ctx_lo", [P, 2, C, SP], F32R)
    qg = sb("q_group", [P, HK, NT])
    qh = sb("q_hi", [P, HK, T], F32R)
    ql = sb("q_lo", [P, HK, T], F32R)
    Kh = sb("K_hi", [P, HK, SP], F32R)
    Kl = sb("K_lo", [P, HK, SP], F32R)
    Vt = sb("V", [P, 3, D])
    Pm = sb("probs", [T, HK, SP])
    PT = sb("probs_T", [P, HK, 3, T])
    oh = sb("o_hi", [P, HK, T], F32R)
    ol = sb("o_lo", [P, HK, T], F32R)
    bv = sb("v_bias", [P, 2, D])
    mxs = sb("max", [T, HK])
    nb = sb("minus_max", [T, HK])
    ssum = sb("sum", [T, HK])
    rsum = sb("inv_sum", [T, HK])
    ctx_stream = Stream("ctx_loaded")
    bv_stream = Stream("bv_loaded")

    units = [(layer, g, b) for layer in (1, 2) for g in range(G) for b in range(B)]
    ctx_raw_free = [None]
    ctx_loaded = [None]

    def load_ctx(n):
        if n < len(units):
            ctx_loaded[0] = ctx_stream.start(ctx_raw[:], ctxT_in[units[n][2]], ctx_raw_free[0])

    load_ctx(0)
    cx_free, cx_ready = [None, None], [None, None]

    def split_ctx(n):
        if n < len(units):
            s = n % 2
            ts = []
            for c in range(0, C, 2):
                ts += split_sbuf(ctx_raw[:, c:c + 2, :], cxh[:, s, c:c + 2, :], cxl[:, s, c:c + 2, :],
                                 ctx_loaded[0], [cx_free[s]])
            cx_ready[s] = ctx_raw_free[0] = ts
            load_ctx(n + 1)

    split_ctx(0)
    work = Ring([0, 1, 2, 3])
    t_logit_free = [None] * HK
    t_x = [None] * B
    free = {"K": None, "V": None, "P": None, "PT": None, "o": None, "q": None, "bv": None, "qg": None}

    def tail(u):
        t_p, t_vs, wo_block, b = u["t_p"], u["t_v"], u["wo"], u["b"]
        t_pt = []

        def transposes(h):
            i = work.take()
            pe.wait(t_p[h])
            for j, (k0, kn) in enumerate(KTILES):
                m = nc.tensor.transpose(bank[i][0:kn, j * T:(j + 1) * T], Pm[:, h, k0:k0 + kn], ident[0:T, 0:T])
            t = pe.done(m)
            e, f = (act, nc.scalar.copy) if h % 2 else (dve, nc.vector.tensor_copy)
            e.wait(t, free["PT"])
            work.free[i] = t2 = e.done(f(PT[:, h].rearrange("p j t -> p (j t)"), bank[i][:, 0:3 * T]))
            t_pt.append(t2)
            if h == HK - 1:
                free["P"] = t

        def values():
            i = work.take()
            pe.wait(t_pt, t_vs)
            for h in range(HK):
                for j, (k0, kn) in enumerate(KTILES):
                    m = nc.tensor.matmul(bank[i][:, h * T:(h + 1) * T], Vt[0:kn, j, h * P:(h + 1) * P],
                                         PT[0:kn, h, j, :], start=j == 0, stop=j == 2)
            t = pe.done(m)
            free["V"] = free["PT"] = t
            ts = split_psum(bank[i][:, 0:HK * T], oh[:].rearrange("p h t -> p (h t)"),
                            ol[:].rearrange("p h t -> p (h t)"), t, [free["o"]])
            work.free[i] = ts
            u["t_o"] = ts

        def outputs():
            i = work.take()
            wo_block.need()
            pe.wait(u["t_o"])
            for h in range(HK):
                m = mm3(bank[i][0:T, :], (oh[:, h, :], ol[:, h, :]), wo_block.block(h, 0, D), h == 0, h == HK - 1)
            free["o"] = t = pe.done(m)
            dve.wait(t, t_x[b])
            work.free[i] = t_x[b] = dve.done(nc.vector.tensor_tensor(X[:, b, :], bank[i][0:T, :], X[:, b, :], ALU.add))
            if b == B - 1:
                wo_block.give_up()

        def norm():
            bs = [b - 1] if b < B - 1 else [b - 1, b]
            normed.update(norm_split(work, bs, *u["norm"], [t_x[k] for k in bs], u["h_read"], u["t_row"]))

        return [lambda: transposes(0), lambda: transposes(1), lambda: transposes(2), lambda: transposes(3),
                values, outputs] + ([norm] if u["norm"] and b > 0 else [])

    n_unit = 0
    last_tail = []
    for layer in (1, 2):
        for g in range(G):
            wq = Weight(f"q{layer}_{g}")
            wk = Weight(f"k{layer}_{g}")
            wv = Weight(f"v{layer}_{g}")
            wo = Weight(f"o{layer}_{g}")
            t_bv = bv_stream.start(bv[:], bv_in[(layer - 1) * G + g], free["bv"])
            wq.need()
            t_q = []
            for half in range(2):
                if half == 1:
                    while last_tail:
                        last_tail.pop(0)()
                for h in range(HK):
                    cols = slice(half * HALF, (half + 1) * HALF)
                    i = work.take()
                    pe.wait([normed[b][0] for b in range(half * HB, half * HB + HB)])
                    for c in range(C):
                        m = mm3(bank[i][:, 0:HALF], wq.block(c, h * P, P), (Hh[:, c, cols], Hl[:, c, cols]),
                                c == 0, c == C - 1)
                    t = pe.done(m)
                    act.wait(t, free["qg"])
                    work.free[i] = t = act.done(nc.scalar.activation(qg[:, h, cols], bank[i][:, 0:HALF], ACT.Identity,
                                                                     bias=V(f"bq{layer}", g * HK + h)))
                    t_q.append(t)
                    for _ in range(2):
                        if last_tail:
                            last_tail.pop(0)()
            wq.give_up()
            h_read = pe.last()
            if g == 0:
                t_x = [normed[b][1] for b in range(B)]
                t_row = load_row("bo2" if layer == 1 else "b_fc2", t_x)
            bk0 = VEC_AT[f"bias_k{layer}"][0] + g * HK
            learned = vec[:, bk0:bk0 + HK]
            t_lk = split_sbuf(learned, Kh[:, :, S], Kl[:, :, S], None, [free["K"]])
            for b in range(B):
                s = n_unit % 2
                cxr = cx_ready[s]
                steps = last_tail
                u = {"b": b, "wo": wo, "t_v": [], "t_p": [], "h_read": h_read, "t_row": t_row,
                     "norm": None if g < G - 1 else ("a2_s", "a2_o") if layer == 1 else ("am_s", "am_o")}
                t_qs = split_sbuf(qg[:, :, b * T:(b + 1) * T], qh[:], ql[:], t_q, [free["q"]])
                if b == B - 1:
                    free["qg"] = t_qs
                wk.need()
                pe.wait(cxr)
                t_ks = []
                for h in range(HK):
                    i = work.take()
                    for c in range(C):
                        m = mm3(bank[i][:, 0:SP], wk.block(c, h * P, P), (cxh[:, s, c, :], cxl[:, s, c, :]),
                                c == 0, c == C - 1)
                    t = pe.done(m)
                    ts = split_psum(bank[i][:, 0:S], Kh[:, h, 0:S], Kl[:, h, 0:S], t, [free["K"]],
                                    bias=V(f"bk{layer}", g * HK + h))
                    work.free[i] = ts
                    t_ks.append(ts)
                    if h >= 1 and steps:
                        steps.pop(0)()
                        if h >= 3:
                            steps.pop(0)()
                if b == B - 1:
                    wk.give_up()
                wv.need()
                for j, (k0, kn) in enumerate(KTILES):
                    i = work.take()
                    for c in range(C):
                        m = mm3(bank[i][0:kn, :], (cxh[:, s, c, k0:k0 + kn], cxl[:, s, c, k0:k0 + kn]),
                                wv.block(c, 0, D), c == 0, c == C - 1)
                    t = pe.done(m)
                    if steps and j == 0:
                        steps.pop(0)()
                    dve.wait(t, t_bv, free["V"])
                    work.free[i] = t = dve.done(nc.vector.tensor_tensor(Vt[0:kn, j, :], bank[i][0:kn, :],
                                                                        bv[0:kn, j // 2, :], ALU.add))
                    u["t_v"].append(t)
                    if steps and j >= 1:
                        steps.pop(0)()
                cx_free[s] = pe.last()
                free["bv"] = dve.last()
                if b == B - 1:
                    wv.give_up()
                pe.wait(t_qs, t_lk)
                t_e, t_m = [], []
                for h in range(HK):
                    pe.wait(t_ks[h], t_logit_free[h])
                    t = pe.done(mm3(bank[4 + h][0:T, 0:SP], (qh[:, h, :], ql[:, h, :]), (Kh[:, h, :], Kl[:, h, :]),
                                    True, True))
                    dve.wait(t)
                    t_m.append(dve.done(nc.vector.tensor_reduce(mxs[:, h:h + 1], bank[4 + h][0:T, 0:SP], AX.X, ALU.max)))
                free["K"] = free["q"] = pe.last()
                n_unit += 1
                split_ctx(n_unit)
                dve.wait(t_m)
                t = dve.done(nc.vector.tensor_scalar(nb[:], mxs[:], -SCALE1, None, ALU.mult))
                act.wait(t, free["P"])
                for h in range(HK):
                    t_logit_free[h] = t = act.done(nc.scalar.activation(
                        Pm[:, h, :], bank[4 + h][0:T, 0:SP], ACT.Exp, bias=nb[:, h:h + 1], scale=SCALE1,
                        accum_out=ssum[:, h:h + 1]))
                    t_e.append(t)
                dve.wait(t_e)
                t = dve.done(nc.vector.reciprocal(rsum[:], ssum[:]))
                pool.wait(t)
                for h in range(HK):
                    u["t_p"].append(pool.done(nc.gpsimd.tensor_scalar(Pm[:, h, :], Pm[:, h, :], rsum[:, h:h + 1], 1.0,
                                                                      ALU.mult, ALU.mult)))
                while steps:
                    steps.pop(0)()
                last_tail = tail(u)
                feed_weights()
    for f in last_tail:
        f()

    def mlp(tag, bias, func, t_h, t_x):
        Gf = sb(f"g_{tag}", [P, 2, HALF])
        Gh = sb(f"g_hi_{tag}", [P, C, NT], F32R)
        Gl = sb(f"g_lo_{tag}", [P, C, NT], F32R)
        gf_free = [None, None]
        gh_free = [None, None]
        n = 0
        for g in range(4):
            w1 = Weight(f"m{tag}a_{g}")
            w2 = Weight(f"m{tag}b_{g}")
            w1.need()
            t_g = {}
            for half in range(2):
                cols = slice(half * HALF, (half + 1) * HALF)
                pe.wait(t_h[half * HB:half * HB + HB])
                for o in range(C):
                    i = ring.take()
                    for c in range(C):
                        m = mm3(bank[i][:, 0:HALF], w1.block(c, o * P, P), (Hh[:, c, cols], Hl[:, c, cols]),
                                c == 0, c == C - 1)
                    t = pe.done(m)
                    s = n % 2
                    n += 1
                    act.wait(t, gf_free[s])
                    ring.free[i] = t = act.done(nc.scalar.activation(Gf[:, s], bank[i][:, 0:HALF], func,
                                                                     bias=V(bias, g * C + o)))
                    t_g[half, o] = gf_free[s] = split_sbuf(Gf[:, s], Gh[:, o, cols], Gl[:, o, cols], t, [gh_free[half]])
                if half == 0:
                    feed_weights()
            w1.give_up()
            w2.need()
            for b in range(B):
                i = ring.take()
                for o in range(C):
                    pe.wait(t_g[b // HB, o])
                    m = mm3(bank[i][0:T, :], (Gh[:, o, b * T:(b + 1) * T], Gl[:, o, b * T:(b + 1) * T]),
                            w2.block(o, 0, D), o == 0, o == C - 1)
                t = pe.done(m)
                gh_free[b // HB] = t
                dve.wait(t, t_x[b])
                ring.free[i] = t_x[b] = dve.done(nc.vector.tensor_tensor(X[:, b, :], bank[i][0:T, :], X[:, b, :], ALU.add))
                if b == HB:
                    feed_weights()
            w2.give_up()
        return t_x

    new_phase()
    ring = Ring(list(range(8)))
    t_h = [normed[b][0] for b in range(B)]
    mlp("1", "b_fc1", ACT.Gelu, t_h, [normed[b][1] for b in range(B)])

    new_phase()
    ring = Ring([0, 1, 2, 3])
    ctx_raw = sb("ctx_raw2", [P, C, SP])
    q2 = sb("q2", [P, C, NT])
    qh = sb("q2_hi", [P, C, T], F32R)
    ql = sb("q2_lo", [P, C, T], F32R)
    Kl_f = sb("K2_latents", [P, C, HALF])
    Kh = sb("K2_hi", [P, C, SK2], F32R)
    Kl = sb("K2_lo", [P, C, SK2], F32R)
    Vt = sb("V2", [P, 2, 4, D])
    Pm = sb("probs2", [T, 4, SK2])
    NPT = 3
    PT = sb("probs2_T", [P, NPT, 4, T])
    mask_i = sb("mask_int", [T, SP], I32)
    mask = sb("mask_bias", [T, SK2])
    o_row = sb("out_bias", [T, D])
    A = sb("attended", [T, D])
    mxs = sb("max2", [T, H2])
    nb = sb("minus_max2", [T, H2])
    ssum = sb("sum2", [T, 2, H2])
    rsum = sb("inv_sum2", [T, H2])
    rows2 = sem("rows2")
    nc.sync.dma_start(o_row[:], rows_in[ROWS.index("out_b")]).then_inc(rows2, 16)
    t_rows2 = (rows2, 16)
    mask_stream = Stream("mask_loaded")
    ctx2_stream = Stream("ctx2_loaded")
    t_ctx = ctx2_stream.start(ctx_raw[:], ctxT_in[0])
    t_mask_in = mask_stream.start(mask_i[:], mask_in[0])
    t_mz = dve.done(nc.vector.memset(mask[:, SP:SK2], 0.0))

    t_h = []
    for b in range(B):
        i, t = turn(ring, X[:, b, :], None)
        cols = slice(b * T, (b + 1) * T)
        ts = split_psum(bank[i][:, 0:C * T].rearrange("p (c t) -> p c t", c=C), Hh[:, :, cols], Hl[:, :, cols], t)
        ring.free[i] = ts
        t_h.append(ts)

    def project2(weight, half, bias, dst, free):
        cols = slice(half * HALF, (half + 1) * HALF)
        pe.wait(t_h[half * HB:half * HB + HB])
        ts = []
        for o in range(C):
            i = ring.take()
            for c in range(C):
                m = mm3(bank[i][:, 0:HALF], weight.block(c, o * P, P), (Hh[:, c, cols], Hl[:, c, cols]), c == 0, c == C - 1)
            t = pe.done(m)
            act.wait(t, free)
            ring.free[i] = t = act.done(nc.scalar.activation(dst(o), bank[i][:, 0:HALF], ACT.Identity, bias=V(bias, o)))
            ts.append(t)
        return ts

    wq = Weight("p_q")
    wq.need()
    t_q = []
    for half in range(2):
        t_q += project2(wq, half, "q2_b", lambda o: q2[:, o, half * HALF:(half + 1) * HALF], None)
    cxh, cxl = Wh[:, wq.slot, :, 0:SP], Wl[:, wq.slot, :, 0:SP]
    cx_free = pe.last()
    wk, wv, wo = Weight("p_k"), Weight("p_v"), Weight("p_o")
    wk.need()
    wv.need()
    logits_read = [None] * 4
    key_read = [None] * C
    value_read = [None, None]
    prob_read = [None] * 4
    pt_read = [None] * NPT
    t_klat_split = t_cx = t_qs = None
    t_klat = []
    t_ks = [None] * C
    t_vs = {}
    t_mask = None
    t_h2 = []
    a_read = None
    n_head = 0

    def split_context(b):
        nonlocal t_cx, t_ctx
        t_cx = []
        for c in range(0, C, 2):
            t_cx += split_sbuf(ctx_raw[:, c:c + 2], cxh[:, c:c + 2], cxl[:, c:c + 2], t_ctx, [cx_free])
        if b + 1 < B:
            t_ctx = ctx2_stream.start(ctx_raw[:], ctxT_in[b + 1], t_cx)

    def keys(b, o):
        i = ring.take()
        pe.wait(t_cx)
        for c in range(C):
            m = mm3(bank[i][:, 0:SP], wk.block(c, o * P, P), (cxh[:, c, :], cxl[:, c, :]), c == 0, c == C - 1)
        t = pe.done(m)
        ring.free[i] = t_ks[o] = split_psum(bank[i][:, 0:SP], Kh[:, o, 0:SP], Kl[:, o, 0:SP], t, [key_read[o]],
                                            bias=V("k2_b", o))

    def latent_keys(b):
        nonlocal t_klat, t_klat_split
        if b % HB == 0:
            t_klat = project2(wk, b // HB, "k2_b", lambda o: Kl_f[:, o, :], t_klat_split)
        k = b % HB
        t_klat_split = split_sbuf(Kl_f[:, :, k * T:(k + 1) * T], Kh[:, :, SP:SK2], Kl[:, :, SP:SK2], t_klat, key_read)

    def values(b, j):
        nonlocal cx_free
        k0, kn = KTILES2[j]
        cols = slice(b * T, (b + 1) * T)
        i = ring.take()
        pe.wait(t_cx, t_h[b])
        for c in range(C):
            left = (cxh[:, c, k0:k0 + kn], cxl[:, c, k0:k0 + kn]) if j < 3 else (Hh[:, c, cols], Hl[:, c, cols])
            m = mm3(bank[i][0:kn, :], left, wv.block(c, 0, D), c == 0, c == C - 1)
        cx_free = t = pe.done(m)
        e, f = (act, nc.scalar.copy) if j % 2 else (dve, nc.vector.tensor_copy)
        e.wait(t, value_read[b % 2])
        ring.free[i] = t_vs[b % 2, j] = e.done(f(Vt[0:kn, b % 2, j, :], bank[i][0:kn, :]))

    def queries(b):
        nonlocal t_qs, t_mask, t_mask_in
        t_qs = split_sbuf(q2[:, :, b * T:(b + 1) * T], qh[:], ql[:], t_q, key_read)
        dve.wait(t_mask_in, logits_read)
        t_mask = dve.done(nc.vector.tensor_scalar(mask[:, 0:SP], mask_i[:], 0.0, GAP, ALU.is_equal, ALU.mult))
        if b + 1 < B:
            t_mask_in = mask_stream.start(mask_i[:], mask_in[b + 1], t_mask)

    t_e = [None] * 4

    def logits(b, o):
        pe.wait(t_qs, t_ks[o], t_klat_split)
        t_m = []
        for k in range(4):
            rows = slice(32 * k, 32 * k + 32)
            pe.wait(logits_read[k])
            t = pe.done(mm3(bank[4 + k][0:T, 0:SK2], (qh[rows, o, :], ql[rows, o, :]), (Kh[rows, o, :], Kl[rows, o, :]),
                            True, True))
            dve.wait(t, t_mask, t_mz, prob_read[k])
            logits_read[k] = t = dve.done(nc.vector.tensor_tensor_reduce(
                out=Pm[:, k, :], in0=bank[4 + k][0:T, 0:SK2], in1=mask[:], scale=1.0, scalar=-3.0e38,
                op0=ALU.add, op1=ALU.max, accum_out=mxs[:, 4 * o + k:4 * o + k + 1]))
            t_m.append(t)
        key_read[o] = pe.last()
        dve.wait(t_m)
        t = dve.done(nc.vector.tensor_scalar(nb[:, 4 * o:4 * o + 4], mxs[:, 4 * o:4 * o + 4], -SCALE2, None, ALU.mult))
        act.wait(t)
        for k in range(4):
            h = 4 * o + k
            t_e[k] = act.done(nc.scalar.activation(Pm[:, k, :], Pm[:, k, :], ACT.Exp, bias=nb[:, h:h + 1],
                                                   scale=SCALE2, accum_out=ssum[:, b % 2, h:h + 1]))

    o_bank = {}

    def block(b, o):
        nonlocal n_head
        later = []

        def transposes(k):
            nonlocal n_head
            s = n_head % NPT
            n_head += 1
            i = ring.take()
            pe.wait(t_e[k])
            for j, (k0, kn) in enumerate(KTILES2):
                m = nc.tensor.transpose(bank[i][0:kn, j * T:(j + 1) * T], Pm[:, k, k0:k0 + kn], ident[0:T, 0:T])
            prob_read[k] = t = pe.done(m)
            act.wait(t, pt_read[s])
            ring.free[i] = t = act.done(nc.scalar.copy(PT[:, s].rearrange("p j t -> p (j t)"), bank[i][:, 0:4 * T]))
            later.append((k, s, t))

        def product():
            k, s, t = later.pop(0)
            h = 4 * o + k
            pe.wait(t, [t_vs[b % 2, j] for j in range(4)])
            for j, (k0, kn) in enumerate(KTILES2):
                m = nc.tensor.matmul(bank[o_bank[b]][0:T, h * D2:(h + 1) * D2], PT[0:kn, s, j, :],
                                     Vt[0:kn, b % 2, j, h * D2:(h + 1) * D2], start=j == 0, stop=j == 3)
            pt_read[s] = value_read[b % 2] = pe.done(m)

        if o == 0:
            o_bank[b] = ring.take()
            ring.banks = [i for i in ring.banks if i != o_bank[b]]
        transposes(0)
        transposes(1)
        for k in range(2, 4):
            transposes(k)
            product()
        product()
        product()

    def divide(b):
        i = o_bank[b]
        dve.wait(act.last(), value_read[b % 2], a_read)
        t = dve.done(nc.vector.reciprocal(rsum[:], ssum[:, b % 2, :]))
        dve.wait(t)
        t = dve.done(nc.vector.tensor_tensor(
            A[:].rearrange("q (h d) -> q h d", h=H2), bank[i][0:T, :].rearrange("q (h d) -> q h d", h=H2),
            rsum[:].unsqueeze(2).broadcast_to([T, H2, D2]), ALU.mult))
        ring.free[i] = t
        ring.banks = ring.banks + [i]
        return t

    late = {}

    def turn_attended(b):
        cols = slice(b * T, (b + 1) * T)
        i, t = turn(ring, A[:], late["A"])
        act.wait(t, value_proj[b])
        ts = [act.done(nc.scalar.activation(Hh[:, c, cols], bank[i][:, c * T:(c + 1) * T], ACT.Identity,
                                            bias=V("v2_b", c))) for c in range(C)]
        dve.wait(ts)
        ts = ts + [dve.done(nc.vector.scalar_tensor_tensor(
            out=Hl[:, c, cols], in0=bank[i][:, c * T:(c + 1) * T], scalar=V("v2_b", c),
            in1=Hh[:, c, cols].bitcast(F32), op0=ALU.add, op1=ALU.subtract)) for c in range(C)]
        ring.free[i] = ts
        late["AT"], late["A_turned"] = ts, t

    def project_out(b):
        nonlocal a_read
        cols = slice(b * T, (b + 1) * T)
        wo.need()
        i = ring.take()
        pe.wait(late["AT"])
        for c in range(C):
            m = mm3(bank[i][0:T, :], (Hh[:, c, cols], Hl[:, c, cols]), wo.block(c, 0, D), c == 0, c == C - 1)
        late["AT_read"] = t = pe.done(m)
        dve.wait(t, t_rows2, late["A_turned"])
        ring.free[i] = t = dve.done(nc.vector.tensor_tensor(A[:], bank[i][0:T, :], o_row[:], ALU.add))
        dve.wait(t)
        t = dve.done(nc.vector.tensor_tensor(A[:], A[:], X[:, b, :], ALU.add))
        dve.wait(t)
        t = dve.done(nc.vector.bn_stats(stats[:, b % 2, :], A[:]))
        dve.wait(t)
        t = dve.done(nc.vector.bn_aggr(mv[:, b % 2, :], stats[:, b % 2, :]))
        dve.wait(t)
        t = dve.done(nc.vector.scalar_tensor_tensor(out=mv[:, b % 2, 1:2], in0=mv[:, b % 2, 0:1], scalar=mv[:, b % 2, 0:1],
                                                    in1=mv[:, b % 2, 1:2], op0=ALU.mult, op1=ALU.add))
        t = inverse_root(1, mv[:, b % 2, 1:2], 1e-6, t)
        dve.wait(t)
        late["A"] = dve.done(nc.vector.tensor_scalar(A[:], A[:], rstd[:, 0, 0:1], None, ALU.mult))

    def turn_normed(b):
        nonlocal a_read
        cols = slice(b * T, (b + 1) * T)
        i, t = turn(ring, A[:], late["A"])
        a_read = t
        ts = []
        act.wait(t)
        for c in range(C):
            ts.append(act.done(nc.scalar.activation(q2[:, c, cols], bank[i][:, c * T:(c + 1) * T], ACT.Copy,
                                                    scale=V("post_w", c))))
        ring.free[i] = ts
        t_h2.append(split_sbuf(q2[:, :, cols], Hh[:, :, cols], Hl[:, :, cols], ts, [late["AT_read"]]))

    value_proj = {}
    split_context(0)
    latent_keys(0)
    for o in range(C):
        keys(0, o)
    for j in range(4):
        values(0, j)
    value_proj[0] = pe.last()
    queries(0)
    for b in range(B):
        n, p = b + 1, b - 1
        nxt, prv = n < B, p >= 0
        if nxt:
            split_context(n)
        if prv:
            late["A"] = divide(p)
        logits(b, 0)
        if prv:
            turn_attended(p)
        if nxt:
            values(n, 0)
            values(n, 1)
        block(b, 0)
        logits(b, 1)
        if prv:
            project_out(p)
        if nxt:
            keys(n, 0)
            values(n, 2)
        block(b, 1)
        logits(b, 2)
        if nxt:
            keys(n, 1)
            values(n, 3)
            value_proj[n] = pe.last()
        feed_weights()
        if prv:
            turn_normed(p)
        block(b, 2)
        logits(b, 3)
        if nxt:
            keys(n, 2)
            latent_keys(n)
            keys(n, 3)
            queries(n)
            if n == B - 1:
                wq.give_up()
                wk.give_up()
                wv.give_up()
        feed_weights()
        block(b, 3)
    late["A"] = divide(B - 1)
    turn_attended(B - 1)
    project_out(B - 1)
    turn_normed(B - 1)
    wo.give_up()

    new_phase()
    ring = Ring(list(range(8)))
    t_row = load_row("mlp_b2")
    dve.wait(t_row)
    t_x = [dve.done(nc.vector.tensor_tensor(X[:, b, :], X[:, b, :], row[:], ALU.add)) for b in range(B)]
    mlp("2", "mlp_b1", ACT.Gelu_apprx_tanh, t_h2, t_x)

    new_phase()
    ring = Ring(list(range(8)))
    ctx_raw = sb("ctx_raw3", [P, C, SP])
    ctx_n = sb("ctx_rows", [P, 2, 3, D])
    Qh = sb("Q_hi", [P, C, NT], F32R)
    Ql = sb("Q_lo", [P, C, NT], F32R)
    Rh = sb("QK_hi", [P, C, NT], F32R)
    Rl = sb("QK_lo", [P, C, NT], F32R)
    Pm = sb("probs3", [T, 2, SP])
    PT = sb("probs3_T", [P, 2, 3, T])
    A = sb("attended3", [T, 2, D])
    mxs = sb("max3", [T, B])
    nb = sb("minus_max3", [T, B])
    ssum = sb("sum3", [T, B])
    rsum = sb("inv_sum3", [T, B])
    O = [Z, row]
    ctx3_stream = Stream("ctx3_loaded")
    rows3 = [sem("rows3_0"), sem("rows3_1")]
    n_rows3 = [0, 0]
    t_ctx = ctx3_stream.start(ctx_raw[:], ctxT_in[0])

    def load_rows(b, after):
        s = b % 2
        sp.wait((rows3[s], n_rows3[s]) if n_rows3[s] else None, after)
        sp.eng.dma_start(ctx_n[:, s, 0:2, :], ctx_in[b, 0:2 * P].rearrange("(j p) d -> p j d", p=P)).then_inc(rows3[s], 16)
        sp.eng.dma_start(ctx_n[0:S - 2 * P, s, 2, :], ctx_in[b, 2 * P:S]).then_inc(rows3[s], 16)
        n_rows3[s] += 32
        return (rows3[s], n_rows3[s])

    t_rows = {0: load_rows(0, None), 1: load_rows(1, None)}
    t_h = []
    for b in range(B):
        i, t = turn(ring, X[:, b, :], None)
        cols = slice(b * T, (b + 1) * T)
        ts = split_psum(bank[i][:, 0:C * T].rearrange("p (c t) -> p c t", c=C), Hh[:, :, cols], Hl[:, :, cols], t)
        ring.free[i] = ts
        t_h.append(ts)

    def project3(w, src, dst, ready, free=()):
        w.need()
        out_t = []
        for half in range(2):
            cols = slice(half * HALF, (half + 1) * HALF)
            pe.wait(ready[half])
            ts_half = []
            for o in range(C):
                i = ring.take()
                for c in range(C):
                    m = mm3(bank[i][:, 0:HALF], w.block(c, o * P, P), (src[0][:, c, cols], src[1][:, c, cols]),
                            c == 0, c == C - 1)
                t = pe.done(m)
                ts = split_psum(bank[i][:, 0:HALF], dst[0][:, o, cols], dst[1][:, o, cols], t, free)
                ring.free[i] = ts
                ts_half.append(ts)
            out_t.append(ts_half)
        return out_t

    Hs, Qs, Rs = (Hh, Hl), (Qh, Ql), (Rh, Rl)
    wq, wk, wv, wo = (Weight(name) for name in ("e_q", "e_k", "e_v", "e_o"))
    t_q = project3(wq, Hs, Qs, [t_h[0:HB], t_h[HB:B]])
    wq_read = pe.last()
    t_qk = project3(wk, Qs, Rs, t_q)
    h_free = pe.last()
    wv.need()
    wo.need()
    cx = [(Wh[:, w.slot, :, 0:SP], Wl[:, w.slot, :, 0:SP]) for w in (wq, wk)]
    cx_read, p_read, pt_read, a_read = [wq_read, h_free], [None, None], [None, None], [None, None]
    t_cx, t_exp, t_rs, t_a, t_pc = {}, {}, {}, {}, {}

    def context(b):
        nonlocal t_ctx
        s = b % 2
        t_cx[b] = []
        for c in range(0, C, 2):
            t_cx[b] += split_sbuf(ctx_raw[:, c:c + 2], cx[s][0][:, c:c + 2], cx[s][1][:, c:c + 2], t_ctx, [cx_read[s]])
        if b + 1 < B:
            t_ctx = ctx3_stream.start(ctx_raw[:], ctxT_in[b + 1], t_cx[b])

    def scores(b):
        s, cols = b % 2, slice(b * T, (b + 1) * T)
        i = ring.take()
        pe.wait(t_cx[b], t_qk[b // HB])
        for c in range(C):
            m = mm3(bank[i][0:T, 0:SP], (Rh[:, c, cols], Rl[:, c, cols]), (cx[s][0][:, c, :], cx[s][1][:, c, :]),
                    c == 0, c == C - 1)
        cx_read[s] = t = pe.done(m)
        dve.wait(t)
        t = dve.done(nc.vector.tensor_reduce(mxs[:, b:b + 1], bank[i][0:T, 0:S], AX.X, ALU.max))
        dve.wait(t)
        t = dve.done(nc.vector.tensor_scalar(nb[:, b:b + 1], mxs[:, b:b + 1], -SCALE3, None, ALU.mult))
        act.wait(t, p_read[s])
        ring.free[i] = t_exp[b] = t = act.done(nc.scalar.activation(
            Pm[:, s, 0:S], bank[i][0:T, 0:S], ACT.Exp, bias=nb[:, b:b + 1], scale=SCALE3, accum_out=ssum[:, b:b + 1]))
        dve.wait(t)
        t_rs[b] = dve.done(nc.vector.reciprocal(rsum[:, b:b + 1], ssum[:, b:b + 1]))

    def attend(b):
        s = b % 2
        i = ring.take()
        pe.wait(t_exp[b])
        for j, (k0, kn) in enumerate(KTILES):
            kn = min(kn, S - k0)
            m = nc.tensor.transpose(bank[i][0:kn, j * T:(j + 1) * T], Pm[:, s, k0:k0 + kn], ident[0:T, 0:T])
        p_read[s] = t = pe.done(m)
        dve.wait(t, pt_read[s])
        ring.free[i] = t_pt = dve.done(nc.vector.tensor_copy(PT[:, s].rearrange("p j t -> p (j t)"), bank[i][:, 0:3 * T]))
        return t_pt

    def gather(b, t_pt):
        s = b % 2
        i = ring.take()
        pe.wait(t_pt, t_rows[b])
        for j, (k0, kn) in enumerate(KTILES):
            kn = min(kn, S - k0)
            m = nc.tensor.matmul(bank[i][0:T, :], PT[0:kn, s, j, :], ctx_n[0:kn, s, j, :], start=j == 0, stop=j == 2)
        pt_read[s] = t = pe.done(m)
        if b + 2 < B:
            t_rows[b + 2] = load_rows(b + 2, t)
        dve.wait(t, t_rs[b], a_read[s])
        ring.free[i] = t_a[b] = dve.done(nc.vector.tensor_scalar(A[:, s, :], bank[i][0:T, :], rsum[:, b:b + 1], None, ALU.mult))

    def gathered_turn(b):
        s, cols = b % 2, slice(b * T, (b + 1) * T)
        i, a_read[s] = turn(ring, A[:, s, :], t_a[b])
        ring.free[i] = t_pc[b] = split_psum(bank[i][:, 0:C * T].rearrange("p (c t) -> p c t", c=C), Hh[:, :, cols],
                                            Hl[:, :, cols], a_read[s], [h_free])

    t_pt = {}
    context(0)
    for b in range(B + 3):
        if b + 1 < B:
            context(b + 1)
        if b < B:
            scores(b)
        if 1 <= b <= B:
            t_pt[b - 1] = attend(b - 1)
        if 2 <= b <= B + 1:
            gather(b - 2, t_pt[b - 2])
        if 3 <= b:
            gathered_turn(b - 3)
    t_pc = [t_pc[b] for b in range(B)]
    q_free = pe.last()
    t_c = project3(wv, Hs, Qs, [t_pc[0:HB], t_pc[HB:B]], [q_free])
    out_sems = [sem("stored0"), sem("stored1")]
    stored = [0, 0]
    for b in range(B):
        i = ring.take()
        pe.wait(t_c[b // HB])
        for c in range(C):
            m = mm3(bank[i][0:T, :], (Qh[:, c, b * T:(b + 1) * T], Ql[:, c, b * T:(b + 1) * T]), wo.block(c, 0, D),
                    c == 0, c == C - 1)
        t = pe.done(m)
        s = b % 2
        dve.wait(t, (out_sems[s], stored[s]) if stored[s] else None)
        ring.free[i] = t = dve.done(nc.vector.scalar_tensor_tensor(
            out=O[s][:], in0=bank[i][0:T, :], scalar=V("alpha", 0, T), in1=X[:, b, :], op0=ALU.mult, op1=ALU.add))
        sp.wait(t)
        sp.eng.dma_start(out[b], O[s][:]).then_inc(out_sems[s], 16)
        stored[s] += 16
    for s in range(2):
        sp.wait((out_sems[s], stored[s]))
    while len(phase) > 1:
        phase.pop().close()
    stack.close()


def _chunked(w):
    return np.ascontiguousarray(w.reshape(C, P, w.shape[1]).transpose(1, 0, 2))


def kernel(**inputs):
    import concourse.bacc as _bacc
    from concourse.bass_utils import run_bass_kernel_spmd as _run

    i = {k: np.asarray(v) for k, v in inputs.items()}
    l0 = {k[9:]: v for k, v in i.items() if k.startswith("L0_")}
    l1 = {k[9:]: v for k, v in i.items() if k.startswith("L1_")}
    l2 = {k[9:]: v for k, v in i.items() if k.startswith("L2_")}
    l3 = {k[9:]: v for k, v in i.items() if k.startswith("L3_")}
    ctx = i["ctx_2048"]

    ctxT = np.zeros((B, D, SP), ctx.dtype)
    ctxT[:, :, :S] = ctx.transpose(0, 2, 1)
    ctxT = np.ascontiguousarray(ctxT.reshape(B, C, P, SP).transpose(0, 2, 1, 3))
    prev = np.ascontiguousarray(ctx[:, 0:2].reshape(B, 2, C, P).transpose(3, 1, 2, 0))
    s0 = ctx[:, 2:2 + S0].reshape(B, C, 8, S0, S0).transpose(2, 3, 1, 4, 0).reshape(P, C, S0, B)
    mask = np.zeros((B, SP), i["mask_BxS2_ik0"].dtype)
    mask[:, :S] = i["mask_BxS2_ik0"]
    mask = np.repeat(mask[:, None, :], T, 1)

    blocks = {"k": l0["Wk"].T, "r": l0["Wr"].T, "v": l0["Wv"].T, "g": l0["Wg"].T, "o": l0["Wo"].T,
              "fr": l0["ffn_Wr"].T, "fk": l0["ffn_Wk"].T, "fv": l0["ffn_Wv"].T,
              "p_q": l2["q_w"], "p_k": l2["kv_w"][:, 0::2], "p_v": l2["kv_w"][:, 1::2], "p_o": l2["out_w"],
              "e_q": l3["w_q"].T, "e_k": l3["w_k"], "e_v": l3["w_v"].T, "e_o": l3["w_o"].T}
    for g in range(4):
        at = slice(g * D, (g + 1) * D)
        for layer in (1, 2):
            for w in "qkv":
                blocks[f"{w}{layer}_{g}"] = l1[f"w{w}{layer}"][:, at]
            blocks[f"o{layer}_{g}"] = l1[f"wo{layer}"][at]
        blocks[f"m1a_{g}"], blocks[f"m1b_{g}"] = l1["w_fc1"][:, at], l1["w_fc2"][at]
        blocks[f"m2a_{g}"], blocks[f"m2b_{g}"] = l2["mlp_w1"][:, at], l2["mlp_w2"][at]
    weights = np.stack([_chunked(blocks[n]) for n in UNIQUE])

    vectors = {"ln1_w": l0["ln1_w"], "ln1_b": l0["ln1_b"], "maa_x": l0["maa_x"], "time_decay": l0["time_decay"],
               "u": l0["faaaa"].reshape(-1), "gn_w": l0["gn_w"], "gn_b": l0["gn_b"], "ln2_w": l0["ln2_w"],
               "ln2_b": l0["ln2_b"], "ffn_maa_k": l0["ffn_maa_k"], "ffn_maa_r": l0["ffn_maa_r"],
               "a1_s": l1["ln1_scale"], "a1_o": l1["ln1_offset"], "a2_s": l1["ln2_scale"], "a2_o": l1["ln2_offset"],
               "am_s": l1["ln_mlp_scale"], "am_o": l1["ln_mlp_offset"], "post_w": l2["postnorm_w"],
               "q2_b": l2["q_b"], "k2_b": l2["kv_b"][0::2], "v2_b": l2["kv_b"][1::2], "alpha": np.repeat(l3["alpha"].reshape(1), P),
               "bq1": l1["bq1"], "bk1": l1["bk1"], "bq2": l1["bq2"], "bk2": l1["bk2"],
               "bias_k1": l1["bias_k1"].reshape(-1), "bias_k2": l1["bias_k2"].reshape(-1),
               "b_fc1": l1["b_fc1"], "mlp_b1": l2["mlp_b1"]}
    for j in range(5):
        vectors[f"maa_{j}"] = l0["maa_stack"][j]
    vec = np.ascontiguousarray(np.concatenate([vectors[n].reshape(w, P) for n, w in VECTORS]).T)
    rows = {"bo1": l1["bo1"], "bo2": l1["bo2"], "b_fc2": l1["b_fc2"],
            "out_b": l2["out_b"], "mlp_b2": l2["mlp_b2"]}
    rows = np.stack([np.repeat(rows[n][None], T, 0) for n in ROWS])
    bv = []
    for layer in (1, 2):
        for g in range(G):
            both = np.repeat(l1[f"bv{layer}"][None, None, g * D:(g + 1) * D], P, 0).repeat(2, 1)
            both[S - 2 * P, 1] = l1[f"bias_v{layer}"].reshape(-1)[g * D:(g + 1) * D]
            bv.append(both)
    bv = np.stack(bv)

    lane = np.arange(P)
    ident = np.eye(P, dtype=np.float32)
    heads = (lane[:, None] // S0 == lane[None, :] // S0).astype(np.float32)
    place = np.zeros((P, P + S0 - 1), np.float32)
    place[lane, S0 - 1 + S0 * (lane // S0)] = 1.0
    pick = (lane[:, None] % S0 == np.arange(S0)[None, :]).astype(np.float32)

    arrays = {"x": i["x"], "ctx": ctx, "ctxT": ctxT, "prev": prev, "s0": s0, "mask": mask, "weights": weights,
              "vec": vec, "rows": rows, "bv": bv, "maa_w1": _chunked(l0["maa_w1"]),
              "maa_w2": l0["maa_w2"].reshape(5 * 32, D), "dec_w1": _chunked(l0["decay_w1"]), "dec_w2": l0["decay_w2"],
              "ident": ident, "heads": heads, "place": place, "pick": pick}
    nc = _bacc.Bacc("TRN2", target_bir_lowering=False, num_devices=1)
    feeds, args = {}, []
    for name, a in arrays.items():
        a = np.ascontiguousarray(a)
        feeds[f"in_{name}"] = a
        args.append(nc.dram_tensor(f"in_{name}", a.shape, mybir.dt.from_np(a.dtype), kind="ExternalInput").ap())
    args.append(nc.dram_tensor("out_y", (B, T, D), F32, kind="ExternalOutput").ap())
    build(nc, *args)
    r = _run(nc, [feeds], core_ids=[0])
    return r.results[0]["out_y"]
```

```python
from contextlib import ExitStack

import numpy as np

import concourse.bass as bass
from concourse import mybir

F32 = mybir.dt.float32
F32R = mybir.dt.float32r
I32 = mybir.dt.int32
ACT = mybir.ActivationFunctionType
ALU = mybir.AluOpType
AX = mybir.AxisListType

P = 128
B, T, D = 8, 112, 512
S = 375
SP = S + 1
C = D // P
NT = B * T
HALF = NT // 2
HB = B // 2
S0 = 16
HK, G = 4, 4
KTILES = [(0, 128), (128, 128), (256, SP - 256)]
KTILES2 = KTILES + [(SP, T)]
SK2 = SP + T
H2, D2 = 16, 32
GAP = -1.0e30
SCALE1 = 128.0 ** -0.5
SCALE2 = 1.0 / D2
SCALE3 = float(D) ** -0.5

VECTORS = [
    ("ln1_w", 4), ("ln1_b", 4), ("maa_x", 4), ("maa_0", 4), ("maa_1", 4), ("maa_2", 4), ("maa_3", 4),
    ("maa_4", 4), ("time_decay", 4), ("u", 4), ("gn_w", 4), ("gn_b", 4), ("ln2_w", 4), ("ln2_b", 4),
    ("ffn_maa_k", 4), ("ffn_maa_r", 4),
    ("a1_s", 4), ("a1_o", 4), ("a2_s", 4), ("a2_o", 4), ("am_s", 4), ("am_o", 4), ("post_w", 4),
    ("q2_b", 4), ("k2_b", 4), ("v2_b", 4), ("alpha", 1),
    ("bq1", 16), ("bk1", 16), ("bq2", 16), ("bk2", 16), ("bias_k1", 16), ("bias_k2", 16),
    ("b_fc1", 16), ("mlp_b1", 16),
]
VEC_AT, _n = {}, 0
for _name, _w in VECTORS:
    VEC_AT[_name] = (_n, _w)
    _n += _w
NVEC = _n

ROWS = ["bo1", "bo2", "b_fc2", "out_b", "mlp_b2"]

UNIQUE = (["k", "r", "v", "g", "o", "fr", "fk", "fv"]
          + [f"{w}{layer}_{g}" for layer in (1, 2) for g in range(G) for w in "qkvo"]
          + [f"m1{w}_{g}" for g in range(4) for w in "ab"]
          + ["p_q", "p_k", "p_v", "p_o"]
          + [f"m2{w}_{g}" for g in range(4) for w in "ab"]
          + ["e_q", "e_k", "e_v", "e_o"])
ORDER = ["k", "r", "v", "g", "o"] + UNIQUE
NSLOT = 4


def build(nc, x_in, ctx_in, ctxT_in, prev_in, s0_in, mask_in, w_in, vec_in, rows_in, bv_in,
          maa_w1_in, maa_w2_in, dec_w1_in, dec_w2_in, ident_in, heads_in, place_in, pick_in_dram, out):
    stack = ExitStack()
    phase = [stack.enter_context(ExitStack())]

    def sem(name):
        return stack.enter_context(nc.semaphore(name))

    class Engine:

        def __init__(self, eng, name):
            self.eng, self.sem, self.count, self.seen = eng, sem(name), 0, {}

        def wait(self, *tokens):
            for token in tokens:
                if token is None:
                    continue
                if isinstance(token, list):
                    self.wait(*token)
                    continue
                s, n = token
                if self.seen.get(s.name, 0) < n:
                    self.eng.wait_ge(s, n)
                    self.seen[s.name] = n

        def done(self, instruction):
            self.count += 1
            instruction.then_inc(self.sem, 1)
            return (self.sem, self.count)

        def last(self):
            return (self.sem, self.count) if self.count else None

    pe = Engine(nc.tensor, "pe_done")
    act = Engine(nc.scalar, "act_done")
    dve = Engine(nc.vector, "dve_done")
    pool = Engine(nc.gpsimd, "pool_done")
    sp = Engine(nc.sync, "sp_unused")

    class Stream:

        def __init__(self, name):
            self.sem, self.count = sem(name), 0

        def start(self, dst, src, *after):
            sp.wait((self.sem, self.count) if self.count else None, *after)
            sp.eng.dma_start(dst, src).then_inc(self.sem, 16)
            self.count += 16
            return (self.sem, self.count)

    def sb(name, shape, dt=F32):
        return phase[-1].enter_context(nc.sbuf_tensor(name, shape, dt))

    def new_phase(levels=1):
        tokens = [e.last() for e in (pe, act, dve, pool)]
        for e in (pe, act, dve, pool, sp):
            e.wait(*tokens)
        for _ in range(levels):
            phase.pop().close()
        phase.append(ExitStack())
        stack.enter_context(phase[-1])

    Wh = sb("W_hi", [P, NSLOT, C, D], F32R)
    Wl = sb("W_lo", [P, NSLOT, C, D], F32R)
    Wraw = sb("W_raw", [P, C, D])
    X = sb("residual", [T, B, D])
    Hh = sb("act_hi", [P, C, NT], F32R)
    Hl = sb("act_lo", [P, C, NT], F32R)
    vec = sb("vectors", [P, NVEC])
    ident = sb("ident", [P, P])
    stats = sb("stats", [T, HB, 6])
    mv = sb("mean_var", [T, HB, 2])
    rstd = sb("rstd", [T, HB, 2])
    minus_half = sb("minus_half", [T, HB])
    Z = sb("normalised", [T, D])
    row = sb("bias_row", [T, D])
    bank = [stack.enter_context(nc.psum_tensor(f"bank{i}", [P, 512], F32)) for i in range(8)]

    def V(name, i, n=P):
        return vec[0:n, VEC_AT[name][0] + i:VEC_AT[name][0] + i + 1]

    class Ring:

        def __init__(self, banks):
            self.banks, self.free, self.at = banks, {b: None for b in banks}, 0

        def take(self):
            i = self.banks[self.at % len(self.banks)]
            self.at += 1
            assert self.free[i] != "taken"
            pe.wait(self.free[i])
            self.free[i] = "taken"
            return i

    const = sem("const")
    x_loaded = [sem("x_loaded0"), sem("x_loaded1")]
    for dst, src, s in ((X[:, 0:HB], x_in[0:HB].rearrange("b t d -> t b d"), x_loaded[0]), (vec[:], vec_in, const),
                        (ident[:], ident_in, const)):
        nc.sync.dma_start(dst, src).then_inc(s, 16)
    constants = (const, 32)
    zeroed = [dve.done(nc.vector.memset(bank[i][:], 0.0)) for i in range(8)]
    t_mh = dve.done(nc.vector.memset(minus_half[:], -0.5))
    for e in (pe, act, dve, pool):
        e.wait(constants, t_mh)
    pe.wait(zeroed)
    act.wait(zeroed)

    w_stream = Stream("w_loaded")
    w_state = {"staged": 0, "split": 0, "raw_free": None, "loaded": None}
    w_ready = {}
    w_free = {}

    def stage_next_weight():
        n = w_state["staged"]
        if n < len(ORDER):
            w_state["loaded"] = w_stream.start(Wraw[:], w_in[UNIQUE.index(ORDER[n])], w_state["raw_free"])
            w_state["staged"] += 1

    def feed_weights():
        n = w_state["split"]
        if n == len(ORDER) or n >= NSLOT and (n - NSLOT) not in w_free:
            return
        slot, free = n % NSLOT, w_free.get(n - NSLOT)
        act.wait(w_state["loaded"], free)
        his, los = [], []
        for c in range(0, C, 2):
            his.append(act.done(nc.scalar.copy(Wh[:, slot, c:c + 2, :], Wraw[:, c:c + 2, :])))
        pool.wait(w_state["loaded"], free)
        for i, c in enumerate(range(0, C, 2)):
            pool.wait(his[i])
            los.append(pool.done(nc.gpsimd.tensor_tensor(
                Wl[:, slot, c:c + 2, :], Wraw[:, c:c + 2, :], Wh[:, slot, c:c + 2, :].bitcast(F32),
                ALU.subtract)))
        w_ready[n] = his + los
        w_state["raw_free"] = his + los
        w_state["split"] += 1
        stage_next_weight()

    w_state["use"] = 0

    class Weight:

        def __init__(self, name):
            self.n = w_state["use"]
            assert ORDER[self.n] == name, (ORDER[self.n], name)
            w_state["use"] += 1
            self.slot = self.n % NSLOT

        def need(self):
            while w_state["split"] <= self.n:
                feed_weights()
            pe.wait(w_ready[self.n])

        def block(self, c, a, n):
            return Wh[:, self.slot, c, a:a + n], Wl[:, self.slot, c, a:a + n]

        def give_up(self):
            w_free[self.n] = [pe.last()]

    def mm3(dst, left, right, first, last):
        nc.tensor.matmul(dst, left[0], right[0], start=first, stop=False)
        nc.tensor.matmul(dst, left[0], right[1], start=False, stop=False)
        return nc.tensor.matmul(dst, left[1], right[0], start=False, stop=last)

    def split_psum(src, hi, lo, ready, free=(), bias=None):
        act.wait(ready, *free)
        if bias is None:
            t_hi = act.done(nc.scalar.copy(hi, src))
        else:
            t_hi = act.done(nc.scalar.activation(hi, src, ACT.Identity, bias=bias))
        dve.wait(ready, t_hi, *free)
        if bias is None:
            t_lo = dve.done(nc.vector.tensor_tensor(lo, src, hi.bitcast(F32), ALU.subtract))
        else:
            t_lo = dve.done(nc.vector.scalar_tensor_tensor(
                out=lo, in0=src, scalar=bias, in1=hi.bitcast(F32), op0=ALU.add, op1=ALU.subtract))
        return [t_hi, t_lo]

    def split_sbuf(src, hi, lo, ready, free=()):
        act.wait(ready, *free)
        t_hi = act.done(nc.scalar.copy(hi, src))
        pool.wait(ready, t_hi, *free)
        t_lo = pool.done(nc.gpsimd.tensor_tensor(lo, src, hi.bitcast(F32), ALU.subtract))
        return [t_hi, t_lo]

    def inverse_root(n, src, eps, ready):
        dve.wait(ready)
        t = dve.done(nc.vector.tensor_scalar(rstd[:, 0:n, 1], src, eps, None, ALU.add))
        pool.wait(t)
        return pool.done(nc.gpsimd.tensor_tensor(rstd[:, 0:n, 0], rstd[:, 0:n, 1], minus_half[:, 0:n], ALU.pow))

    def moments(srcs, ready):
        for k, src in enumerate(srcs):
            dve.wait(ready[k])
            t = dve.done(nc.vector.bn_stats(stats[:, k, :], src))
        for k, src in enumerate(srcs):
            dve.wait(t)
            t = dve.done(nc.vector.bn_aggr(mv[:, k, :], stats[:, k, :]))
        return inverse_root(len(srcs), mv[:, 0:len(srcs), 1], 1e-5, t)

    def turn(ring, z, ready):
        i = ring.take()
        pe.wait(ready)
        for c in range(C):
            m = nc.tensor.transpose(bank[i][:, c * T:(c + 1) * T], z[:, c * P:(c + 1) * P], ident[0:T, 0:T])
        return i, pe.done(m)

    z_read = [None, None]

    def norm_steps(ring, b, scale, offset, ready, h_free, t_row, out, z=Z, zn=0):
        got = {}

        def start():
            t = moments([X[:, b, :]], [ready()])
            dve.wait(t, z_read[zn])
            got["z"] = dve.done(nc.vector.tensor_scalar(z[:], X[:, b, :], mv[:, 0, 0:1], rstd[:, 0, 0:1],
                                                        ALU.subtract, ALU.mult))
            pool.wait(t_row, got["z"])
            got["x"] = pool.done(nc.gpsimd.tensor_tensor(X[:, b, :], X[:, b, :], row[:], ALU.add))

        def finish():
            i, t = turn(ring, z[:], got["z"])
            z_read[zn] = t
            act.wait(t)
            ts = []
            for c in range(C):
                at = bank[i][:, c * T:(c + 1) * T]
                ts.append(act.done(nc.scalar.activation(at, at, ACT.Identity, scale=V(scale, c), bias=V(offset, c))))
            cols = slice(b * T, (b + 1) * T)
            ts = split_psum(bank[i][:, 0:C * T].rearrange("p (c t) -> p c t", c=C), Hh[:, :, cols], Hl[:, :, cols],
                            ts, [h_free])
            ring.free[i] = ts
            out[b] = ts, got["x"]

        return [start, finish]

    def begin(step, active):
        g = step()
        if g is not None and next(g, "over") != "over":
            active.append(g)

    def advance(active):
        for g in list(active):
            if next(g, "over") == "over":
                active.remove(g)

    def run(step):
        for _ in step() or ():
            pass

    row_stream = Stream("row_loaded")

    def load_row(name, *after):
        return row_stream.start(row[:], rows_in[ROWS.index(name)], *after)

    phase.append(ExitStack())
    stack.enter_context(phase[-1])
    ring = Ring([0, 1, 2, 3, 4, 5])
    y_banks = [6, 7]
    xn = sb("xn", [P, C, HB, T + 1])
    sx = sb("sx", [P, C, HB, T])
    prev = sb("prev", [P, 2, C, B])
    phase.append(ExitStack())
    stack.enter_context(phase[-1])
    tmp = sb("tmp", [P, 2, HB, T + 1])
    mx = sb("mx", [P, 2, HB, T])
    x5 = sb("x5", [P, 2, HB, T])
    th = sb("th", [P, HALF])
    th4 = sb("th4", [32, HALF])
    thd = sb("thd", [64, HALF])
    kT = sb("kT", [P, C, HB, T])
    rT = sb("rT", [P, C, HB, T])
    wT = sb("wT", [P, C, HB, T + 1])
    att = sb("att", [P, C, HB, T])
    ab2 = sb("kv_then_state", [P, 2, HB, T + 1])
    yb2 = sb("y", [P, 2, HB, T])
    s0 = sb("s0", [P, C, S0, B])
    maa_w1 = sb("maa_w1", [P, C, 160])
    maa_w2 = sb("maa_w2", [P, D])
    maa_w24 = sb("maa_w24", [32, D])
    dec_w1 = sb("dec_w1", [P, C, 64])
    dec_w2 = sb("dec_w2", [64, D])
    heads = sb("heads", [P, P])
    place = sb("place", [P, P + S0 - 1])
    pick_in = sb("pick_row", [P, S0])
    pick = sb("pick", [P, S0, P], F32R)
    AB = [ab2[:, 0], ab2[:, 1], tmp[:, 0], tmp[:, 1]]
    YB = [yb2[:, 0], yb2[:, 1], x5[:, 0], x5[:, 1]]
    NB = 4

    def load_constants(name, queue, *pairs):
        done = sem(name)
        for dst, src in pairs:
            queue.dma_start(dst, src).then_inc(done, 16)
        return (done, 16 * len(pairs))

    mix_consts = load_constants("mix_constants", nc.scalar, (prev[:], prev_in), (maa_w1[:], maa_w1_in), (maa_w2[:], maa_w2_in[0:P]),
                                (maa_w24[:], maa_w2_in[P:P + 32]))
    decay_consts = load_constants("decay_constants", nc.sync, (dec_w1[:], dec_w1_in), (dec_w2[:], dec_w2_in))
    stage_next_weight()
    rec_consts = load_constants("recurrence_constants", nc.sync, (heads[:], heads_in), (place[:], place_in),
                                (pick_in[:], pick_in_dram), (s0[:], s0_in))
    nc.sync.dma_start(X[:, HB:B], x_in[HB:B].rearrange("b t d -> t b d")).then_inc(x_loaded[1], 16)

    def flat(ap):
        return ap.rearrange("p b t -> p (b t)")

    def by_batch(ap):
        return ap.rearrange("p (b t) -> p b t", b=HB)

    Xs = [([Hh[:, c, k * HALF:(k + 1) * HALF] for c in range(C)], [Hl[:, c, k * HALF:(k + 1) * HALF] for c in range(C)])
          for k in range(2)]
    xs_read = [None, None]
    vh, vl = Xs[0]
    last_mix = None
    scratch = {f"{name}{s}": tile[:, s, :, 0:T] for name, tile in (("tmp", tmp), ("x5", x5), ("mx", mx)) for s in range(2)}
    scratch_read = {name: None for name in scratch}
    t_prep = {}

    def norm_shift(half, got, ln, row0, x_ready):
        b0 = half * HB
        t_xn, t_sx = got["xn"], got["sx"] = [], []

        def first():
            got["root"] = moments([X[:, b0 + k, :] for k in range(HB)], x_ready)

        def norm(k):
            dve.wait(got["root"], z_read[0])
            t = dve.done(nc.vector.tensor_scalar(Z[:], X[:, b0 + k, :], mv[:, k, 0:1], rstd[:, k, 0:1],
                                                 ALU.subtract, ALU.mult))
            yield
            i, z_read[0] = turn(ring, Z[:], t)
            act.wait(z_read[0], last_mix)
            ts = [act.done(nc.scalar.activation(xn[:, c, k, 1:T + 1], bank[i][:, c * T:(c + 1) * T], ACT.Identity,
                                                scale=V(ln + "_w", c), bias=V(ln + "_b", c))) for c in range(C)]
            ring.free[i] = ts
            t_xn.extend(ts)

        def shift():
            act.wait(mix_consts, last_mix)
            t_xn.append(act.done(nc.scalar.copy(xn[:, :, :, 0], prev[:, row0, :, b0:b0 + HB])))
            pool.wait(t_xn, last_mix)
            for c in range(C):
                t_sx.append(pool.done(nc.gpsimd.tensor_tensor(sx[:, c], xn[:, c, :, 0:T], xn[:, c, :, 1:T + 1],
                                                              ALU.subtract)))

        return [first, lambda: norm(0), lambda: norm(1), lambda: norm(2), lambda: norm(3), shift]

    def prepare(half):
        got = t_prep[half] = {}
        steps = norm_shift(half, got, "ln1", 1, [(x_loaded[half], 16)] * HB)
        t_xn, t_sx = got["xn"], got["sx"]

        def low_rank():
            i1, i2 = ring.take(), ring.take()
            pe.wait(mix_consts)
            for c in range(C):
                dve.wait(t_xn, t_sx[c], scratch_read[f"mx{c % 2}"])
                t = dve.done(nc.vector.scalar_tensor_tensor(out=mx[:, c % 2], in0=sx[:, c], scalar=V("maa_x", c),
                                                            in1=xn[:, c, :, 1:T + 1], op0=ALU.mult, op1=ALU.add))
                pe.wait(t)
                nc.tensor.matmul(bank[i1][:, 0:HALF], maa_w1[:, c, 0:P], flat(mx[:, c % 2]), start=c == 0, stop=c == C - 1)
                scratch_read[f"mx{c % 2}"] = pe.done(nc.tensor.matmul(
                    bank[i2][0:32, 0:HALF], maa_w1[:, c, P:160], flat(mx[:, c % 2]), start=c == 0, stop=c == C - 1))
            act.wait(scratch_read["mx1"], last_mix)
            got["th"] = [act.done(nc.scalar.activation(th[:], bank[i1][:, 0:HALF], ACT.Tanh)),
                         act.done(nc.scalar.activation(th4[:], bank[i2][0:32, 0:HALF], ACT.Tanh))]
            ring.free[i1] = ring.free[i2] = got["th"]

        return steps + [low_rank]

    def mixed_chunk(half, j, k, c, a, b, out_t):
        got = t_prep[half]
        pe.wait(got["th"])
        i = ring.take()
        if j < 4:
            left, right = maa_w2[32 * j:32 * j + 32, c * P:(c + 1) * P], th[32 * j:32 * j + 32, :]
        else:
            left, right = maa_w24[:, c * P:(c + 1) * P], th4[:]
        t = pe.done(nc.tensor.matmul(bank[i][:, 0:HALF], left, right, start=True, stop=True))
        yield
        dve.wait(t, scratch_read[a], got["sx"])
        t = dve.done(nc.vector.scalar_tensor_tensor(
            out=scratch[a], in0=by_batch(bank[i][:, 0:HALF]), scalar=V(f"maa_{j}", c), in1=sx[:, c], op0=ALU.add,
            op1=ALU.mult))
        ring.free[i] = t
        dve.wait(t, scratch_read[b], got["xn"])
        scratch_read[a] = t = dve.done(nc.vector.tensor_tensor(scratch[b], scratch[a], xn[:, c, :, 1:T + 1], ALU.add))
        yield
        scratch_read[b] = t = split_sbuf(flat(scratch[b]), Xs[k][0][c], Xs[k][1][c], t, [xs_read[k]])
        out_t.append(t)

    def mixed(half, j, k):
        out_t = []
        for c in range(C):
            run(lambda: mixed_chunk(half, j, k, c, f"tmp{c % 2}", f"x5{c % 2}", out_t))
        return out_t

    def project_block(weight, o, k, t_in):
        i = ring.take()
        for c in range(C):
            pe.wait(t_in[c])
            m = mm3(bank[i][:, 0:HALF], weight.block(c, o * P, P), (Xs[k][0][c], Xs[k][1][c]), c == 0, c == C - 1)
        xs_read[k] = t = pe.done(m)
        return i, t

    first_steps = prepare(0)
    first_steps[0]()
    feed_weights()
    for f in first_steps[1:]:
        run(f)
    dve.wait(rec_consts)
    t_pick_made = [dve.done(nc.vector.tensor_scalar(pick[:, d, :], heads[:], pick_in[:, d:d + 1], None, ALU.mult))
                   for d in range(S0)]
    t_w0 = dve.done(nc.vector.memset(wT[:, :, :, 0:1], 0.0))
    act.wait(rec_consts)
    pe.wait(decay_consts, rec_consts)
    ab_free, yb_free = [None] * NB, [None] * NB
    t_x0 = []
    ffn_got = [{}, {}]
    att_read = None

    for half in range(2):
        b0 = half * HB
        t_in1 = mixed(half, 1, 0)
        feed_weights()
        t_in0 = mixed(half, 0, 1)
        i = ring.take()
        for c in range(C):
            pe.wait(t_in1[c])
            nc.tensor.matmul(bank[i][0:64, 0:HALF], dec_w1[:, c, :], Xs[0][0][c].bitcast(F32), start=c == 0, stop=False)
            m = nc.tensor.matmul(bank[i][0:64, 0:HALF], dec_w1[:, c, :], Xs[0][1][c].bitcast(F32), start=False, stop=c == C - 1)
        xs_read[0] = t = pe.done(m)
        act.wait(t)
        ring.free[i] = t_thd = act.done(nc.scalar.activation(thd[:], bank[i][0:64, 0:HALF], ACT.Tanh))
        t_in3 = mixed(half, 3, 0)
        feed_weights()
        pe.wait(t_thd)
        t_w = []
        for c in range(C):
            i = ring.take()
            t = pe.done(nc.tensor.matmul(bank[i][:, 0:HALF], dec_w2[:, c * P:(c + 1) * P], thd[:], start=True, stop=True))
            act.wait(t, t_w0)
            inner = wT[:, c, :, 1:T + 1]
            ring.free[i] = t = act.done(nc.scalar.activation(
                inner, by_batch(bank[i][:, 0:HALF]), ACT.Exp, bias=V("time_decay", c)))
            act.wait(t)
            t_w.append(act.done(nc.scalar.activation(inner, inner, ACT.Exp, scale=-1.0)))

        t_k, t_r, t_v = [], [], []
        wk = Weight("k")
        wk.need()
        for o in range(C):
            i, t = project_block(wk, o, 1, t_in0)
            act.wait(t)
            ring.free[i] = t = act.done(nc.scalar.copy(flat(kT[:, o]), bank[i][:, 0:HALF]))
            t_k.append(t)
        wk.give_up()
        feed_weights()
        t_in2 = mixed(half, 2, 1)
        wr = Weight("r")
        wr.need()
        for o in range(C):
            i, t = project_block(wr, o, 0, t_in3)
            act.wait(t)
            ring.free[i] = t = act.done(nc.scalar.copy(flat(rT[:, o]), bank[i][:, 0:HALF]))
            t_r.append(t)
        wr.give_up()
        feed_weights()
        wv = Weight("v")
        wv.need()
        for o in range(C):
            i, t = project_block(wv, o, 1, t_in2)
            ts = split_psum(bank[i][:, 0:HALF], vh[o], vl[o], t, [xs_read[0]])
            ring.free[i] = ts
            t_v.append(ts)
        wv.give_up()
        feed_weights()
        ab_free[2:4] = scratch_read["tmp0"], scratch_read["tmp1"]
        yb_free[2:4] = scratch_read["x50"], scratch_read["x51"]

        wg = Weight("g")
        sums = []
        t_att, t_in4, t_gn = {}, [], []
        t_c, t_g = {}, {}
        t_kv_of, t_y_of = {}, {}
        steps = [(o, d) for o in range(C) for d in range(S0)]
        picked = {}

        def spread(n):
            if n < len(steps):
                o, d = steps[n]
                i = pick_ring.take()
                pe.wait(t_v[o], t_pick_made)
                nc.tensor.matmul(bank[i][:, 0:HALF], pick[:, d, :], vh[o], start=True, stop=False)
                picked[n] = i, pe.done(nc.tensor.matmul(bank[i][:, 0:HALF], pick[:, d, :], vl[o], start=False, stop=True))

        def sum_rows(n, t):
            o, d = steps[n]
            j = y_banks[o % 2]
            pe.wait(t)
            if d == 0:
                pe.wait(ring.free.get(j))
            yb_free[n % NB] = t = pe.done(nc.tensor.matmul(
                bank[j][:, 0:HALF], place[:, S0 - 1 - d:S0 - 1 - d + P], flat(YB[n % NB]),
                start=d == 0, stop=d == S0 - 1))
            if d == S0 - 1:
                yield
                dve.wait(t, t_att[o])
                ring.free[j] = t_att[o] = dve.done(nc.vector.tensor_tensor(
                    flat(att[:, o]), bank[j][:, 0:HALF], flat(att[:, o]), ALU.add))

        def bonus(o):
            dve.wait(t_k[o], t_r[o], t_v[o], scratch_read["mx0"], att_read)
            t = dve.done(nc.vector.scalar_tensor_tensor(out=mx[:, 0], in0=rT[:, o], scalar=V("u", o), in1=kT[:, o],
                                                        op0=ALU.mult, op1=ALU.mult))
            yield
            i = ring.take()
            pe.wait(t)
            scratch_read["mx0"] = t = pe.done(nc.tensor.matmul(bank[i][:, 0:HALF], heads[:], flat(mx[:, 0]), start=True, stop=True))
            yield
            dve.wait(t, scratch_read["mx1"])
            t1 = dve.done(nc.vector.tensor_tensor(flat(att[:, o]), bank[i][:, 0:HALF], vh[o].bitcast(F32), ALU.mult))
            ring.free[i] = t2 = dve.done(nc.vector.tensor_tensor(flat(mx[:, 1]), bank[i][:, 0:HALF], vl[o].bitcast(F32), ALU.mult))
            dve.wait(t1, t2)
            scratch_read["mx1"] = t_att[o] = dve.done(nc.vector.tensor_tensor(flat(att[:, o]), flat(att[:, o]), flat(mx[:, 1]), ALU.add))

        def gate(o, c):
            if c == 0:
                wg.need()
            pe.wait(t_in4[c])
            t = pe.done(mm3(bank[gate_bank][:, 0:HALF], wg.block(c, o * P, P), (Xs[1][0][c], Xs[1][1][c]), c == 0, c == C - 1))
            if c == C - 1:
                xs_read[1] = t
                act.wait(t, t_kv_of[o])
                t_g[o] = act.done(nc.scalar.activation(flat(kT[:, o]), bank[gate_bank][:, 0:HALF], ACT.Silu))
                pe.wait(t_g[o])

        def centre(o):
            i = ring.take()
            pe.wait(t_att[o])
            t = pe.done(nc.tensor.matmul(bank[i][:, 0:HALF], heads[:], flat(att[:, o]), start=True, stop=True))
            yield
            dve.wait(t)
            ring.free[i] = t_c[o] = dve.done(nc.vector.scalar_tensor_tensor(
                out=flat(att[:, o]), in0=bank[i][:, 0:HALF], scalar=-1.0 / S0, in1=flat(att[:, o]),
                op0=ALU.mult, op1=ALU.add))

        def variance(o):
            act.wait(t_c[o], scratch_read["mx0"])
            t = act.done(nc.scalar.activation(flat(mx[:, 0]), flat(att[:, o]), ACT.Square))
            yield
            i = ring.take()
            pe.wait(t)
            scratch_read["mx0"] = t = pe.done(nc.tensor.matmul(bank[i][:, 0:HALF], heads[:], flat(mx[:, 0]), start=True, stop=True))
            yield
            dve.wait(t, t_y_of[o])
            ring.free[i] = t_c[o] = dve.done(nc.vector.tensor_scalar(flat(rT[:, o]), bank[i][:, 0:HALF], 1.0 / S0, 1e-5,
                                                                     ALU.mult, ALU.add))

        def finish(o):
            act.wait(t_c[o])
            t = act.done(nc.scalar.activation(flat(rT[:, o]), flat(rT[:, o]), ACT.Sqrt))
            yield
            dve.wait(t)
            t = dve.done(nc.vector.reciprocal(flat(rT[:, o]), flat(rT[:, o])))
            dve.wait(t)
            t = dve.done(nc.vector.scalar_tensor_tensor(out=flat(att[:, o]), in0=flat(att[:, o]), scalar=V("gn_w", o),
                                                        in1=flat(rT[:, o]), op0=ALU.mult, op1=ALU.mult))
            yield
            dve.wait(t, t_g[o])
            t = dve.done(nc.vector.scalar_tensor_tensor(out=flat(att[:, o]), in0=flat(att[:, o]), scalar=V("gn_b", o),
                                                        in1=flat(kT[:, o]), op0=ALU.add, op1=ALU.mult))
            yield
            t_gn.append(split_sbuf(flat(att[:, o]), Xs[0][0][o], Xs[0][1][o], t, [pe.last()]))

        if half == 0:
            prep = prepare(1)
        else:
            prep = norm_shift(0, ffn_got[0], "ln2", 0, t_x0)
        ahead, lag = 2, 2
        pick_ring = Ring([0, 1, 2])
        pick_ring.free = ring.free
        gate_bank = 3
        pe.wait(ring.free[gate_bank])
        ring.banks = [4, 5]
        t_init, active = {}, []

        def initial(n):
            if n < len(steps):
                o, d = steps[n]
                act.wait(ab_free[n % NB])
                t_init[n] = act.done(nc.scalar.copy(AB[n % NB][:, :, 0], s0[:, o, d, b0:b0 + HB]))

        def outer(n):
            if n < len(steps):
                o = steps[n][0]
                i, t = picked.pop(n)
                dve.wait(t, ab_free[n % NB], t_k[o])
                ring.free[i] = t_kv_of[o] = t_kv[n] = dve.done(nc.vector.tensor_tensor(
                    AB[n % NB][:, :, 1:T + 1], by_batch(bank[i][:, 0:HALF]), kT[:, o], ALU.mult))

        t_kv = {}
        for n in range(ahead):
            spread(n)
            initial(n)
        outer(0)
        for n, (o, d) in enumerate(steps):
            s = n % NB
            spread(n + ahead)
            initial(n + 2)
            outer(n + 1)
            dve.wait(t_kv.pop(n), t_init.pop(n), t_w[o])
            t = dve.done(nc.vector.tensor_tensor_scan(flat(AB[s]), flat(wT[:, o]), flat(AB[s]), 0.0, ALU.mult, ALU.add))
            pool.wait(t, yb_free[s], t_r[o])
            ab_free[s] = t_y_of[o] = t = pool.done(nc.gpsimd.tensor_tensor(YB[s], AB[s][:, :, 0:T], rT[:, o], ALU.mult))
            sums.append((n, t))
            advance(active)
            if len(sums) > lag:
                m, t = sums.pop(0)
                begin(lambda: sum_rows(m, t), active)
            if n < C:
                begin(lambda: mixed_chunk(half, 4, 1, n, "mx0", "mx1", t_in4), active)
            if n == C + 3:
                last_mix = [pool.last(), pe.last(), dve.last()]
            if o > 0 and d in (1, 3, 5, 7):
                gate(o - 1, d // 2)
            if o > 0 and d == 3:
                begin(lambda: centre(o - 1), active)
            if o > 0 and d == 5:
                begin(lambda: variance(o - 1), active)
            if d == 9:
                begin(lambda: bonus(o), active)
            if o > 0 and d == 11:
                begin(lambda: finish(o - 1), active)
            if prep and n > C + 3 and n % 8 == 7:
                begin(prep.pop(0), active)
            if n in (20, 40):
                feed_weights()
        for m, t in sums:
            run(lambda: sum_rows(m, t))
        assert not active
        for f in prep:
            run(f)
        for c in range(C):
            gate(C - 1, c)
        wg.give_up()
        run(lambda: centre(C - 1))
        run(lambda: variance(C - 1))
        ring.banks = [0, 1, 2, 3, 4, 5]
        ring.free[gate_bank] = t_g[C - 1]
        scratch_read["tmp0"], scratch_read["tmp1"] = ab_free[2:4]
        scratch_read["x50"], scratch_read["x51"] = yb_free[2:4]
        run(lambda: finish(C - 1))
        att_read = t_gn
        wo = Weight("o")
        wo.need()
        out_bank = [ring.take() for _ in range(HB)]
        for chunks in (range(C - 1), range(C - 1, C)):
            for i4 in range(HB):
                for c in chunks:
                    pe.wait(t_gn[c])
                    m = mm3(bank[out_bank[i4]][0:T, :], (Xs[0][0][c][:, i4 * T:(i4 + 1) * T], Xs[0][1][c][:, i4 * T:(i4 + 1) * T]),
                            wo.block(c, 0, D), c == 0, c == C - 1)
                if c == C - 1:
                    xs_read[0] = t = pe.done(m)
                    dve.wait(t)
                    t = dve.done(nc.vector.tensor_tensor(X[:, b0 + i4, :], bank[out_bank[i4]][0:T, :], X[:, b0 + i4, :], ALU.add))
                    ring.free[out_bank[i4]] = t
                    if half == 0:
                        t_x0.append(t)
        wo.give_up()
        feed_weights()

    new_phase()
    ring = Ring(list(range(8)))
    xn_half, sx_half = [xn], [sx]
    xn = sb("xn1", [P, C, HB, T + 1])
    sx = sb("sx1", [P, C, HB, T])
    xn_half.append(xn)
    sx_half.append(sx)
    xm = sb("xm1", [P, 2, HB, T])
    rr = sb("rr", [T, B, D])
    kh = sb("kk_hi", [P, C, NT], F32R)
    kl = sb("kk_lo", [P, C, NT], F32R)
    f_tmp = sb("f_tmp", [T, 2, D])
    Z2 = sb("normalised2", [T, D])
    t_row = load_row("bo1")
    xm_free = [None, None]
    n_xm = 0

    def ffn_mix(name, half, hi, lo):
        nonlocal n_xm
        ts = []
        for c in range(C):
            s = n_xm % 2
            n_xm += 1
            dve.wait(ffn_got[half]["sx"][c], ffn_got[half]["xn"], xm_free[s])
            t = dve.done(nc.vector.scalar_tensor_tensor(out=xm[:, s], in0=sx_half[half][:, c], scalar=V(name, c),
                                                        in1=xn_half[half][:, c, :, 1:T + 1], op0=ALU.mult, op1=ALU.add))
            cols = slice(half * HALF, (half + 1) * HALF)
            xm_free[s] = split_sbuf(flat(xm[:, s]), hi[:, c, cols], lo[:, c, cols], t)
            ts.append(xm_free[s])
        return ts

    wr = Weight("fr")
    wk = Weight("fk")
    wv = Weight("fv")
    t_rr = {}
    t_kk = {}
    t_km = {}

    def receptance(half, t_in):
        wr.need()
        for b in range(half * HB, half * HB + HB):
            i = ring.take()
            for c in range(C):
                pe.wait(t_in[c])
                m = mm3(bank[i][0:T, :], (kh[:, c, b * T:(b + 1) * T], kl[:, c, b * T:(b + 1) * T]), wr.block(c, 0, D),
                        c == 0, c == C - 1)
            t = pe.done(m)
            act.wait(t)
            ring.free[i] = t_rr[b] = act.done(nc.scalar.activation(rr[:, b, :], bank[i][0:T, :], ACT.Sigmoid))
        return pe.last()

    def ffn_keys(half, kh_free):
        nonlocal n_xm
        wk.need()
        cols = slice(half * HALF, (half + 1) * HALF)
        for o in range(C):
            i = ring.take()
            for c in range(C):
                pe.wait(t_km[half][c])
                m = mm3(bank[i][:, 0:HALF], wk.block(c, o * P, P), (Hh[:, c, cols], Hl[:, c, cols]), c == 0, c == C - 1)
            t = pe.done(m)
            s = n_xm % 2
            n_xm += 1
            act.wait(t, xm_free[s])
            ring.free[i] = t = act.done(nc.scalar.activation(flat(xm[:, s]), bank[i][:, 0:HALF], ACT.Relu))
            dve.wait(t)
            t = dve.done(nc.vector.tensor_tensor(flat(xm[:, s]), flat(xm[:, s]), flat(xm[:, s]), ALU.mult))
            t_kk[half, o] = xm_free[s] = split_sbuf(flat(xm[:, s]), kh[:, o, cols], kl[:, o, cols], t, [kh_free])

    last_mix = None
    t_r0 = ffn_mix("ffn_maa_r", 0, kh, kl)
    norm_second = norm_shift(1, ffn_got[1], "ln2", 0, [None] * HB)
    norm_second.pop(0)()
    t_km[0] = ffn_mix("ffn_maa_k", 0, Hh, Hl)
    r0_read = receptance(0, t_r0)
    for f in norm_second:
        run(f)
    t_r1 = ffn_mix("ffn_maa_r", 1, kh, kl)
    t_km[1] = ffn_mix("ffn_maa_k", 1, Hh, Hl)
    feed_weights()
    ffn_keys(0, r0_read)
    r1_read = receptance(1, t_r1)
    wr.give_up()
    ffn_keys(1, r1_read)
    wk.give_up()
    wv.need()
    ft = [None, None]
    t_x = [None] * B
    h_read = pe.last()
    normed = {}
    turns = []
    for b in range(B):
        i = ring.take()
        for c in range(C):
            pe.wait(t_kk[b // HB, c])
            m = mm3(bank[i][0:T, :], (kh[:, c, b * T:(b + 1) * T], kl[:, c, b * T:(b + 1) * T]), wv.block(c, 0, D),
                    c == 0, c == C - 1)
        t = pe.done(m)
        if b >= 1:
            zn = (b - 1) % 2
            start, finish = norm_steps(ring, b - 1, "a1_s", "a1_o", lambda: t_x[b - 1], h_read, t_row, normed,
                                       (Z, Z2)[zn], zn)
            start()
            turns.append(finish)
        if b >= 2:
            turns.pop(0)()
        dve.wait(t, t_rr[b], ft[b % 2])
        ring.free[i] = t = dve.done(nc.vector.tensor_tensor(f_tmp[:, b % 2, :], bank[i][0:T, :], rr[:, b, :], ALU.mult))
        dve.wait(t)
        t_x[b] = ft[b % 2] = dve.done(nc.vector.tensor_tensor(X[:, b, :], f_tmp[:, b % 2, :], X[:, b, :], ALU.add))
        if b % 3 == 0:
            feed_weights()
    wv.give_up()
    turns.pop(0)()

    new_phase(2)
    ctx_raw = sb("ctx_raw", [P, C, SP])
    cxh = sb("ctx_hi", [P, 2, C, SP], F32R)
    cxl = sb("ctx_lo", [P, 2, C, SP], F32R)
    qg = sb("q_group", [P, HK, NT])
    qh = sb("q_hi", [P, HK, T], F32R)
    ql = sb("q_lo", [P, HK, T], F32R)
    Kh = sb("K_hi", [P, HK, SP], F32R)
    Kl = sb("K_lo", [P, HK, SP], F32R)
    Vt = sb("V", [P, 3, D])
    Pm = sb("probs", [T, HK, SP])
    PT = sb("probs_T", [P, HK, 3, T])
    oh = sb("o_hi", [P, HK, T], F32R)
    ol = sb("o_lo", [P, HK, T], F32R)
    bv = sb("v_bias", [P, 2, D])
    mxs = sb("max", [T, HK])
    nb = sb("minus_max", [T, HK])
    ssum = sb("sum", [T, HK])
    rsum = sb("inv_sum", [T, HK])
    ctx_stream = Stream("ctx_loaded")
    bv_stream = Stream("bv_loaded")

    units = [(layer, g, b) for layer in (1, 2) for g in range(G) for b in range(B)]
    ctx_raw_free = [None]
    ctx_loaded = [None]

    def load_ctx(n):
        if n < len(units):
            ctx_loaded[0] = ctx_stream.start(ctx_raw[:], ctxT_in[units[n][2]], ctx_raw_free[0])

    load_ctx(0)
    cx_free, cx_ready = [None, None], [None, None]

    def split_ctx(n):
        if n < len(units):
            s = n % 2
            ts = []
            for c in range(0, C, 2):
                ts += split_sbuf(ctx_raw[:, c:c + 2, :], cxh[:, s, c:c + 2, :], cxl[:, s, c:c + 2, :],
                                 ctx_loaded[0], [cx_free[s]])
            cx_ready[s] = ctx_raw_free[0] = ts
            load_ctx(n + 1)

    split_ctx(0)
    work = Ring([0, 1, 2, 3])
    last_tail = [], norm_steps(work, B - 1, "a1_s", "a1_o", lambda: t_x[B - 1], h_read, t_row, normed)
    t_logit_free = [None] * HK
    free = {"K": None, "V": None, "P": None, "PT": None, "o": None, "q": None, "bv": None, "qg": None}

    def tail(u):
        t_p, t_vs, wo_block, b = u["t_p"], u["t_v"], u["wo"], u["b"]
        t_pt = []

        def transposes(h):
            i = work.take()
            pe.wait(t_p[h])
            for j, (k0, kn) in enumerate(KTILES):
                m = nc.tensor.transpose(bank[i][0:kn, j * T:(j + 1) * T], Pm[:, h, k0:k0 + kn], ident[0:T, 0:T])
            t = pe.done(m)
            e, f = (act, nc.scalar.copy) if h % 2 else (dve, nc.vector.tensor_copy)
            e.wait(t, free["PT"])
            work.free[i] = t2 = e.done(f(PT[:, h].rearrange("p j t -> p (j t)"), bank[i][:, 0:3 * T]))
            t_pt.append(t2)
            if h == HK - 1:
                free["P"] = t

        def values():
            i = work.take()
            pe.wait(t_pt, t_vs)
            for h in range(HK):
                for j, (k0, kn) in enumerate(KTILES):
                    m = nc.tensor.matmul(bank[i][:, h * T:(h + 1) * T], Vt[0:kn, j, h * P:(h + 1) * P],
                                         PT[0:kn, h, j, :], start=j == 0, stop=j == 2)
            t = pe.done(m)
            free["V"] = free["PT"] = t
            ts = split_psum(bank[i][:, 0:HK * T], oh[:].rearrange("p h t -> p (h t)"),
                            ol[:].rearrange("p h t -> p (h t)"), t, [free["o"]])
            work.free[i] = ts
            u["t_o"] = ts

        def outputs():
            i = work.take()
            wo_block.need()
            pe.wait(u["t_o"])
            for h in range(HK):
                m = mm3(bank[i][0:T, :], (oh[:, h, :], ol[:, h, :]), wo_block.block(h, 0, D), h == 0, h == HK - 1)
            free["o"] = t = pe.done(m)
            dve.wait(t, t_x[b])
            work.free[i] = t_x[b] = dve.done(nc.vector.tensor_tensor(X[:, b, :], bank[i][0:T, :], X[:, b, :], ALU.add))
            if b == B - 1:
                wo_block.give_up()

        parts = [[], [lambda: transposes(0)], [lambda: transposes(1)], [lambda: transposes(2), lambda: transposes(3)]]
        rest = [values, outputs]
        if u["norm"] and b > 0:
            start, finish = norm_steps(work, b - 1, *u["norm"], lambda: t_x[b - 1], h_read[(b - 1) // HB], u["t_row"], normed)
            parts[1].insert(0, start)
            parts[3].append(finish)
        if u["norm"] and b == B - 1:
            rest += norm_steps(work, b, *u["norm"], lambda: t_x[b], h_read[b // HB], u["t_row"], normed)
        return parts, rest

    def run_part(u):
        for f in u[0].pop(0) if u[0] else []:
            f()

    def run_rest(u):
        if u[1]:
            u[1].pop(0)()

    n_unit = 0
    h_read = [None, None]
    for layer in (1, 2):
        for g in range(G):
            wq = Weight(f"q{layer}_{g}")
            wk = Weight(f"k{layer}_{g}")
            wv = Weight(f"v{layer}_{g}")
            wo = Weight(f"o{layer}_{g}")
            t_bv = bv_stream.start(bv[:], bv_in[(layer - 1) * G + g], free["bv"])
            wq.need()
            t_q = [[], []]

            def queries(half, h):
                cols = slice(half * HALF, (half + 1) * HALF)
                i = work.take()
                pe.wait([normed[b][0] for b in range(half * HB, half * HB + HB)])
                for c in range(C):
                    m = mm3(bank[i][:, 0:HALF], wq.block(c, h * P, P), (Hh[:, c, cols], Hl[:, c, cols]),
                            c == 0, c == C - 1)
                h_read[half] = t = pe.done(m)
                act.wait(t, free["qg"])
                work.free[i] = t = act.done(nc.scalar.activation(qg[:, h, cols], bank[i][:, 0:HALF], ACT.Identity,
                                                                 bias=V(f"bq{layer}", g * HK + h)))
                t_q[half].append(t)

            for h in range(HK):
                queries(0, h)
                for _ in range((0, 3, 1, 0)[h]):
                    run_part(last_tail)
                if h == 3:
                    run_rest(last_tail)
            feed_weights()
            bk0 = VEC_AT[f"bias_k{layer}"][0] + g * HK
            learned = vec[:, bk0:bk0 + HK]
            t_lk = split_sbuf(learned, Kh[:, :, S], Kl[:, :, S], None, [free["K"]])
            for b in range(B):
                s = n_unit % 2
                cxr = cx_ready[s]
                u = {"b": b, "wo": wo, "t_v": [], "t_p": [], "t_row": t_row,
                     "norm": None if g < G - 1 else ("a2_s", "a2_o") if layer == 1 else ("am_s", "am_o")}
                t_qs = split_sbuf(qg[:, :, b * T:(b + 1) * T], qh[:], ql[:], t_q[b // HB], [free["q"]])
                if b == B - 1:
                    free["qg"] = t_qs
                wk.need()
                pe.wait(cxr)
                t_ks = []
                for h in range(HK):
                    i = work.take()
                    for c in range(C):
                        m = mm3(bank[i][:, 0:SP], wk.block(c, h * P, P), (cxh[:, s, c, :], cxl[:, s, c, :]),
                                c == 0, c == C - 1)
                    t = pe.done(m)
                    ts = split_psum(bank[i][:, 0:S], Kh[:, h, 0:S], Kl[:, h, 0:S], t, [free["K"]],
                                    bias=V(f"bk{layer}", g * HK + h))
                    work.free[i] = ts
                    t_ks.append(ts)
                    run_part(last_tail)
                    if b == 0 and h:
                        run_rest(last_tail)
                    if h == 2:
                        split_ctx(n_unit + 1)
                if b == B - 1:
                    wk.give_up()
                if b < HB:
                    queries(1, b)
                if b == HB - 1:
                    wq.give_up()
                wv.need()
                for j, (k0, kn) in enumerate(KTILES):
                    i = work.take()
                    for c in range(C):
                        m = mm3(bank[i][0:kn, :], (cxh[:, s, c, k0:k0 + kn], cxl[:, s, c, k0:k0 + kn]),
                                wv.block(c, 0, D), c == 0, c == C - 1)
                    t = pe.done(m)
                    if j == 0:
                        run_rest(last_tail)
                    dve.wait(t, t_bv, free["V"])
                    work.free[i] = t = dve.done(nc.vector.tensor_tensor(Vt[0:kn, j, :], bank[i][0:kn, :],
                                                                        bv[0:kn, j // 2, :], ALU.add))
                    u["t_v"].append(t)
                    if j >= 1:
                        run_rest(last_tail)
                cx_free[s] = pe.last()
                free["bv"] = dve.last()
                if b == B - 1:
                    wv.give_up()
                pe.wait(t_qs, t_lk)
                t_m = []
                for h in range(HK):
                    pe.wait(t_ks[h], t_logit_free[h])
                    t = pe.done(mm3(bank[4 + h][0:T, 0:SP], (qh[:, h, :], ql[:, h, :]), (Kh[:, h, :], Kl[:, h, :]),
                                    True, True))
                    dve.wait(t)
                    t_m.append(dve.done(nc.vector.tensor_reduce(mxs[:, h:h + 1], bank[4 + h][0:T, 0:SP], AX.X, ALU.max)))
                free["K"] = free["q"] = pe.last()
                n_unit += 1
                for h in range(HK):
                    dve.wait(t_m[h])
                    t = dve.done(nc.vector.tensor_scalar(nb[:, h:h + 1], mxs[:, h:h + 1], -SCALE1, None, ALU.mult))
                    act.wait(t, free["P"])
                    t_logit_free[h] = t = act.done(nc.scalar.activation(
                        Pm[:, h, :], bank[4 + h][0:T, 0:SP], ACT.Exp, bias=nb[:, h:h + 1], scale=SCALE1,
                        accum_out=ssum[:, h:h + 1]))
                for h in range(HK):
                    dve.wait(t_logit_free[h])
                    t = dve.done(nc.vector.reciprocal(rsum[:, h:h + 1], ssum[:, h:h + 1]))
                    pool.wait(t)
                    u["t_p"].append(pool.done(nc.gpsimd.tensor_scalar(Pm[:, h, :], Pm[:, h, :], rsum[:, h:h + 1], 1.0,
                                                                      ALU.mult, ALU.mult)))
                assert not any(last_tail[0]) and not last_tail[1]
                last_tail = tail(u)
                if g == 0 and b == 0:
                    t_x = [normed[k][1] for k in range(B)]
                    t_row = load_row("bo2" if layer == 1 else "b_fc2", t_x)
                feed_weights()
    for _ in range(4):
        run_part(last_tail)
    while last_tail[1]:
        run_rest(last_tail)

    def mlp(tag, bias, func, t_h, t_x):
        Gf = sb(f"g_{tag}", [P, 2, HALF])
        Gh = sb(f"g_hi_{tag}", [P, C, NT], F32R)
        Gl = sb(f"g_lo_{tag}", [P, C, NT], F32R)
        gf_free = [None, None]
        gh_free = [None, None]
        n = 0
        for g in range(4):
            w1 = Weight(f"m{tag}a_{g}")
            w2 = Weight(f"m{tag}b_{g}")
            w1.need()
            t_g = {}
            for half in range(2):
                cols = slice(half * HALF, (half + 1) * HALF)
                pe.wait(t_h[half * HB:half * HB + HB])
                for o in range(C):
                    i = ring.take()
                    for c in range(C):
                        m = mm3(bank[i][:, 0:HALF], w1.block(c, o * P, P), (Hh[:, c, cols], Hl[:, c, cols]),
                                c == 0, c == C - 1)
                    t = pe.done(m)
                    s = n % 2
                    n += 1
                    act.wait(t, gf_free[s])
                    ring.free[i] = t = act.done(nc.scalar.activation(Gf[:, s], bank[i][:, 0:HALF], func,
                                                                     bias=V(bias, g * C + o)))
                    t_g[half, o] = gf_free[s] = split_sbuf(Gf[:, s], Gh[:, o, cols], Gl[:, o, cols], t, [gh_free[half]])
                if half == 0:
                    feed_weights()
            w1.give_up()
            w2.need()
            for b in range(B):
                i = ring.take()
                for o in range(C):
                    pe.wait(t_g[b // HB, o])
                    m = mm3(bank[i][0:T, :], (Gh[:, o, b * T:(b + 1) * T], Gl[:, o, b * T:(b + 1) * T]),
                            w2.block(o, 0, D), o == 0, o == C - 1)
                t = pe.done(m)
                gh_free[b // HB] = t
                dve.wait(t, t_x[b])
                ring.free[i] = t_x[b] = dve.done(nc.vector.tensor_tensor(X[:, b, :], bank[i][0:T, :], X[:, b, :], ALU.add))
                if b == HB:
                    feed_weights()
            w2.give_up()
            if g < 3:
                feed_weights()
        return t_x

    new_phase()
    ring = Ring(list(range(8)))
    t_h = [normed[b][0] for b in range(B)]
    mlp("1", "b_fc1", ACT.Gelu, t_h, [normed[b][1] for b in range(B)])

    new_phase()
    feed_weights()
    ring = Ring([0, 1, 2, 3])
    ctx_raw = sb("ctx_raw2", [P, C, SP])
    q2 = sb("q2", [P, C, NT])
    qh = sb("q2_hi", [P, C, T], F32R)
    ql = sb("q2_lo", [P, C, T], F32R)
    Kl_f = sb("K2_latents", [P, C, HALF])
    Kh = sb("K2_hi", [P, C, SK2], F32R)
    Kl = sb("K2_lo", [P, C, SK2], F32R)
    Vh = sb("V2_hi", [P, 4, D], F32R)
    Vl = sb("V2_lo", [P, 4, D], F32R)
    Pm = sb("probs2", [T, 4, SK2])
    PTh = sb("probs2_T_hi", [P, 4, 4, T], F32R)
    PTl = sb("probs2_T_lo", [P, 4, 4, T], F32R)
    mask = sb("mask_bias", [T, SK2])
    mxs = sb("max2", [T, H2])
    nb = sb("minus_max2", [T, H2])
    ssum = sb("sum2", [T, H2])
    rsum = sb("inv_sum2", [T, H2])
    t_row = load_row("out_b")
    mask_stream = Stream("mask_loaded")
    ctx2_stream = Stream("ctx2_loaded")
    t_ctx = ctx2_stream.start(ctx_raw[:], ctxT_in[0])
    t_mz = dve.done(nc.vector.memset(mask[:, SP:SK2], 0.0))

    t_h = []
    for b in range(B):
        i, t = turn(ring, X[:, b, :], None)
        cols = slice(b * T, (b + 1) * T)
        ts = split_psum(bank[i][:, 0:C * T].rearrange("p (c t) -> p c t", c=C), Hh[:, :, cols], Hl[:, :, cols], t)
        ring.free[i] = ts
        t_h.append(ts)

    def project2(weight, half, bias, dst, free):
        cols = slice(half * HALF, (half + 1) * HALF)
        pe.wait(t_h[half * HB:half * HB + HB])
        ts = []
        for o in range(C):
            i = ring.take()
            for c in range(C):
                m = mm3(bank[i][:, 0:HALF], weight.block(c, o * P, P), (Hh[:, c, cols], Hl[:, c, cols]), c == 0, c == C - 1)
            t = pe.done(m)
            act.wait(t, free)
            ring.free[i] = t = act.done(nc.scalar.activation(dst(o), bank[i][:, 0:HALF], ACT.Identity, bias=V(bias, o)))
            ts.append(t)
        return ts

    wq = Weight("p_q")
    wq.need()
    t_q = []
    for half in range(2):
        t_q += project2(wq, half, "q2_b", lambda o: q2[:, o, half * HALF:(half + 1) * HALF], None)
    cxh, cxl = Wh[:, wq.slot, :, 0:SP], Wl[:, wq.slot, :, 0:SP]
    mask_i = mask[:, 0:SP].bitcast(I32)
    cx_free = pe.last()
    wk, wv, wo = Weight("p_k"), Weight("p_v"), Weight("p_o")
    wk.need()
    wv.need()
    logits_read = [None] * 4
    key_read = [None] * C
    value_read = None
    prob_read = [None] * 4
    pt_read = None
    t_klat_split = t_cx = t_qs = None
    t_klat = []
    t_ks = [None] * C
    t_vs = [None] * 4
    t_mask = None
    t_h2 = []

    def split_context(b):
        nonlocal t_cx, t_ctx
        t_cx = []
        for c in range(0, C, 2):
            t_cx += split_sbuf(ctx_raw[:, c:c + 2], cxh[:, c:c + 2], cxl[:, c:c + 2], t_ctx, [cx_free])
        if b + 1 < B:
            t_ctx = ctx2_stream.start(ctx_raw[:], ctxT_in[b + 1], t_cx)

    def keys(b, o):
        i = ring.take()
        pe.wait(t_cx)
        for c in range(C):
            m = mm3(bank[i][:, 0:SP], wk.block(c, o * P, P), (cxh[:, c, :], cxl[:, c, :]), c == 0, c == C - 1)
        t = pe.done(m)
        ring.free[i] = t_ks[o] = split_psum(bank[i][:, 0:SP], Kh[:, o, 0:SP], Kl[:, o, 0:SP], t, [key_read[o]],
                                            bias=V("k2_b", o))

    def latent_keys(b):
        nonlocal t_klat, t_klat_split
        if b % HB == 0:
            t_klat = project2(wk, b // HB, "k2_b", lambda o: Kl_f[:, o, :], t_klat_split)
        k = b % HB
        t_klat_split = split_sbuf(Kl_f[:, :, k * T:(k + 1) * T], Kh[:, :, SP:SK2], Kl[:, :, SP:SK2], t_klat, key_read)

    def values(b, j):
        nonlocal cx_free
        k0, kn = KTILES2[j]
        cols = slice(b * T, (b + 1) * T)
        i = ring.take()
        pe.wait(t_cx if j < 3 else t_h[b])
        for c in range(C):
            left = (cxh[:, c, k0:k0 + kn], cxl[:, c, k0:k0 + kn]) if j < 3 else (Hh[:, c, cols], Hl[:, c, cols])
            m = mm3(bank[i][0:kn, :], left, wv.block(c, 0, D), c == 0, c == C - 1)
        t = pe.done(m)
        if j < 3:
            cx_free = t
        ring.free[i] = t_vs[j] = split_psum(bank[i][0:kn, :], Vh[0:kn, j, :], Vl[0:kn, j, :], t, [value_read])

    def queries(b):
        nonlocal t_qs
        t_qs = split_sbuf(q2[:, :, b * T:(b + 1) * T], qh[:], ql[:], t_q, key_read)

    def load_mask(b):
        t_mask_in = mask_stream.start(mask_i, mask_in[b], logits_read)

        def convert():
            nonlocal t_mask
            dve.wait(t_mask_in)
            t_mask = dve.done(nc.vector.tensor_scalar(mask[:, 0:SP], mask_i, 0.0, GAP, ALU.is_equal, ALU.mult))

        return convert

    t_m, t_e, t_p, t_pt, t_at = [None] * 4, [None] * 4, [None] * 4, [None] * 4, {}

    def logits(b, o, ks=range(4)):
        pe.wait(t_qs, t_ks[o], t_klat_split)
        for k in ks:
            rows = slice(32 * k, 32 * k + 32)
            pe.wait(logits_read[k])
            t = pe.done(mm3(bank[4 + k][0:T, 0:SK2], (qh[rows, o, :], ql[rows, o, :]), (Kh[rows, o, :], Kl[rows, o, :]),
                            True, True))
            dve.wait(t, t_mask, t_mz, prob_read[k])
            logits_read[k] = t = dve.done(nc.vector.tensor_tensor_reduce(
                out=Pm[:, k, :], in0=bank[4 + k][0:T, 0:SK2], in1=mask[:], scale=1.0, scalar=-3.0e38,
                op0=ALU.add, op1=ALU.max, accum_out=mxs[:, 4 * o + k:4 * o + k + 1]))
            t_m[k] = t
        if 3 not in ks:
            return
        key_read[o] = pe.last()
        for k in range(4):
            h = 4 * o + k
            dve.wait(t_m[k])
            t = dve.done(nc.vector.tensor_scalar(nb[:, h:h + 1], mxs[:, h:h + 1], -SCALE2, None, ALU.mult))
            act.wait(t)
            t_e[k] = act.done(nc.scalar.activation(Pm[:, k, :], Pm[:, k, :], ACT.Exp, bias=nb[:, h:h + 1],
                                                   scale=SCALE2, accum_out=ssum[:, h:h + 1]))
        for k in range(4):
            h = 4 * o + k
            dve.wait(t_e[k])
            t = dve.done(nc.vector.reciprocal(rsum[:, h:h + 1], ssum[:, h:h + 1]))
            pool.wait(t)
            t_p[k] = pool.done(nc.gpsimd.tensor_scalar(Pm[:, k, :], Pm[:, k, :], rsum[:, h:h + 1], 1.0,
                                                       ALU.mult, ALU.mult))

    def transposes(ks):
        for k in ks:
            i = ring.take()
            pe.wait(t_p[k])
            for j, (k0, kn) in enumerate(KTILES2):
                m = nc.tensor.transpose(bank[i][0:kn, j * T:(j + 1) * T], Pm[:, k, k0:k0 + kn], ident[0:T, 0:T])
            prob_read[k] = t = pe.done(m)
            ring.free[i] = t_pt[k] = split_psum(bank[i][:, 0:4 * T].rearrange("p (j t) -> p j t", j=4),
                                                PTh[:, :, k, :], PTl[:, :, k, :], t, [pt_read])

    def attend(b, o):
        nonlocal pt_read, value_read
        cols = slice(b * T, (b + 1) * T)
        i = ring.take()
        pe.wait(t_pt, t_vs)
        for j, (k0, kn) in enumerate(KTILES2):
            m = mm3(bank[i][:, 0:4 * T], (Vh[0:kn, j, o * P:(o + 1) * P], Vl[0:kn, j, o * P:(o + 1) * P]),
                    (PTh[0:kn, j].rearrange("p h t -> p (h t)"), PTl[0:kn, j].rearrange("p h t -> p (h t)")),
                    j == 0, j == 3)
        pt_read = value_read = t = pe.done(m)
        ts = []
        for k in range(4):
            rows = slice(32 * k, 32 * k + 32)
            at = bank[i][rows, k * T:(k + 1) * T]
            bias = vec[rows, VEC_AT["v2_b"][0] + o:VEC_AT["v2_b"][0] + o + 1]
            ts += split_psum(at, Hh[rows, o, cols], Hl[rows, o, cols], t, bias=bias)
        ring.free[i] = t_at[b, o] = ts

    late = {}

    def project_out(b):
        cols = slice(b * T, (b + 1) * T)
        wo.need()
        i = ring.take()
        pe.wait([t_at[b, o] for o in range(C)])
        for c in range(C):
            m = mm3(bank[i][0:T, :], (Hh[:, c, cols], Hl[:, c, cols]), wo.block(c, 0, D), c == 0, c == C - 1)
        late["AT_read"] = t = pe.done(m)
        dve.wait(t, t_row, z_read[0])
        ring.free[i] = t = dve.done(nc.vector.tensor_tensor(Z[:], bank[i][0:T, :], row[:], ALU.add))
        dve.wait(t)
        t = dve.done(nc.vector.tensor_tensor(Z[:], Z[:], X[:, b, :], ALU.add))
        dve.wait(t)
        t = dve.done(nc.vector.bn_stats(stats[:, b % 2, :], Z[:]))
        dve.wait(t)
        t = dve.done(nc.vector.bn_aggr(mv[:, b % 2, :], stats[:, b % 2, :]))
        dve.wait(t)
        t = dve.done(nc.vector.scalar_tensor_tensor(out=mv[:, b % 2, 1:2], in0=mv[:, b % 2, 0:1], scalar=mv[:, b % 2, 0:1],
                                                    in1=mv[:, b % 2, 1:2], op0=ALU.mult, op1=ALU.add))
        t = inverse_root(1, mv[:, b % 2, 1:2], 1e-6, t)
        dve.wait(t)
        late["Z"] = dve.done(nc.vector.tensor_scalar(Z[:], Z[:], rstd[:, 0, 0:1], None, ALU.mult))

    def turn_normed(b):
        cols = slice(b * T, (b + 1) * T)
        i, z_read[0] = turn(ring, Z[:], late["Z"])
        ts = []
        act.wait(z_read[0])
        for c in range(C):
            ts.append(act.done(nc.scalar.activation(q2[:, c, cols], bank[i][:, c * T:(c + 1) * T], ACT.Copy,
                                                    scale=V("post_w", c))))
        ring.free[i] = ts
        t_h2.append(split_sbuf(q2[:, :, cols], Hh[:, :, cols], Hl[:, :, cols], ts, [late["AT_read"]]))

    convert_mask = load_mask(0)
    split_context(0)
    latent_keys(0)
    for o in range(C):
        keys(0, o)
    queries(0)
    convert_mask()
    for b in range(B):
        nxt, prv = b + 1 < B, b > 0
        logits(b, 0)
        for j in range(3):
            values(b, j)
        if nxt:
            split_context(b + 1)
        else:
            wq.give_up()
        transposes((0, 1))
        logits(b, 1, (0, 1))
        transposes((2, 3))
        values(b, 3)
        if b == B - 1:
            wv.give_up()
        logits(b, 1, (2, 3))
        attend(b, 0)
        if b == B - 1:
            feed_weights()
        if prv:
            project_out(b - 1)
        for ks in ((0, 1), (2, 3)):
            transposes(ks)
            logits(b, 2, ks)
        if nxt:
            keys(b + 1, 0)
        attend(b, 1)
        if nxt:
            keys(b + 1, 1)
        for ks in ((0, 1), (2, 3)):
            transposes(ks)
            logits(b, 3, ks)
        if nxt:
            convert_mask = load_mask(b + 1)
            keys(b + 1, 2)
        attend(b, 2)
        if nxt:
            latent_keys(b + 1)
        feed_weights()
        transposes((0, 1))
        if nxt:
            keys(b + 1, 3)
        transposes((2, 3))
        if nxt:
            queries(b + 1)
            convert_mask()
        if prv:
            turn_normed(b - 1)
        if b == B - 2:
            wk.give_up()
        attend(b, 3)
        feed_weights()
    project_out(B - 1)
    turn_normed(B - 1)
    wo.give_up()

    new_phase()
    ring = Ring(list(range(8)))
    t_row = load_row("mlp_b2")
    dve.wait(t_row)
    t_x = [dve.done(nc.vector.tensor_tensor(X[:, b, :], X[:, b, :], row[:], ALU.add)) for b in range(B)]
    mlp("2", "mlp_b1", ACT.Gelu_apprx_tanh, t_h2, t_x)

    new_phase()
    feed_weights()
    ring = Ring(list(range(8)))
    ctx_raw = sb("ctx_raw3", [P, C, SP])
    ctx_n = sb("ctx_rows", [P, 2, 3, D])
    Qh = sb("Q_hi", [P, C, NT], F32R)
    Ql = sb("Q_lo", [P, C, NT], F32R)
    Rh = sb("QK_hi", [P, C, NT], F32R)
    Rl = sb("QK_lo", [P, C, NT], F32R)
    Pm = sb("probs3", [T, 2, SP])
    PT = sb("probs3_T", [P, 2, 3, T])
    A = sb("attended3", [T, 2, D])
    mxs = sb("max3", [T, B])
    nb = sb("minus_max3", [T, B])
    ssum = sb("sum3", [T, B])
    rsum = sb("inv_sum3", [T, B])
    O = [Z, row]
    ctx3_streams = [Stream("ctx3_loaded0"), Stream("ctx3_loaded1")]
    rows3 = [sem("rows3_0"), sem("rows3_1")]
    n_rows3 = [0, 0]
    t_ctx = [ctx3_streams[k].start(ctx_raw[:, 2 * k:2 * k + 2], ctxT_in[0, :, 2 * k:2 * k + 2]) for k in range(2)]

    def load_rows(b, after):
        s = b % 2
        sp.wait((rows3[s], n_rows3[s]) if n_rows3[s] else None, after)
        sp.eng.dma_start(ctx_n[:, s, 0:2, :], ctx_in[b, 0:2 * P].rearrange("(j p) d -> p j d", p=P)).then_inc(rows3[s], 16)
        sp.eng.dma_start(ctx_n[0:S - 2 * P, s, 2, :], ctx_in[b, 2 * P:S]).then_inc(rows3[s], 16)
        n_rows3[s] += 32
        return (rows3[s], n_rows3[s])

    t_rows = {0: load_rows(0, None), 1: load_rows(1, None)}
    t_h = []
    for b in range(B):
        i, t = turn(ring, X[:, b, :], None)
        cols = slice(b * T, (b + 1) * T)
        ts = split_psum(bank[i][:, 0:C * T].rearrange("p (c t) -> p c t", c=C), Hh[:, :, cols], Hl[:, :, cols], t)
        ring.free[i] = ts
        t_h.append(ts)

    def project3(w, src, dst, ready, free=()):
        w.need()
        out_t = []
        for half in range(2):
            cols = slice(half * HALF, (half + 1) * HALF)
            pe.wait(ready[half])
            ts_half = []
            for o in range(C):
                i = ring.take()
                for c in range(C):
                    m = mm3(bank[i][:, 0:HALF], w.block(c, o * P, P), (src[0][:, c, cols], src[1][:, c, cols]),
                            c == 0, c == C - 1)
                t = pe.done(m)
                ts = split_psum(bank[i][:, 0:HALF], dst[0][:, o, cols], dst[1][:, o, cols], t, free)
                ring.free[i] = ts
                ts_half.append(ts)
            out_t.append(ts_half)
        return out_t

    Hs, Qs, Rs = (Hh, Hl), (Qh, Ql), (Rh, Rl)
    wq, wk, wv, wo = (Weight(name) for name in ("e_q", "e_k", "e_v", "e_o"))
    t_q = project3(wq, Hs, Qs, [t_h[0:HB], t_h[HB:B]])
    wq_read = pe.last()
    feed_weights()
    t_qk = project3(wk, Qs, Rs, t_q)
    h_free = pe.last()
    cx = [(Wh[:, w.slot, :, 0:SP], Wl[:, w.slot, :, 0:SP]) for w in (wq, wk)]
    cx_read, p_read, pt_read, a_read = [wq_read, h_free], [None, None], [None, None], [None, None]
    t_cx, t_exp, t_rs, t_a, t_pc = {}, {}, {}, {}, {}

    def context(b):
        s = b % 2
        t_cx[b] = []
        for k in range(2):
            cs = slice(2 * k, 2 * k + 2)
            act.wait(t_ctx[k], cx_read[s])
            t = act.done(nc.scalar.copy(cx[s][0][:, cs], ctx_raw[:, cs]))
            e, f = ((pool, nc.gpsimd), (dve, nc.vector))[k]
            e.wait(t_ctx[k], cx_read[s], t)
            t_cx[b] += [t, e.done(f.tensor_tensor(cx[s][1][:, cs], ctx_raw[:, cs], cx[s][0][:, cs].bitcast(F32),
                                                  ALU.subtract))]
            if b + 1 < B:
                t_ctx[k] = ctx3_streams[k].start(ctx_raw[:, cs], ctxT_in[b + 1, :, cs], t_cx[b][-2:])

    def scores(b):
        s, cols = b % 2, slice(b * T, (b + 1) * T)
        i = ring.take()
        pe.wait(t_cx[b], t_qk[b // HB])
        for c in range(C):
            m = mm3(bank[i][0:T, 0:SP], (Rh[:, c, cols], Rl[:, c, cols]), (cx[s][0][:, c, :], cx[s][1][:, c, :]),
                    c == 0, c == C - 1)
        cx_read[s] = t = pe.done(m)
        dve.wait(t)
        t = dve.done(nc.vector.tensor_reduce(mxs[:, b:b + 1], bank[i][0:T, 0:S], AX.X, ALU.max))
        dve.wait(t)
        t = dve.done(nc.vector.tensor_scalar(nb[:, b:b + 1], mxs[:, b:b + 1], -SCALE3, None, ALU.mult))
        act.wait(t, p_read[s])
        ring.free[i] = t_exp[b] = t = act.done(nc.scalar.activation(
            Pm[:, s, 0:S], bank[i][0:T, 0:S], ACT.Exp, bias=nb[:, b:b + 1], scale=SCALE3, accum_out=ssum[:, b:b + 1]))
        dve.wait(t)
        t_rs[b] = dve.done(nc.vector.reciprocal(rsum[:, b:b + 1], ssum[:, b:b + 1]))

    def attend(b):
        s = b % 2
        i = ring.take()
        pe.wait(t_exp[b])
        for j, (k0, kn) in enumerate(KTILES):
            kn = min(kn, S - k0)
            m = nc.tensor.transpose(bank[i][0:kn, j * T:(j + 1) * T], Pm[:, s, k0:k0 + kn], ident[0:T, 0:T])
        p_read[s] = t = pe.done(m)
        dve.wait(t, pt_read[s])
        ring.free[i] = t_pt = dve.done(nc.vector.tensor_copy(PT[:, s].rearrange("p j t -> p (j t)"), bank[i][:, 0:3 * T]))
        return t_pt

    def gather(b, t_pt):
        s = b % 2
        i = ring.take()
        pe.wait(t_pt, t_rows[b])
        for j, (k0, kn) in enumerate(KTILES):
            kn = min(kn, S - k0)
            m = nc.tensor.matmul(bank[i][0:T, :], PT[0:kn, s, j, :], ctx_n[0:kn, s, j, :], start=j == 0, stop=j == 2)
        pt_read[s] = t = pe.done(m)
        if b + 2 < B:
            t_rows[b + 2] = load_rows(b + 2, t)
        dve.wait(t, t_rs[b], a_read[s])
        ring.free[i] = t_a[b] = dve.done(nc.vector.tensor_scalar(A[:, s, :], bank[i][0:T, :], rsum[:, b:b + 1], None, ALU.mult))

    def gathered_turn(b):
        s, cols = b % 2, slice(b * T, (b + 1) * T)
        i, a_read[s] = turn(ring, A[:, s, :], t_a[b])
        ring.free[i] = t_pc[b] = split_psum(bank[i][:, 0:C * T].rearrange("p (c t) -> p c t", c=C), Hh[:, :, cols],
                                            Hl[:, :, cols], a_read[s], [h_free])

    t_pt = {}
    context(0)
    for b in range(B + 3):
        if b + 1 < B:
            context(b + 1)
        if b < B:
            scores(b)
        if 1 <= b <= B:
            t_pt[b - 1] = attend(b - 1)
        if 2 <= b <= B + 1:
            gather(b - 2, t_pt[b - 2])
        if 3 <= b:
            gathered_turn(b - 3)
        if b == HB:
            feed_weights()
    t_pc = [t_pc[b] for b in range(B)]
    q_free = pe.last()
    t_c = project3(wv, Hs, Qs, [t_pc[0:HB], t_pc[HB:B]], [q_free])
    out_sems = [sem("stored0"), sem("stored1")]
    stored = [0, 0]
    wo.need()
    for b in range(B):
        i = ring.take()
        pe.wait(t_c[b // HB])
        for c in range(C):
            m = mm3(bank[i][0:T, :], (Qh[:, c, b * T:(b + 1) * T], Ql[:, c, b * T:(b + 1) * T]), wo.block(c, 0, D),
                    c == 0, c == C - 1)
        t = pe.done(m)
        s = b % 2
        dve.wait(t, (out_sems[s], stored[s]) if stored[s] else None)
        ring.free[i] = t = dve.done(nc.vector.scalar_tensor_tensor(
            out=O[s][:], in0=bank[i][0:T, :], scalar=V("alpha", 0, T), in1=X[:, b, :], op0=ALU.mult, op1=ALU.add))
        sp.wait(t)
        sp.eng.dma_start(out[b], O[s][:]).then_inc(out_sems[s], 16)
        stored[s] += 16
    for s in range(2):
        sp.wait((out_sems[s], stored[s]))
    while len(phase) > 1:
        phase.pop().close()
    stack.close()


def _chunked(w):
    return np.ascontiguousarray(w.reshape(C, P, w.shape[1]).transpose(1, 0, 2))


def kernel(**inputs):
    import concourse.bacc as _bacc
    from concourse.bass_utils import run_bass_kernel_spmd as _run

    i = {k: np.asarray(v) for k, v in inputs.items()}
    l0 = {k[9:]: v for k, v in i.items() if k.startswith("L0_")}
    l1 = {k[9:]: v for k, v in i.items() if k.startswith("L1_")}
    l2 = {k[9:]: v for k, v in i.items() if k.startswith("L2_")}
    l3 = {k[9:]: v for k, v in i.items() if k.startswith("L3_")}
    ctx = i["ctx_2048"]

    ctxT = np.zeros((B, D, SP), ctx.dtype)
    ctxT[:, :, :S] = ctx.transpose(0, 2, 1)
    ctxT = np.ascontiguousarray(ctxT.reshape(B, C, P, SP).transpose(0, 2, 1, 3))
    prev = np.ascontiguousarray(ctx[:, 0:2].reshape(B, 2, C, P).transpose(3, 1, 2, 0))
    s0 = ctx[:, 2:2 + S0].reshape(B, C, 8, S0, S0).transpose(2, 3, 1, 4, 0).reshape(P, C, S0, B)
    mask = np.zeros((B, SP), i["mask_BxS2_ik0"].dtype)
    mask[:, :S] = i["mask_BxS2_ik0"]
    mask = np.repeat(mask[:, None, :], T, 1)

    blocks = {"k": l0["Wk"].T, "r": l0["Wr"].T, "v": l0["Wv"].T, "g": l0["Wg"].T, "o": l0["Wo"].T,
              "fr": l0["ffn_Wr"].T, "fk": l0["ffn_Wk"].T, "fv": l0["ffn_Wv"].T,
              "p_q": l2["q_w"], "p_k": l2["kv_w"][:, 0::2], "p_v": l2["kv_w"][:, 1::2], "p_o": l2["out_w"],
              "e_q": l3["w_q"].T, "e_k": l3["w_k"], "e_v": l3["w_v"].T, "e_o": l3["w_o"].T}
    for g in range(4):
        at = slice(g * D, (g + 1) * D)
        for layer in (1, 2):
            for w in "qkv":
                blocks[f"{w}{layer}_{g}"] = l1[f"w{w}{layer}"][:, at]
            blocks[f"o{layer}_{g}"] = l1[f"wo{layer}"][at]
        blocks[f"m1a_{g}"], blocks[f"m1b_{g}"] = l1["w_fc1"][:, at], l1["w_fc2"][at]
        blocks[f"m2a_{g}"], blocks[f"m2b_{g}"] = l2["mlp_w1"][:, at], l2["mlp_w2"][at]
    weights = np.stack([_chunked(blocks[n]) for n in UNIQUE])

    vectors = {"ln1_w": l0["ln1_w"], "ln1_b": l0["ln1_b"], "maa_x": l0["maa_x"], "time_decay": l0["time_decay"],
               "u": l0["faaaa"].reshape(-1), "gn_w": l0["gn_w"], "gn_b": l0["gn_b"], "ln2_w": l0["ln2_w"],
               "ln2_b": l0["ln2_b"], "ffn_maa_k": l0["ffn_maa_k"], "ffn_maa_r": l0["ffn_maa_r"],
               "a1_s": l1["ln1_scale"], "a1_o": l1["ln1_offset"], "a2_s": l1["ln2_scale"], "a2_o": l1["ln2_offset"],
               "am_s": l1["ln_mlp_scale"], "am_o": l1["ln_mlp_offset"], "post_w": l2["postnorm_w"],
               "q2_b": l2["q_b"], "k2_b": l2["kv_b"][0::2], "v2_b": l2["kv_b"][1::2], "alpha": np.repeat(l3["alpha"].reshape(1), P),
               "bq1": l1["bq1"], "bk1": l1["bk1"], "bq2": l1["bq2"], "bk2": l1["bk2"],
               "bias_k1": l1["bias_k1"].reshape(-1), "bias_k2": l1["bias_k2"].reshape(-1),
               "b_fc1": l1["b_fc1"], "mlp_b1": l2["mlp_b1"]}
    for j in range(5):
        vectors[f"maa_{j}"] = l0["maa_stack"][j]
    vec = np.ascontiguousarray(np.concatenate([vectors[n].reshape(w, P) for n, w in VECTORS]).T)
    rows = {"bo1": l1["bo1"], "bo2": l1["bo2"], "b_fc2": l1["b_fc2"],
            "out_b": l2["out_b"], "mlp_b2": l2["mlp_b2"]}
    rows = np.stack([np.repeat(rows[n][None], T, 0) for n in ROWS])
    bv = []
    for layer in (1, 2):
        for g in range(G):
            both = np.repeat(l1[f"bv{layer}"][None, None, g * D:(g + 1) * D], P, 0).repeat(2, 1)
            both[S - 2 * P, 1] = l1[f"bias_v{layer}"].reshape(-1)[g * D:(g + 1) * D]
            bv.append(both)
    bv = np.stack(bv)

    lane = np.arange(P)
    ident = np.eye(P, dtype=np.float32)
    heads = (lane[:, None] // S0 == lane[None, :] // S0).astype(np.float32)
    place = np.zeros((P, P + S0 - 1), np.float32)
    place[lane, S0 - 1 + S0 * (lane // S0)] = 1.0
    pick = (lane[:, None] % S0 == np.arange(S0)[None, :]).astype(np.float32)

    arrays = {"x": i["x"], "ctx": ctx, "ctxT": ctxT, "prev": prev, "s0": s0, "mask": mask, "weights": weights,
              "vec": vec, "rows": rows, "bv": bv, "maa_w1": _chunked(l0["maa_w1"]),
              "maa_w2": l0["maa_w2"].reshape(5 * 32, D), "dec_w1": _chunked(l0["decay_w1"]), "dec_w2": l0["decay_w2"],
              "ident": ident, "heads": heads, "place": place, "pick": pick}
    nc = _bacc.Bacc("TRN2", target_bir_lowering=False, num_devices=1)
    feeds, args = {}, []
    for name, a in arrays.items():
        a = np.ascontiguousarray(a)
        feeds[f"in_{name}"] = a
        args.append(nc.dram_tensor(f"in_{name}", a.shape, mybir.dt.from_np(a.dtype), kind="ExternalInput").ap())
    args.append(nc.dram_tensor("out_y", (B, T, D), F32, kind="ExternalOutput").ap())
    build(nc, *args)
    r = _run(nc, [feeds], core_ids=[0])
    return r.results[0]["out_y"]
```
